# Optimizing a Trainium2 kernel written in Bass

```python
import numpy as np
import jax
import jax.numpy as jnp

def _softmax(x, axis=-1):
    return jax.nn.softmax(x, axis=axis)

def _gelu(x):
    return jax.nn.gelu(x, approximate=True)

def _silu(x):
    return jax.nn.silu(x)

def _sigmoid(x):
    return jax.nn.sigmoid(x)

def _layernorm(x, axis=-1, eps=1e-05):
    m = jnp.mean(x, axis=axis, keepdims=True)
    v = jnp.var(x, axis=axis, keepdims=True)
    return (x - m) / jnp.sqrt(v + eps)

def _scatter_add(tgt, idx, src, axis=0):
    return tgt.at[idx].add(src)

def _segment_sum(src, seg, n):
    return jax.ops.segment_sum(src, seg, n)
kernel_name = 'mk_conv_attn_hybrid_d2_conv_nchw256_r2_6672eb'

def setup_inputs(seed: int=0):
    np.random.seed(seed)
    _w = jnp.asarray

    def _rec_inputs():
        import jax
        import jax.numpy as jnp
        _gk = jax.random.key(seed)
        x = 7.22e-05 + 1 * jax.random.normal(jax.random.fold_in(_gk, 1), (8, 128, 32, 32), jnp.float32)
        return x
    x = _rec_inputs()

    def _L0_conv_setup():
        import jax, jax.numpy as jnp
        import numpy as np
        key = jax.random.key(seed)
        ks = jax.random.split(key, 9)
        B, C, H, W = (8, 128, 32, 32)
        ck, cv, co = (64, 64, 128)
        return {'x': jax.random.normal(ks[0], (B, C, H, W), jnp.float32), 'Wq': jax.random.normal(ks[1], (ck, C), jnp.float32) * 0.05, 'bq': jax.random.normal(ks[2], (ck,), jnp.float32) * 0.05, 'Wk': jax.random.normal(ks[3], (ck, C), jnp.float32) * 0.05, 'bk': jax.random.normal(ks[4], (ck,), jnp.float32) * 0.05, 'Wv': jax.random.normal(ks[5], (cv, C), jnp.float32) * 0.05, 'bv': jax.random.normal(ks[6], (cv,), jnp.float32) * 0.05, 'Wo': jax.random.normal(ks[7], (co, cv), jnp.float32) * 0.05, 'bo': jax.random.normal(ks[8], (co,), jnp.float32) * 0.05}
    _L0_conv_all = _L0_conv_setup()
    _L0_conv_in = {k: v for k, v in _L0_conv_all.items() if k in ('Wq', 'bq', 'Wk', 'bk', 'Wv', 'bv', 'Wo', 'bo')}
    del _L0_conv_all

    def _L1_attn_setup():
        import jax, jax.numpy as jnp
        import numpy as np
        D_MODEL = 128
        D_STATE = 32
        D_CONV = 4
        EXPAND = 2
        HEADDIM = 32
        D_INNER = EXPAND * D_MODEL
        NHEADS = D_INNER // HEADDIM
        CONV_DIM = D_INNER + 2 * D_STATE
        BATCH = 8
        SEQ = 2048

        def _rmsnorm(x, w, eps):
            return x * jax.lax.rsqrt(jnp.mean(x * x, axis=-1, keepdims=True) + eps) * w
        key = jax.random.key(seed)
        ks = jax.random.split(key, 6)
        x = jax.random.normal(ks[0], (BATCH, SEQ, D_MODEL), jnp.float32)
        d_in_proj = 2 * D_INNER + 2 * D_STATE + NHEADS
        W_in = jax.random.normal(ks[1], (d_in_proj, D_MODEL), jnp.float32) / np.sqrt(D_MODEL)
        conv_w = jax.random.normal(ks[2], (CONV_DIM, D_CONV), jnp.float32) / np.sqrt(D_CONV)
        conv_b = jnp.zeros((CONV_DIM,), jnp.float32)
        dt = jnp.exp(jax.random.uniform(ks[3], (NHEADS,), jnp.float32, np.log(0.001), np.log(0.1)))
        dt_bias = dt + jnp.log(-jnp.expm1(-dt))
        A_log = jnp.log(jax.random.uniform(ks[4], (NHEADS,), jnp.float32, 1.0, 16.0))
        Dp = jnp.ones((NHEADS,), jnp.float32)
        gnorm_w = jnp.ones((D_INNER,), jnp.float32)
        norm_w = jnp.ones((D_MODEL,), jnp.float32)
        W_out = jax.random.normal(ks[5], (D_MODEL, D_INNER), jnp.float32) / np.sqrt(D_INNER)
        return {'x': x, 'W_in': W_in, 'conv_w': conv_w, 'conv_b': conv_b, 'dt_bias': dt_bias, 'A_log': A_log, 'Dp': Dp, 'gnorm_w': gnorm_w, 'norm_w': norm_w, 'W_out': W_out}
    _L1_attn_all = _L1_attn_setup()
    _L1_attn_in = {k: v for k, v in _L1_attn_all.items() if k in ('W_in', 'conv_w', 'conv_b', 'dt_bias', 'A_log', 'Dp', 'gnorm_w', 'norm_w', 'W_out')}
    del _L1_attn_all

    def _L1_ffn_setup():
        import jax, jax.numpy as jnp
        import numpy as np
        NUM_EXPERTS = 8
        TOP_K = 2
        B, S, D = (8, 4096, 128)

        def _moe(tokens, router_w, w1, b1, w2, b2):
            N = tokens.shape[0]
            E = router_w.shape[0]
            logits = tokens.astype(jnp.float32) @ router_w.astype(jnp.float32).T
            probs = jax.nn.softmax(logits, axis=-1)
            rw, re = jax.lax.top_k(probs, TOP_K)
            if TOP_K > 1:
                rw = rw / jnp.maximum(rw.sum(-1, keepdims=True), 1e-12)
            rw = rw.astype(tokens.dtype)
            combine = jnp.zeros((N, E), tokens.dtype).at[jnp.arange(N)[:, None], re].set(rw)
            out = tokens
            for e in range(E):
                h = jax.nn.gelu(tokens @ w1[e] + b1[e], approximate=False)
                y = h @ w2[e] + b2[e]
                out = out + combine[:, e:e + 1] * y
            return out
        key = jax.random.key(seed)
        ks = jax.random.split(key, 4)
        scale = 1.0 / np.sqrt(D).astype(np.float32)
        return {'input_embeddings': jax.random.normal(ks[0], (B, S, D), jnp.float32), 'router_w': jax.random.normal(ks[1], (NUM_EXPERTS, D), jnp.float32) * scale, 'w1': jax.random.normal(ks[2], (NUM_EXPERTS, D, D), jnp.float32) * scale, 'b1': jnp.zeros((NUM_EXPERTS, D), jnp.float32), 'w2': jax.random.normal(ks[3], (NUM_EXPERTS, D, D), jnp.float32) * scale, 'b2': jnp.zeros((NUM_EXPERTS, D), jnp.float32)}
    _L1_ffn_all = _L1_ffn_setup()
    _L1_ffn_in = {k: v for k, v in _L1_ffn_all.items() if k in ('router_w', 'w1', 'b1', 'w2', 'b2')}
    del _L1_ffn_all
    return {'x': x, 'L0_conv_Wq': _L0_conv_in['Wq'], 'L0_conv_bq': _L0_conv_in['bq'], 'L0_conv_Wk': _L0_conv_in['Wk'], 'L0_conv_bk': _L0_conv_in['bk'], 'L0_conv_Wv': _L0_conv_in['Wv'], 'L0_conv_bv': _L0_conv_in['bv'], 'L0_conv_Wo': _L0_conv_in['Wo'], 'L0_conv_bo': _L0_conv_in['bo'], 'L1_attn_W_in': _L1_attn_in['W_in'], 'L1_attn_conv_w': _L1_attn_in['conv_w'], 'L1_attn_conv_b': _L1_attn_in['conv_b'], 'L1_attn_dt_bias': _L1_attn_in['dt_bias'], 'L1_attn_A_log': _L1_attn_in['A_log'], 'L1_attn_Dp': _L1_attn_in['Dp'], 'L1_attn_gnorm_w': _L1_attn_in['gnorm_w'], 'L1_attn_norm_w': _L1_attn_in['norm_w'], 'L1_attn_W_out': _L1_attn_in['W_out'], 'L1_ffn_router_w': _L1_ffn_in['router_w'], 'L1_ffn_w1': _L1_ffn_in['w1'], 'L1_ffn_b1': _L1_ffn_in['b1'], 'L1_ffn_w2': _L1_ffn_in['w2'], 'L1_ffn_b2': _L1_ffn_in['b2']}

def reference(x, L0_conv_Wq, L0_conv_bq, L0_conv_Wk, L0_conv_bk, L0_conv_Wv, L0_conv_bv, L0_conv_Wo, L0_conv_bo, L1_attn_W_in, L1_attn_conv_w, L1_attn_conv_b, L1_attn_dt_bias, L1_attn_A_log, L1_attn_Dp, L1_attn_gnorm_w, L1_attn_norm_w, L1_attn_W_out, L1_ffn_router_w, L1_ffn_w1, L1_ffn_b1, L1_ffn_w2, L1_ffn_b2):
    import jax
    import jax.numpy as jnp

    def _L0_conv_ref(x, Wq, bq, Wk, bk, Wv, bv, Wo, bo):
        import jax, jax.numpy as jnp
        import numpy as np
        B, C, H, W = x.shape
        ck = Wq.shape[0]
        cv = Wv.shape[0]
        xf = x.reshape(B, C, H * W)
        q = jnp.einsum('kc,bcn->bnk', Wq, xf) + bq
        k = jnp.einsum('kc,bcn->bkn', Wk, xf) + bk[None, :, None]
        v = jnp.einsum('vc,bcn->bnv', Wv, xf) + bv
        scale = 1.0 / jnp.sqrt(jnp.asarray(ck, x.dtype))
        attn = jax.nn.softmax(jnp.einsum('bnk,bkm->bnm', q, k) * scale, axis=-1)
        out = jnp.einsum('bnm,bmv->bnv', attn, v)
        out = out.reshape(B, cv, H, W)
        y = jnp.einsum('ov,bvhw->bohw', Wo, out) + bo[None, :, None, None]
        return y

    def _L1_attn_ref(x, W_in, conv_w, conv_b, dt_bias, A_log, Dp, gnorm_w, norm_w, W_out):
        import jax, jax.numpy as jnp
        import numpy as np
        D_MODEL = 128
        D_STATE = 32
        D_CONV = 4
        EXPAND = 2
        HEADDIM = 32
        D_INNER = EXPAND * D_MODEL
        NHEADS = D_INNER // HEADDIM
        CONV_DIM = D_INNER + 2 * D_STATE
        BATCH = 8
        SEQ = 2048

        def _rmsnorm(x, w, eps):
            return x * jax.lax.rsqrt(jnp.mean(x * x, axis=-1, keepdims=True) + eps) * w
        Bsz, L, _ = x.shape
        xn = _rmsnorm(x, norm_w, jnp.finfo(x.dtype).eps)
        zxbcdt = jnp.einsum('bld,ed->ble', xn, W_in)
        z = zxbcdt[..., :D_INNER]
        xBC = zxbcdt[..., D_INNER:D_INNER + CONV_DIM]
        dt = zxbcdt[..., -NHEADS:]
        xpad = jnp.pad(xBC, ((0, 0), (D_CONV - 1, 0), (0, 0)))
        conv = sum((xpad[:, k:k + L, :] * conv_w[:, k] for k in range(D_CONV))) + conv_b
        xBC = jax.nn.silu(conv)
        xs = xBC[..., :D_INNER].reshape(Bsz, L, NHEADS, HEADDIM)
        Bm = xBC[..., D_INNER:D_INNER + D_STATE]
        Cm = xBC[..., D_INNER + D_STATE:]
        dt = jax.nn.softplus(dt + dt_bias)
        dA = jnp.exp(dt * -jnp.exp(A_log))

        def step(state, inp):
            dA_t, dt_t, B_t, C_t, x_t = inp
            state = state * dA_t[:, :, None, None] + (dt_t[:, :, None] * x_t)[..., None] * B_t[:, None, None, :]
            y = jnp.einsum('bhpn,bn->bhp', state, C_t)
            return (state, y)
        init = jnp.zeros((Bsz, NHEADS, HEADDIM, D_STATE), x.dtype)
        tm = lambda a: jnp.moveaxis(a, 1, 0)
        _, ys = jax.lax.scan(step, init, (tm(dA), tm(dt), tm(Bm), tm(Cm), tm(xs)))
        y = jnp.moveaxis(ys, 0, 1) + Dp[None, None, :, None] * xs
        y = y.reshape(Bsz, L, D_INNER)
        y = _rmsnorm(y * jax.nn.silu(z), gnorm_w, 1e-05)
        return x + jnp.einsum('ble,de->bld', y, W_out)

    def _L1_ffn_ref(input_embeddings, router_w, w1, b1, w2, b2):
        import jax, jax.numpy as jnp
        import numpy as np
        NUM_EXPERTS = 8
        TOP_K = 2
        B, S, D = (8, 4096, 128)

        def _moe(tokens, router_w, w1, b1, w2, b2):
            N = tokens.shape[0]
            E = router_w.shape[0]
            logits = tokens.astype(jnp.float32) @ router_w.astype(jnp.float32).T
            probs = jax.nn.softmax(logits, axis=-1)
            rw, re = jax.lax.top_k(probs, TOP_K)
            if TOP_K > 1:
                rw = rw / jnp.maximum(rw.sum(-1, keepdims=True), 1e-12)
            rw = rw.astype(tokens.dtype)
            combine = jnp.zeros((N, E), tokens.dtype).at[jnp.arange(N)[:, None], re].set(rw)
            out = tokens
            for e in range(E):
                h = jax.nn.gelu(tokens @ w1[e] + b1[e], approximate=False)
                y = h @ w2[e] + b2[e]
                out = out + combine[:, e:e + 1] * y
            return out
        b, s, d = input_embeddings.shape
        tokens = input_embeddings.reshape(b * s, d)
        return _moe(tokens, router_w, w1, b1, w2, b2).reshape(b, s, d)

    def _gn(v, G=32, eps=1e-05):
        B_, C_, H_, W_ = v.shape
        g = v.reshape(B_, G, C_ // G, H_, W_)
        m = jnp.mean(g, axis=(2, 3, 4), keepdims=True)
        s = jnp.var(g, axis=(2, 3, 4), keepdims=True)
        return ((g - m) / jnp.sqrt(s + eps)).reshape(v.shape)

    def _ln_c(v, eps=1e-06):
        m = jnp.mean(v, axis=1, keepdims=True)
        s = jnp.var(v, axis=1, keepdims=True)
        return (v - m) / jnp.sqrt(s + eps)

    def _ln_t(v, eps=1e-05):
        m = jnp.mean(v, axis=-1, keepdims=True)
        s = jnp.var(v, axis=-1, keepdims=True)
        return (v - m) / jnp.sqrt(s + eps)

    def _to_tokens(v):
        B_, C_, H_, W_ = v.shape
        return v.reshape(B_, C_, H_ * W_).transpose(0, 2, 1)

    def _from_tokens(t, like):
        B_, C_, H_, W_ = like.shape
        return t.transpose(0, 2, 1).reshape(B_, C_, H_, W_)
    x = x + _L0_conv_ref(_gn(x), L0_conv_Wq, L0_conv_bq, L0_conv_Wk, L0_conv_bk, L0_conv_Wv, L0_conv_bv, L0_conv_Wo, L0_conv_bo)
    t = _to_tokens(x)
    t = t + _L1_attn_ref(_ln_t(t), L1_attn_W_in, L1_attn_conv_w, L1_attn_conv_b, L1_attn_dt_bias, L1_attn_A_log, L1_attn_Dp, L1_attn_gnorm_w, L1_attn_norm_w, L1_attn_W_out)
    t = t + _L1_ffn_ref(_ln_t(t), L1_ffn_router_w, L1_ffn_w1, L1_ffn_b1, L1_ffn_w2, L1_ffn_b2)
    x = _from_tokens(t, x)
    return x

_drawn_inputs = setup_inputs


def setup_inputs(seed=0):
    import zlib

    import numpy as np

    out = dict(_drawn_inputs(seed))
    spreads = {'L1_attn_conv_b': (0.0, 0.1),
     'L1_attn_Dp': (1.0, 0.2),
     'L1_attn_gnorm_w': (1.0, 0.2),
     'L1_attn_norm_w': (1.0, 0.2),
     'L1_ffn_b1': (0.0, 0.514),
     'L1_ffn_b2': (0.0, 0.347)}
    factors = {'L0_conv_Wq': 4.702,
     'L0_conv_bq': 8.0,
     'L0_conv_Wk': 4.904,
     'L0_conv_bk': 8.0,
     'L0_conv_Wv': 4.113}
    for name, (base, spread) in spreads.items():
        noise = np.random.default_rng([zlib.crc32(name.encode()), seed]).standard_normal(out[name].shape)
        drawn = base * np.exp(spread * noise) if base else spread * noise
        out[name] = jnp.asarray(drawn.astype(out[name].dtype))
    for name, factor in factors.items():
        out[name] = (out[name] * factor).astype(out[name].dtype)
    return out
```

```python
from contextlib import ExitStack

import concourse.bass as bass
from concourse import mybir

ALU = mybir.AluOpType
ACT = mybir.ActivationFunctionType
F32 = mybir.dt.float32
F32R = mybir.dt.float32r
AX_X = mybir.AxisListType.X
AX_XY = mybir.AxisListType.XY

P = 128
BANK = 512


def hybrid_kernel(nc, x, wqk, bqk, wv, bv_rows, wo2, bo, ident, fold, group_mean,
                  wz, wx, norm_w, conv_w, conv_b, dt_bias, a_log, d_skip, wout, gnorm_w,
                  tri, ones, neg_mask, sel_rows, head_rows,
                  router, w1, b1, w2, b2_blocks, iota8, out):
    B, C, N = x.shape
    DK = bqk.shape[0] // 2
    DV = wv.shape[1]
    NT = N // P
    GN_EPS = 1e-5
    R = N // DV
    QSCALE = DK ** -0.5
    DI = wout.shape[1] * P
    NH = dt_bias.shape[1]
    HD = DI // NH
    DS = 32
    DCONV = conv_w.shape[2]
    LN_EPS = 1e-5
    POOL_STEPS = 7 + NT
    DVE_STEPS = 24
    F32_EPS = 2.0 ** -23
    GN2_EPS = 1e-5
    NE = w1.shape[1]
    EXPERT_STEPS = 15

    with ExitStack() as ctx:
        def sb(name, shape, dt=F32):
            return ctx.enter_context(nc.sbuf_tensor(name, shape, dt))

        def sem(name):
            return ctx.enter_context(nc.semaphore(name))

        ps = ctx.enter_context(nc.psum_tensor("ps", [P, 8, BANK], F32))

        w_qk = sb("w_qk", [P, 2 * DK])
        b_qk = sb("b_qk", [P, 1])
        w_v = sb("w_v", [P, DV])
        b_v = sb("b_v", [P, DV])
        w_o = sb("w_o", [P, P])
        b_o = sb("b_o", [P, 1])
        id_f = sb("id_f", [P, P])
        neg_half = sb("neg_half", [P, NT])
        neg_one = sb("neg_one", [P, NT])
        eps_t = sb("eps_t", [P, NT])
        X = sb("X", [P, B, N])
        gst = sb("gst", [P, B, 2, 6])
        gmv = sb("gmv", [P, B, 2])
        gE = sb("gE", [P, B, 2])
        gm = sb("gm", [P, B, 2])
        gvar = sb("gvar", [P, B])
        grs = sb("grs", [P, B])
        w_zh = sb("w_zh", [P, DI + NH], F32R)
        w_zl = sb("w_zl", [P, DI + NH], F32R)
        w_xh = sb("w_xh", [P, 3, P], F32R)
        w_xl = sb("w_xl", [P, 3, P], F32R)
        n_w = sb("n_w", [P, 1])
        cw = sb("cw", [P, 3, DCONV])
        cb = sb("cb", [P, 3])
        dtb = sb("dtb", [P, NH])
        a_neg = sb("a_neg", [P, NH])
        dsk = sb("dsk", [P, NH])
        w_out = sb("w_out", [P, 2, P])
        g_w = sb("g_w", [P, 2])
        tri_f = sb("tri_f", [P, P])
        ones_f = sb("ones_f", [P, P])
        mask_r = sb("mask_r", [P, BANK], F32R)
        id_r = sb("id_r", [P, P], F32R)
        lhs_c = [sb(f"lhs_c{u}", [32, NT, P], F32R) for u in range(2)]
        rhs_c = [sb(f"rhs_c{u}", [32, NH, P], F32R) for u in range(2)]

        A = ExitStack()
        M = ExitStack()

        def asb(name, shape, dt=F32):
            return A.enter_context(nc.sbuf_tensor(name, shape, dt))

        def msb(name, shape, dt=F32):
            return M.enter_context(nc.sbuf_tensor(name, shape, dt))

        xn = asb("xn", [P, N])
        q_a = asb("q_a", [P, N], F32R)
        q_b = asb("q_b", [P, N], F32R)
        k_a = asb("k_a", [P, N], F32R)
        v_f = asb("v_f", [P, NT, DV])
        v_st = asb("v_st", [P, NT, 2 * DV], F32R)
        probs = asb("probs", [P, 2, N])
        pt_h = asb("pt_h", [P, NT, N], F32R)
        pt_l = asb("pt_l", [P, NT, N], F32R)
        nmax = asb("nmax", [P, NT])
        rsum = asb("rsum", [P, NT])
        rinv = asb("rinv", [P, NT])
        o_t = asb("o_t", [P, N])
        o_n = asb("o_n", [P, NT, DV])


        w_z = asb("w_z", [P, DI + NH])
        w_x = asb("w_x", [P, 3, P])
        mask_f = asb("mask_f", [P, BANK])
        cst_f = asb("cst_f", [32, 2, N])
        fold_f = asb("fold_f", [P, DV])
        gmean = asb("gmean", [P, P])
        A.close()
        xs = [msb(f"xs{u}", [P, NT, DI]) for u in range(2)]
        zs = [msb(f"zs{u}", [P, NT, DI]) for u in range(2)]
        c_t = [msb(f"c_t{u}", [DS, N]) for u in range(2)]
        b_tok = [msb(f"b_tok{u}", [P, NT, DS]) for u in range(2)]
        g_sb = [msb(f"g_sb{u}", [P, NT, P]) for u in range(2)]
        res = [msb(f"res{u}", [P, NT, P]) for u in range(2)]
        dts = [msb(f"dts{u}", [P, NT, NH]) for u in range(2)]
        wend = [msb(f"wend{u}", [P, NT, NH]) for u in range(2)]
        eo = [msb(f"eo{u}", [P, 3, NT * NH]) for u in range(2)]
        xc = msb("xc", [P, N])
        xt = msb("xt", [P, NT, P])
        xh = msb("xh", [P, N], F32R)
        xl = msb("xl", [P, N], F32R)
        bst = msb("bst", [P, NT, 6])
        bmv = msb("bmv", [P, NT, 2])
        bve = msb("bve", [P, NT])
        bvar = msb("bvar", [P, NT])
        rs1 = msb("rs1", [P, NT])
        rs2 = msb("rs2", [P, NT])
        rs12 = msb("rs12", [P, NT])
        rp1 = msb("rp1", [P, NT])
        rnb = msb("rnb", [P, NT])
        cacc = msb("cacc", [P, 3, N])
        xst = msb("xst", [P, 2, N])
        b_t = msb("b_t", [DS, N])
        dtr = msb("dtr", [P, NT, NH])
        dta = msb("dta", [P, NT * NH])
        dte = msb("dte", [P, NT * NH])
        dtw = msb("dtw", [P, NT * NH])
        dtl = msb("dtl", [P, NT * NH])
        dtc = msb("dtc", [P, NT * NH])
        dti = msb("dti", [P, NT * NH])
        dec_a = msb("dec_a", [P, NT * NH])
        ein = msb("ein", [P, 3, NT * NH])
        cth = msb("cth", [NT * NH, P], F32R)
        ctl = msb("ctl", [NT * NH, P], F32R)
        dcy = [msb(f"dcy{u}", [P, NH, P]) for u in range(2)]
        mix = dcy
        xdt = [msb(f"xdt{u}", [P, DI]) for u in range(2)]
        xw = [msb(f"xw{u}", [P, DI]) for u in range(2)]
        xsk = [msb(f"xsk{u}", [P, DI]) for u in range(2)]
        state = [msb(f"state{u}", [DS, DI]) for u in range(2)]
        sdec = msb("sdec", [DS, DI])
        yof = msb("yof", [P, DI])
        y1 = [msb(f"y1_{u}", [P, DI]) for u in range(2)]
        y2 = [msb(f"y2_{u}", [P, DI]) for u in range(2)]
        yz = [msb(f"yz{u}", [P, DI]) for u in range(2)]
        sq = [msb(f"sq{u}", [P, DI]) for u in range(2)]
        ssq = msb("ssq", [P, NT])
        sve = msb("sve", [P, NT])
        srs = msb("srs", [P, NT])
        y_t = msb("y_t", [P, 2, N])
        M.close()
        E = ExitStack()

        def esb(name, shape, dt=F32):
            return E.enter_context(nc.sbuf_tensor(name, shape, dt))

        w1_f = esb("w1_f", [P, NE, P])
        w1_h = esb("w1_h", [P, NE, P], F32R)
        w1_l = esb("w1_l", [P, NE, P], F32R)
        w2_f = esb("w2_f", [P, NE, P])
        b1_f = esb("b1_f", [P, NE])
        b2_f = esb("b2_f", [NT * NE, N])
        rw_f = esb("rw_f", [P, NE])
        rw_h = esb("rw_h", [P, NE], F32R)
        rw_l = esb("rw_l", [P, NE], F32R)
        iota = esb("iota", [P, NE])
        est = esb("est", [P, NT, 6])
        emv = esb("emv", [P, NT, 2])
        eve = esb("eve", [P, NT])
        ers = esb("ers", [P, NT])
        un = esb("un", [P, NT, P])
        acc = esb("acc", [P, NT, P])
        uh = esb("uh", [P, N], F32R)
        ul = esb("ul", [P, N], F32R)
        lg = esb("lg", [P, NT, NE])
        top = esb("top", [P, NT, 8])
        tix = esb("tix", [P, NT, 8], mybir.dt.uint32)
        tif = esb("tif", [P, NT, 2])
        tsh = esb("tsh", [P, NT, 8])
        tex = esb("tex", [P, NT, 8])
        tsum = esb("tsum", [P, NT])
        trc = esb("trc", [P, NT])
        tp = esb("tp", [P, NT, 2])
        tw = esb("tw", [P, NT])
        oh1 = esb("oh1", [P, NT, NE])
        oh2 = esb("oh2", [P, NT, NE])
        comb = esb("comb", [P, NT, NE])
        comb_t = esb("comb_t", [NT * NE, P])
        hid = [esb(f"hid{u}", [P, BANK]) for u in range(2)]
        o_ch = [esb(f"o_ch{u}", [P, N]) for u in range(2)]
        E.close()

        s_w = sem("s_w")
        s_c = sem("s_c")
        s_ld = sem("s_ld")
        s_g1 = sem("s_g1")
        s_g2 = sem("s_g2")
        s_g3 = sem("s_g3")
        s_g4 = sem("s_g4")
        s_pre = sem("s_pre")
        s_turn = sem("s_turn")
        s_xn = sem("s_xn")
        s_qk = sem("s_qk")
        s_vp = sem("s_vp")
        s_h = sem("s_h")
        s_l = sem("s_l")
        s_vsb = sem("s_vsb")
        s_sc = sem("s_sc")
        s_mx = sem("s_mx")
        s_ex = sem("s_ex")
        s_tr = sem("s_tr")
        s_ph = sem("s_ph")
        s_pl = sem("s_pl")
        s_pv = sem("s_pv")
        s_ot = sem("s_ot")
        s_on = sem("s_on")
        s_nrm = sem("s_nrm")
        s_wo = sem("s_wo")
        s_res = sem("s_res")
        s_v1 = sem("s_v1")
        s_out = sem("s_out")
        e_w = sem("e_w")
        e_wc = sem("e_wc")
        e_in = sem("e_in")
        e_n = sem("e_n")
        e_ve = sem("e_ve")
        e_rs = sem("e_rs")
        e_un = sem("e_un")
        e_acc0 = sem("e_acc0")
        e_tr = sem("e_tr")
        e_uh = sem("e_uh")
        e_ul = sem("e_ul")
        e_lg = sem("e_lg")
        e_top = sem("e_top")
        e_ex = sem("e_ex")
        e_cb = sem("e_cb")
        e_ct = sem("e_ct")
        e_ctc = sem("e_ctc")
        e_bb = sem("e_bb")
        e_bba = sem("e_bba")
        e_h = sem("e_h")
        e_g = sem("e_g")
        e_y = sem("e_y")
        e_a = sem("e_a")
        e_to = sem("e_to")
        e_oc = sem("e_oc")
        e_fin = sem("e_fin")
        e_v = sem("e_v")
        e_gate2 = sem("e_gate2")
        m_xc = sem("m_xc")
        m_rw = sem("m_rw")
        m_t1 = sem("m_t1")
        m_ve = sem("m_ve")
        m_rs = sem("m_rs")
        m_xnt = sem("m_xnt")
        m_r = sem("m_r")
        m_t2 = sem("m_t2")
        m_xh = sem("m_xh")
        m_xl = sem("m_xl")
        m_z = sem("m_z")
        m_zs = sem("m_zs")
        m_xg = sem("m_xg")
        m_tap = sem("m_tap")
        m_cv = sem("m_cv")
        m_si = sem("m_si")
        m_dt = sem("m_dt")
        m_e1 = sem("m_e1")
        m_cum = sem("m_cum")
        m_cte = sem("m_cte")
        m_tx = sem("m_tx")
        m_txe = sem("m_txe")
        m_gp = sem("m_gp")
        m_gs = sem("m_gs")
        m_rr = sem("m_rr")
        m_pm = sem("m_pm")
        m_df = sem("m_df")
        m_L = sem("m_L")
        m_M = sem("m_M")
        m_xd = sem("m_xd")
        m_xw = sem("m_xw")
        m_sm = sem("m_sm")
        m_U = sem("m_U")
        m_S = sem("m_S")
        m_Y = sem("m_Y")
        m_y1 = sem("m_y1")
        m_y2 = sem("m_y2")
        m_yz = sem("m_yz")
        m_ty = sem("m_ty")
        m_yT = sem("m_yT")
        m_sq = sem("m_sq")
        m_op = sem("m_op")
        m_sv = sem("m_sv")
        m_sr = sem("m_sr")
        m_t2o = sem("m_t2o")
        m_v2 = sem("m_v2")
        m_p2 = sem("m_p2")
        m_q2 = sem("m_q2")
        m_a2 = sem("m_a2")
        m_eo = sem("m_eo")
        m_w2 = sem("m_w2")
        m_pe2 = sem("m_pe2")
        m_gate = sem("m_gate")

        S = [ps[:, 0:2, :], ps[:, 2:4, :]]
        T = ps[:, 4:6, :]
        O = ps[:, 6:8, :]

        cum_dram = nc.dram_tensor("cum_dram", (2, 2, NT * NH, P), F32, kind="Internal").ap()
        block = ctx.enter_context(nc.Block())

        loads = [(w_qk, wqk), (b_qk, bqk), (w_v, wv), (b_v, bv_rows), (w_o, wo2), (b_o, bo),
                 (id_f, ident), (fold_f, fold), (gmean, group_mean), (w_z, wz), (w_x, wx), (n_w, norm_w),
                 (cw, conv_w), (cb, conv_b), (dtb, dt_bias), (a_neg, a_log), (dsk, d_skip), (w_out, wout),
                 (g_w, gnorm_w), (tri_f, tri), (ones_f, ones), (mask_f, neg_mask)]

        expert_loads = [(w1_f, w1), (w2_f, w2), (b1_f, b1), (b2_f, b2_blocks), (rw_f, router), (iota, iota8)]

        @block.sync
        def _(sp):
            for b in range(B):
                sp.dma_start(X[:, b, :], x[b]).then_inc(s_ld, 16)
                if b == 0:
                    for dst, src in loads:
                        sp.dma_start(dst[:], src).then_inc(s_w, 16)
                    sp.dma_start(cst_f[:, 0, :], sel_rows).then_inc(s_w, 16)
                    sp.dma_start(cst_f[:, 1, :], head_rows).then_inc(s_w, 16)
                sp.wait_ge(s_ld, 16 * (b + 1))
            with sp.Fori(0, B // 2) as i:
                for u in range(2):
                    b = 2 * i + u
                    sp.wait_ge(m_cte, b + 1)
                    sp.sem_inc(s_turn, 1)
                    sp.wait_ge(m_df, NT * b)
                    for part, src in ((0, cth), (1, ctl)):
                        sp.dma_start(cum_dram[u, part], src[:].bitcast(F32)).then_inc(m_rw, 16)
                    sp.wait_ge(m_rw, 32 * (b + 1))
                    for part in range(2):
                        rows = cum_dram[u, part].rearrange("(c h) t -> c h t", h=NH)
                        sp.dma_start(rhs_c[u][NT * part:NT * part + NT].bitcast(F32), rows).then_inc(m_rr, 16)
                        rows = cum_dram[u, part].rearrange("(c h) t -> h c t", h=NH)
                        r0 = 2 * NT + NH * part
                        sp.dma_start(lhs_c[u][r0:r0 + NH].bitcast(F32), rows).then_inc(m_rr, 16)
                    sp.wait_ge(m_rr, 64 * (b + 1))
                    sp.sem_inc(s_turn, 1)
            sp.wait_ge(m_t2o, B)
            for dst, src in expert_loads:
                sp.dma_start(dst[:], src).then_inc(e_w, 16)
            with sp.Fori(0, B // 2) as i:
                for u in range(2):
                    b = 2 * i + u
                    sp.wait_ge(e_oc, b + 1)
                    sp.dma_start(out[b], o_ch[u][:]).then_inc(s_out, 16)
                    sp.wait_ge(s_out, 16 * (b + 1))
                    sp.sem_inc(s_turn, 1)

        @block.gpsimd
        def _(pool):
            nc.gpsimd.memset(neg_one[:], -1.0)
            nc.gpsimd.memset(eps_t[:], F32_EPS)
            nc.gpsimd.memset(neg_half[:], -0.5).then_inc(s_c, 1)
            pool.wait_ge(s_c, 1)
            pool.wait_ge(s_g3, 1)
            nc.gpsimd.tensor_tensor(grs[:], gvar[:], neg_half[:, 0:B], ALU.pow).then_inc(s_g4, 1)
            pool.wait_ge(s_res, 2 * B)
            with pool.Fori(0, B // 2) as i:
                for u in range(2):
                    b = 2 * i + u
                    n = [0]

                    def step(ins, b=b, n=n):
                        n[0] += 1
                        ins.then_inc(m_p2, 1)
                        pool.wait_ge(m_p2, POOL_STEPS * b + n[0])

                    pool.wait_ge(m_t1, b)
                    nc.gpsimd.tensor_copy(xc[:], X[:, b, :]).then_inc(m_xc, 1)
                    pool.wait_ge(m_ve, b + 1)
                    step(nc.gpsimd.tensor_tensor(rs1[:], bve[:], neg_half[:, 0:NT], ALU.pow))
                    step(nc.gpsimd.tensor_tensor(rs2[:], rs1[:], rs1[:], ALU.mult))
                    step(nc.gpsimd.tensor_tensor(rs2[:], rs2[:], bmv[:, :, 1], ALU.mult))
                    step(nc.gpsimd.tensor_tensor(rs2[:], rs2[:], eps_t[:], ALU.add))
                    step(nc.gpsimd.tensor_tensor(rs2[:], rs2[:], neg_half[:, 0:NT], ALU.pow))
                    step(nc.gpsimd.tensor_tensor(rnb[:], rs1[:], bmv[:, :, 0], ALU.mult))
                    step(nc.gpsimd.tensor_tensor(rnb[:], rnb[:], neg_one[:], ALU.mult))
                    nc.gpsimd.tensor_tensor(rp1[:], rs1[:], ones_f[:, 0:NT], ALU.add).then_inc(m_rs, 1)
                    nc.gpsimd.tensor_tensor(rs12[:], rs1[:], rs2[:], ALU.mult).then_inc(m_rs, 1)
                    pool.wait_ge(m_w2, b + 1)
                    pool.wait_ge(m_txe, 3 * b + 2)

                    def heads(t):
                        return t.rearrange("p (h d) -> p h d", h=NH)

                    def per_head(t):
                        return t.rearrange("p (h o) -> p h o", o=1).to_broadcast([t.shape[0], NH, HD])

                    def operands(c):
                        if c >= 2:
                            pool.wait_ge(m_Y, NT * b + c - 1)
                        nc.gpsimd.tensor_tensor(heads(xw[c % 2][:]), heads(xs[u][:, c, :]), per_head(wend[u][:, c, :]),
                                                ALU.mult).then_inc(m_xw, 1)
                        nc.gpsimd.tensor_tensor(heads(xdt[c % 2][:]), heads(xs[u][:, c, :]), per_head(dts[u][:, c, :]),
                                                ALU.mult).then_inc(m_xd, 1)
                        nc.gpsimd.tensor_tensor(heads(xsk[c % 2][:]), heads(xs[u][:, c, :]), per_head(dsk[:, :]),
                                                ALU.mult).then_inc(m_pm, 1)

                    operands(0)
                    for c in range(NT):
                        if 1 <= c < NT - 1:
                            pool.wait_ge(m_S, (NT - 1) * b + c)
                            nc.gpsimd.tensor_tensor(heads(sdec[:]), heads(state[c % 2][:]),
                                                    per_head(eo[u][0:DS, 2, NH * c:NH * c + NH]),
                                                    ALU.mult).then_inc(m_sm, 1)
                        if c + 1 < NT:
                            operands(c + 1)
                        pool.wait_ge(m_pm, NT * b + c + 1)
                        pool.wait_ge(m_y1, NT * b + c + 1)
                        step(nc.gpsimd.tensor_tensor(y2[c % 2][:], y1[c % 2][:], xsk[c % 2][:], ALU.add))
                        pool.wait_ge(m_zs, NT * b + NT)
                        if c >= 2:
                            pool.wait_ge(m_ty, NT * b + c - 1)
                            pool.wait_ge(m_sq, NT * b + c - 1)
                        nc.gpsimd.tensor_tensor(yz[c % 2][:], y2[c % 2][:], zs[u][:, c, :], ALU.mult).then_inc(m_yz, 1)
                    pool.wait_ge(m_sv, b + 1)
                    nc.gpsimd.tensor_tensor(srs[:], sve[:], neg_half[:, 0:NT], ALU.pow).then_inc(m_sr, 1)
                    assert n[0] == POOL_STEPS
            with pool.Fori(0, B) as b:
                pool.wait_ge(e_ve, b + 1)
                nc.gpsimd.tensor_tensor(ers[:], eve[:], neg_half[:, 0:NT], ALU.pow).then_inc(e_rs, 1)
                pool.wait_ge(e_un, b + 1)
                pool.wait_ge(e_to, b)
                nc.gpsimd.tensor_tensor(acc[:].rearrange("p t c -> p (t c)"), X[:, b, :],
                                        un[:].rearrange("p t c -> p (t c)"), ALU.add).then_inc(e_acc0, 1)

        @block.tensor
        def _(pe):
            pe.wait_ge(s_w, 16 * (len(loads) + 2))
            pe.wait_ge(s_g1, 1)
            nc.tensor.matmul(ps[:, 0, 0:2 * B], gmean[:], gE[:].rearrange("p b s -> p (b s)"),
                             start=True, stop=True).then_inc(s_g2, 1)
            pe.wait_ge(s_pre, 1)

            def scores(b, j):
                if j >= 2:
                    pe.wait_ge(s_ex, NT * b + j - 1)
                for h in range(2):
                    o = S[j % 2][:, h, :]
                    kk = k_a[:, h * BANK:(h + 1) * BANK]
                    nc.tensor.matmul(o, q_a[:, j * P:(j + 1) * P], kk, start=True, stop=False)
                    last = nc.tensor.matmul(o, q_b[:, j * P:(j + 1) * P], kk, start=False, stop=True)
                last.then_inc(s_sc, 1)

            def pv(b, h):
                pe.wait_ge(s_ph, NT * b + 4 * (h + 1))
                pe.wait_ge(s_pl, NT * b + 4 * (h + 1))
                for k in range(NT):
                    for part in (pt_h, pt_l):
                        last = nc.tensor.matmul(O[:, h, :], v_st[:, k, :], part[:, k, h * BANK:(h + 1) * BANK],
                                                start=(k == 0 and part is pt_h), stop=(k == NT - 1 and part is pt_l))
                last.then_inc(s_pv, 1)

            with pe.Fori(0, B) as b:
                pe.wait_ge(s_xn, b + 1)
                pe.wait_ge(s_res, 2 * b)
                for h in range(2):
                    last = nc.tensor.matmul(T[:, h, :], w_qk[:], xn[:, h * BANK:(h + 1) * BANK], start=True, stop=True)
                last.then_inc(s_qk, 1)
                for k in range(NT):
                    last = nc.tensor.matmul(O[:, 0, k * DV:(k + 1) * DV], xn[:, k * P:(k + 1) * P], w_v[:],
                                            start=True, stop=True)
                last.then_inc(s_vp, 1)
                pe.wait_ge(s_h, 3 * b + 3)
                pe.wait_ge(s_l, 3 * b + 3)
                scores(b, 0)
                for j in range(NT):
                    if j + 1 < NT:
                        scores(b, j + 1)
                    pe.wait_ge(s_ex, NT * b + j + 1)
                    if j >= 1:
                        pe.wait_ge(s_ph, NT * b + j)
                        pe.wait_ge(s_pl, NT * b + j)
                    for k in range(NT):
                        last = nc.tensor.transpose(T[:, k // 4, (k % 4) * P:(k % 4 + 1) * P],
                                                   probs[:, j % 2, k * P:(k + 1) * P], id_f[:])
                    last.then_inc(s_tr, 1)
                    if j == 4:
                        pe.wait_ge(s_vsb, b + 1)
                        pv(b, 0)
                pv(b, 1)
                pe.wait_ge(s_ot, b + 1)
                for j in range(NT):
                    last = nc.tensor.matmul(O[:, 0, j * DV:(j + 1) * DV], o_t[:, j * P:(j + 1) * P], fold_f[:],
                                            start=True, stop=True)
                last.then_inc(s_on, 1)
                pe.wait_ge(s_nrm, b + 1)
                for e in range(2):
                    r = slice(64 * e, 64 * e + 64)
                    last = nc.tensor.matmul(T[:, e, :], w_o[r, :], o_n[r].rearrange("p j v -> p (j v)"),
                                            start=True, stop=True)
                last.then_inc(s_wo, 1)

            pe.wait_ge(m_gate, 1)
            lo_banks = ps[:, 0:2, :]
            hi_banks = ps[:, 2:4, :]

            def cols(banks, t, w):
                q = BANK // w
                return banks[:, t // q, (t % q) * w:(t % q + 1) * w]

            def split(o, lhs, rhs, N0=None):
                nc.tensor.matmul(o, lhs[0], rhs[0], start=True, stop=False)
                nc.tensor.matmul(o, lhs[0], rhs[1], start=False, stop=False)
                return nc.tensor.matmul(o, lhs[1], rhs[0], start=False, stop=True)

            def group(b, g, banks):
                for h in range(2):
                    r = slice(h * BANK, (h + 1) * BANK)
                    last = split(banks[:, h, :], (w_xh[:, g, :], w_xl[:, g, :]), (xh[:, r], xl[:, r]))
                last.then_inc(m_xg, 1)

            def front(b, u):
                pe.wait_ge(m_xc, b + 1)
                pe.wait_ge(m_txe, 3 * b)
                for t in range(NT):
                    last = nc.tensor.transpose(cols(lo_banks, t, P), xc[:, t * P:(t + 1) * P], id_f[:])
                last.then_inc(m_t1, 1)
                pe.wait_ge(m_xnt, b + 1)
                pe.wait_ge(m_gs, b)
                for t in range(NT):
                    last = nc.tensor.transpose(cols(hi_banks, t, P), xt[:, t, :], id_f[:])
                last.then_inc(m_t2, 1)
                pe.wait_ge(m_xl, b + 1)
                group(b, 0, hi_banks)
                pe.wait_ge(m_r, b + 1)
                for t in range(NT):
                    if t >= 2:
                        pe.wait_ge(m_zs, NT * b + t - 1)
                    r = slice(t * P, (t + 1) * P)
                    split(lo_banks[:, t % 2, 0:DI + NH], (xh[:, r], xl[:, r]), (w_zh[:], w_zl[:])).then_inc(m_z, 1)
                pe.wait_ge(m_zs, NT * b + NT)
                group(b, 1, lo_banks)
                pe.wait_ge(m_cv, 3 * b + 1)
                group(b, 2, hi_banks)
                pe.wait_ge(m_dt, b + 1)
                pe.wait_ge(m_cv, 3 * b + 2)
                nc.tensor.matmul(lo_banks[:, 0, 0:64], tri_f[:], dec_a[:], start=True, stop=True)
                nc.tensor.matmul(lo_banks[:, 0, 64:128], ones_f[:], dec_a[:], start=True, stop=True)
                nc.tensor.matmul(lo_banks[0:64, 1, 0:P], dec_a[:], tri_f[:], start=True, stop=True).then_inc(m_cum, 1)
                pe.wait_ge(m_cte, b + 1)
                pe.wait_ge(m_si, 3 * b + 2)
                for t in range(NT):
                    last = nc.tensor.transpose(cols(lo_banks, t, P), xst[:, 0, t * P:(t + 1) * P], id_f[:])
                last.then_inc(m_tx, 1)
                pe.wait_ge(m_cv, 3 * b + 3)
                for t in range(NT):
                    last = nc.tensor.transpose(cols(hi_banks, t, P), xst[:, 1, t * P:(t + 1) * P], id_f[:])
                last.then_inc(m_tx, 1)
                pe.wait_ge(m_si, 3 * b + 3)
                pe.wait_ge(m_txe, 3 * b + 1)
                pe.sem_inc(s_turn, 1)
                for t in range(NT):
                    last = nc.tensor.transpose(lo_banks[:, 0, t * DS:(t + 1) * DS], b_t[:, t * P:(t + 1) * P],
                                               id_f[0:DS, 0:DS])
                last.then_inc(m_tx, 1)
                pe.wait_ge(m_txe, 3 * b + 2)
                for t in range(NT):
                    r = slice(t * P, (t + 1) * P)
                    last = nc.tensor.matmul(cols(hi_banks, t, P), b_t[:, r], c_t[u][:, r], start=True, stop=True)
                last.then_inc(m_gp, 1)

            def decay(b, u, c):
                if c >= 1:
                    pe.wait_ge(m_L, NT * b + c)
                for h in range(2):
                    o = ps[:, 4 + h, :]
                    nc.tensor.matmul(o, id_r[:], mask_r[:], start=True, stop=False)
                    last = nc.tensor.matmul(o, lhs_c[u][:, c, :],
                                            rhs_c[u][:, 4 * h:4 * h + 4, :].rearrange("p h t -> p (h t)"),
                                            start=False, stop=True)
                last.then_inc(m_df, 1)

            def turn_y(b, c):
                pe.wait_ge(m_yz, NT * b + c + 1)
                if c < NT - 2:
                    pe.wait_ge(m_S, (NT - 1) * b + c + 2)
                if c == NT - 1:
                    pe.wait_ge(m_yT, NT * b + c)
                for g in range(2):
                    last = nc.tensor.transpose(ps[:, 7, g * P:(g + 1) * P], yz[c % 2][:, g * P:(g + 1) * P], id_f[:])
                last.then_inc(m_ty, 1)

            def chunks(b, u):
                pe.wait_ge(m_rr, 64 * (b + 1))
                pe.wait_ge(m_txe, 3 * b + 3)
                pe.wait_ge(m_t2o, b)
                decay(b, u, 0)
                for c in range(NT):
                    if c < NT - 1:
                        pe.wait_ge(m_xw, NT * b + c + 1)
                        pe.wait_ge(m_yT, NT * b + max(c - 1, 0))
                        pe.wait_ge(m_S, (NT - 1) * b + c)
                        nc.tensor.matmul(ps[0:DS, 7, 0:DI], b_tok[u][:, c, :], xw[c % 2][:], start=True,
                                         stop=True).then_inc(m_U, 1)
                        decay(b, u, c + 1)
                    if c >= 1:
                        pe.wait_ge(m_S, (NT - 1) * b + c)
                    pe.wait_ge(m_y1, NT * b + c)
                    if c >= 1:
                        nc.tensor.matmul(ps[:, 6, DI:2 * DI], c_t[u][:, c * P:(c + 1) * P], state[c % 2][:],
                                         start=True, stop=True)
                    pe.wait_ge(m_M, NT * b + c + 1)
                    pe.wait_ge(m_xd, NT * b + c + 1)
                    for h in range(NH):
                        last = nc.tensor.matmul(ps[:, 6, h * HD:(h + 1) * HD], mix[c % 2][:, h, :],
                                                xdt[c % 2][:, h * HD:(h + 1) * HD], start=True, stop=True)
                    last.then_inc(m_Y, 1)
                    if c >= 1:
                        turn_y(b, c - 1)
                turn_y(b, NT - 1)
                pe.wait_ge(m_yT, NT * b + NT)
                for c in range(NT):
                    for g in range(2):
                        last = nc.tensor.matmul(ps[:, 4 + c // 4, (c % 4) * P:(c % 4 + 1) * P],
                                                y_t[:, g, c * P:(c + 1) * P], w_out[:, g, :],
                                                start=(g == 0), stop=(g == 1))
                last.then_inc(m_op, 1)

            with pe.Fori(0, B // 2) as i:
                for u in range(2):
                    front(2 * i + u, u)
                    chunks(2 * i + u, u)

            pe.wait_ge(e_wc, 1)

            def expert(b, n):
                e, h = n // 2, n % 2
                if n >= 2:
                    pe.wait_ge(e_g, 2 * NE * b + n - 1)
                else:
                    pe.wait_ge(e_g, 2 * NE * b)
                r = slice(h * BANK, (h + 1) * BANK)
                split(ps[:, 4 + n % 2, :], (w1_h[:, e, :], w1_l[:, e, :]), (uh[:, r], ul[:, r])).then_inc(e_h, 1)

            def second(b, n):
                e, h = n // 2, n % 2
                pe.wait_ge(e_g, 2 * NE * b + n + 1)
                if n >= 2:
                    pe.wait_ge(e_a, 2 * NE * b + n - 1)
                for t in range(4):
                    last = nc.tensor.matmul(ps[:, 6 + n % 2, t * P:(t + 1) * P], hid[n % 2][:, t * P:(t + 1) * P],
                                            w2_f[:, e, :], start=True, stop=True)
                last.then_inc(e_y, 1)

            with pe.Fori(0, B) as b:
                pe.wait_ge(e_un, b + 1)
                pe.wait_ge(e_oc, b)
                for t in range(NT):
                    last = nc.tensor.transpose(cols(lo_banks, t, P), un[:, t, :], id_f[:])
                last.then_inc(e_tr, 1)
                pe.wait_ge(e_ul, b + 1)
                for t in range(NT):
                    r = slice(t * P, (t + 1) * P)
                    last = split(ps[:, 2, t * NE:(t + 1) * NE], (uh[:, r], ul[:, r]), (rw_h[:], rw_l[:]))
                last.then_inc(e_lg, 1)
                expert(b, 0)
                expert(b, 1)
                pe.wait_ge(e_cb, b + 1)
                pe.sem_inc(s_turn, 1)
                nc.tensor.transpose(ps[0:NT * NE, 3, 0:P], comb[:].rearrange("p t e -> p (t e)"), id_f[:]).then_inc(e_ct, 1)
                pe.wait_ge(e_ctc, b + 1)
                for h in range(2):
                    last = nc.tensor.matmul(lo_banks[:, h, :], comb_t[:], b2_f[:, h * BANK:(h + 1) * BANK],
                                            start=True, stop=True)
                last.then_inc(e_bb, 1)
                for n in range(2 * NE):
                    second(b, n)
                    if n + 2 < 2 * NE:
                        expert(b, n + 2)
                pe.wait_ge(e_a, 2 * NE * b + 2 * NE)
                pe.wait_ge(e_bba, b + 1)
                for t in range(NT):
                    last = nc.tensor.transpose(cols(lo_banks, t, P), acc[:, t, :], id_f[:])
                last.then_inc(e_to, 1)

        @block.scalar
        def _(act):
            def hi(b, j):
                act.wait_ge(s_tr, NT * b + j + 1)
                nc.scalar.activation(pt_h[:, :, j * P:(j + 1) * P], T.rearrange("p a (k n) -> p (a k) n", n=P),
                                     ACT.Copy).then_inc(s_ph, 1)

            act.wait_ge(s_w, 16 * (len(loads) + 2))
            nc.scalar.activation(a_neg[:], a_neg[:], ACT.Exp).then_inc(m_q2, 1)
            act.wait_ge(s_pre, 1)
            with act.Fori(0, B) as b:
                act.wait_ge(s_qk, b + 1)
                tq = T[0:DK].rearrange("p a (c r) -> p (a c) r", r=R)
                for dst, r0 in ((q_a, 0), (q_b, DK)):
                    nc.scalar.activation(dst[r0:r0 + DK].rearrange("p (r c) -> p c r", r=R), tq,
                                         ACT.Identity, bias=b_qk[0:DK, 0:1]).then_inc(s_h, 1)
                nc.scalar.activation(k_a[0:DK].rearrange("p (a n) -> p a n", a=2), T[DK:2 * DK],
                                     ACT.Identity, bias=b_qk[DK:2 * DK, 0:1]).then_inc(s_h, 1)
                for j in range(NT):
                    act.wait_ge(s_mx, NT * b + j + 1)
                    if j >= 2:
                        act.wait_ge(s_tr, NT * b + j - 1)
                    nc.scalar.activation(probs[:, j % 2, :].rearrange("p (a n) -> p a n", a=2), S[j % 2], ACT.Exp,
                                         bias=nmax[:, j:j + 1], accum_out=rsum[:, j:j + 1]).then_inc(s_ex, 1)
                    if j >= 1:
                        hi(b, j - 1)
                hi(b, NT - 1)
                act.wait_ge(s_pv, 2 * b + 2)
                nc.scalar.activation(o_t[:].rearrange("p (a n) -> p a n", a=2), O, ACT.Copy).then_inc(s_ot, 1)

            lo_banks = ps[:, 0:2, :]
            hi_banks = ps[:, 2:4, :]
            act.wait_ge(m_gate, 1)

            def two(t):
                return t.rearrange("p (a n) -> p a n", a=2)

            def front(b, u):
                act.wait_ge(m_xnt, b + 1)
                act.wait_ge(m_rs, 2 * b + 1)
                act.wait_ge(m_t2o, b)
                for t in range(NT):
                    last = nc.scalar.activation(res[u][:, t, :], lo_banks[:, t // 4, (t % 4) * P:(t % 4 + 1) * P],
                                                ACT.Identity, bias=rnb[:, t:t + 1], scale=rp1[:, t:t + 1])
                last.then_inc(m_r, 1)
                act.wait_ge(m_t2, b + 1)
                nc.scalar.activation(two(xh[:]), hi_banks, ACT.Copy).then_inc(m_xh, 1)
                for t in range(NT):
                    act.wait_ge(m_z, NT * b + t + 1)
                    nc.scalar.activation(dtr[:, t, :], lo_banks[:, t % 2, DI:DI + NH], ACT.Copy)
                    nc.scalar.activation(zs[u][:, t, :], lo_banks[:, t % 2, 0:DI], ACT.Silu).then_inc(m_zs, 1)
                for g in range(3):
                    banks = (hi_banks, lo_banks, hi_banks)[g]
                    act.wait_ge(m_xg, 3 * b + g + 1)
                    nc.scalar.activation(two(cacc[:, g, :]), banks, ACT.Identity, bias=cb[:, g:g + 1],
                                         scale=cw[:, g, DCONV - 1:DCONV]).then_inc(m_tap, 1)
                for g in range(2):
                    act.wait_ge(m_cv, 3 * b + g + 1)
                    nc.scalar.activation(xst[:, g, :], cacc[:, g, :], ACT.Silu).then_inc(m_si, 1)
                act.wait_ge(m_cv, 3 * b + 3)
                nc.scalar.activation(b_t[:], cacc[0:DS, 2, :], ACT.Silu)
                nc.scalar.activation(c_t[u][:], cacc[DS:2 * DS, 2, :], ACT.Silu).then_inc(m_si, 1)

            def steps(b, u):
                nc.scalar.preload_act_table_set("natural_log_exp_and_others")
                act.wait_ge(m_e1, 2 * b + 1)
                nc.scalar.activation(dte[:], dta[:], ACT.Exp, scale=-1.0).then_inc(m_a2, 1)
                act.wait_ge(m_a2, 2 * b + 1)
                nc.scalar.activation(dtl[:], dte[:], ACT.Ln, bias=1.0).then_inc(m_a2, 1)
                act.wait_ge(m_e1, 2 * b + 2)
                nc.scalar.activation(eo[u][:], ein[:], ACT.Exp).then_inc(m_eo, 1)

            def gather(b, u):
                for g in range(2):
                    act.wait_ge(m_tx, 3 * b + g + 1)
                    nc.scalar.activation(xs[u][:, :, g * P:(g + 1) * P].rearrange("p (a t) c -> p a t c", a=2),
                                         (lo_banks, hi_banks)[g].rearrange("p a (t c) -> p a t c", c=P),
                                         ACT.Copy).then_inc(m_txe, 1)
                act.wait_ge(m_tx, 3 * b + 3)
                nc.scalar.activation(b_tok[u][:].rearrange("p t s -> p (t s)"), lo_banks[:, 0, 0:NT * DS],
                                     ACT.Copy).then_inc(m_txe, 1)

            def turned(b, c):
                act.wait_ge(m_ty, NT * b + c + 1)
                nc.scalar.activation(y_t[:, :, c * P:(c + 1) * P], ps[:, 7, 0:2 * P].rearrange("p (g t) -> p g t", g=2),
                                     ACT.Copy).then_inc(m_yT, 1)

            def chunks(b, u):
                for c in range(NT):
                    act.wait_ge(m_df, NT * b + c + 1)
                    if c >= 2:
                        act.wait_ge(m_Y, NT * b + c - 1)
                    nc.scalar.activation(dcy[c % 2][:].rearrange("p (a h) t -> p a (h t)", a=2), ps[:, 4:6, :],
                                         ACT.Exp).then_inc(m_L, 1)
                    if c >= 1:
                        act.wait_ge(m_yz, NT * b + c)
                        nc.scalar.activation(sq[(c - 1) % 2][:], yz[(c - 1) % 2][:], ACT.Square,
                                             accum_out=ssq[:, c - 1:c]).then_inc(m_sq, 1)
                        turned(b, c - 1)
                act.wait_ge(m_yz, NT * b + NT)
                nc.scalar.activation(sq[1][:], yz[1][:], ACT.Square, accum_out=ssq[:, NT - 1:NT]).then_inc(m_sq, 1)
                turned(b, NT - 1)

            with act.Fori(0, B // 2) as i:
                for u in range(2):
                    front(2 * i + u, u)
                    steps(2 * i + u, u)
                    gather(2 * i + u, u)
                    chunks(2 * i + u, u)

            with act.Fori(0, B // 2) as i:
                for u in range(2):
                    b = 2 * i + u
                    act.wait_ge(e_tr, b + 1)
                    nc.scalar.activation(two(uh[:]), lo_banks, ACT.Copy).then_inc(e_uh, 1)
                    act.wait_ge(e_top, b + 1)
                    nc.scalar.activation(tex[:], tsh[:], ACT.Exp).then_inc(e_ex, 1)
                    for n in range(2 * NE):
                        act.wait_ge(e_h, 2 * NE * b + n + 1)
                        if n >= 2:
                            act.wait_ge(e_y, 2 * NE * b + n - 1)
                        nc.scalar.activation(hid[n % 2][:], ps[:, 4 + n % 2, :], ACT.Gelu,
                                             bias=b1_f[:, n // 2:n // 2 + 1]).then_inc(e_g, 1)
                    act.wait_ge(e_to, b + 1)
                    act.wait_ge(s_out, 32 * i)
                    nc.scalar.activation(two(o_ch[u][:]), lo_banks, ACT.Copy).then_inc(e_oc, 1)

        @block.vector
        def _(dve):
            links = [0]

            def link(ins):
                links[0] += 1
                ins.then_inc(s_v1, 1)
                dve.wait_ge(s_v1, links[0])

            dve.wait_ge(s_w, 16 * (len(loads) + 2))
            nc.vector.tensor_scalar(w_qk[:, 0:DK], w_qk[:, 0:DK], QSCALE, None, ALU.mult)
            link(nc.vector.tensor_scalar(b_qk[0:DK, :], b_qk[0:DK, :], QSCALE, None, ALU.mult))
            link(nc.vector.tensor_scalar(w_z[:], w_z[:], n_w[:, 0:1], None, ALU.mult))
            link(nc.vector.tensor_scalar(w_x[:], w_x[:], n_w[:, 0:1], None, ALU.mult))
            for g in range(2):
                nc.vector.tensor_scalar(w_out[:, g, :], w_out[:, g, :], g_w[:, g:g + 1], None, ALU.mult)
            nc.vector.tensor_copy(w_zh[:], w_z[:])
            nc.vector.tensor_copy(w_xh[:], w_x[:])
            nc.vector.tensor_copy(mask_r[:], mask_f[:])
            nc.vector.tensor_copy(id_r[:], id_f[:])
            for u in range(2):
                nc.vector.tensor_copy(lhs_c[u][:].rearrange("p c t -> p (c t)"), cst_f[:, 0, :])
                last = nc.vector.tensor_copy(rhs_c[u][:].rearrange("p c t -> p (c t)"), cst_f[:, 1, :])
            link(last)
            nc.vector.tensor_tensor(w_zl[:], w_z[:], w_zh[:].bitcast(F32), ALU.subtract)
            link(nc.vector.tensor_tensor(w_xl[:], w_x[:], w_xh[:].bitcast(F32), ALU.subtract))
            dve.wait_ge(m_q2, 1)
            link(nc.vector.tensor_scalar(a_neg[:], a_neg[:], -1.0, None, ALU.mult))
            for b in range(B):
                dve.wait_ge(s_ld, 16 * (b + 1))
                for h in range(2):
                    last = nc.vector.bn_stats(gst[:, b, h, :], X[:, b, h * BANK:(h + 1) * BANK])
                link(last)
                last = nc.vector.bn_aggr(gmv[:, b, :], gst[:, b, :, :].rearrange("p h s -> p (h s)"))
            link(last)
            nc.vector.tensor_copy(gE[:, :, 0], gmv[:, :, 0])
            link(nc.vector.tensor_tensor(gE[:, :, 1], gmv[:, :, 0], gmv[:, :, 0], ALU.mult))
            nc.vector.tensor_tensor(gE[:, :, 1], gE[:, :, 1], gmv[:, :, 1], ALU.add).then_inc(s_g1, 1)
            dve.wait_ge(s_g2, 1)
            link(nc.vector.tensor_copy(gm[:].rearrange("p b s -> p (b s)"), ps[:, 0, 0:2 * B]))
            link(nc.vector.tensor_tensor(gvar[:], gm[:, :, 0], gm[:, :, 0], ALU.mult))
            link(nc.vector.tensor_tensor(gvar[:], gm[:, :, 1], gvar[:], ALU.subtract))
            nc.vector.tensor_scalar(gvar[:], gvar[:], 0.0, GN_EPS, ALU.max, ALU.add).then_inc(s_g3, 1)
            dve.wait_ge(s_g4, 1)
            dve.sem_inc(s_pre, 1)

            n0 = links[0]
            PER = 3

            def low(b, j):
                dve.wait_ge(s_ph, NT * b + j + 1)
                cols = slice(j * P, (j + 1) * P)
                nc.vector.tensor_tensor(pt_l[:, :, cols], T.rearrange("p a (k n) -> p (a k) n", n=P),
                                        pt_h[:, :, cols].bitcast(F32), ALU.subtract).then_inc(s_pl, 1)

            with dve.Fori(0, B) as b:
                done = [0]

                def step(ins):
                    done[0] += 1
                    ins.then_inc(s_v1, 1)
                    dve.wait_ge(s_v1, b * PER + (n0 + done[0]))

                nc.vector.tensor_scalar(xn[:], X[:, b, :], gm[:, b, 0:1], grs[:, bass.ds(b, 1)],
                                        ALU.subtract, ALU.mult).then_inc(s_xn, 1)
                dve.wait_ge(s_vp, b + 1)
                for_b = b_v[:].rearrange("p (o v) -> p o v", o=1).to_broadcast([P, NT, DV])
                step(nc.vector.tensor_tensor(v_f[:], O[:, 0, :].rearrange("p (k v) -> p k v", v=DV), for_b, ALU.add))
                step(nc.vector.tensor_copy(v_st[:, :, 0:DV], v_f[:]))
                nc.vector.tensor_tensor(v_st[:, :, DV:2 * DV], v_f[:], v_st[:, :, 0:DV].bitcast(F32),
                                        ALU.subtract).then_inc(s_vsb, 1)
                dve.wait_ge(s_h, 3 * b + 3)
                tq = T[0:DK].rearrange("p a (c r) -> p (a c) r", r=R)
                qh = q_a[0:DK].bitcast(F32).rearrange("p (r c) -> p c r", r=R)
                for dst, r0 in ((q_b, 0), (q_a, DK)):
                    nc.vector.scalar_tensor_tensor(dst[r0:r0 + DK].rearrange("p (r c) -> p c r", r=R), tq,
                                                   b_qk[0:DK, 0:1], qh, ALU.add, ALU.subtract).then_inc(s_l, 1)
                nc.vector.scalar_tensor_tensor(k_a[DK:2 * DK].rearrange("p (a n) -> p a n", a=2), T[DK:2 * DK],
                                               b_qk[DK:2 * DK, 0:1],
                                               k_a[0:DK].bitcast(F32).rearrange("p (a n) -> p a n", a=2),
                                               ALU.add, ALU.subtract).then_inc(s_l, 1)
                for j in range(NT):
                    dve.wait_ge(s_sc, NT * b + j + 1)
                    nc.vector.tensor_reduce(nmax[:, j:j + 1], S[j % 2], AX_XY, ALU.max, negate=True).then_inc(s_mx, 1)
                    if j >= 1:
                        low(b, j - 1)
                low(b, NT - 1)
                dve.wait_ge(s_ex, NT * b + NT)
                step(nc.vector.reciprocal(rinv[:], rsum[:]))
                dve.wait_ge(s_on, b + 1)
                nc.vector.tensor_tensor(o_n[:], O[:, 0, :].rearrange("p (k v) -> p k v", v=DV),
                                        rinv[:].rearrange("p (k o) -> p k o", o=1).to_broadcast([P, NT, DV]),
                                        ALU.mult).then_inc(s_nrm, 1)
                dve.wait_ge(s_wo, b + 1)
                for e in range(2):
                    xe = X[:, b, :].rearrange("p (j e v) -> p e j v", e=2, v=DV)[:, e]
                    nc.vector.scalar_tensor_tensor(xe, T[:, e, :].rearrange("p (j v) -> p j v", v=DV),
                                                   b_o[:, 0:1], xe, ALU.add, ALU.add).then_inc(s_res, 1)
                assert done[0] == 3, done

            lo_banks = ps[:, 0:2, :]
            hi_banks = ps[:, 2:4, :]
            dve.wait_ge(s_res, 2 * B)
            dve.sem_inc(m_gate, 1)

            def two(t):
                return t.rearrange("p (a n) -> p a n", a=2)

            def heads(t):
                return t.rearrange("p (h d) -> p h d", h=NH)

            def per_head(t, d=HD):
                return t.rearrange("p (h o) -> p h o", o=1).to_broadcast([t.shape[0], NH, d])

            def mamba(b, u):
                n = [0]

                def step(ins):
                    n[0] += 1
                    ins.then_inc(m_v2, 1)
                    dve.wait_ge(m_v2, DVE_STEPS * b + n[0])

                def tile(t):
                    return lo_banks[:, t // 4, (t % 4) * P:(t % 4 + 1) * P]

                dve.wait_ge(m_t1, b + 1)
                for t in range(NT):
                    last = nc.vector.bn_stats(bst[:, t, :], tile(t))
                step(last)
                dve.sem_inc(s_turn, 1)
                for t in range(NT):
                    last = nc.vector.bn_aggr(bmv[:, t, :], bst[:, t, :])
                step(last)
                nc.vector.tensor_scalar(bve[:], bmv[:, :, 1], LN_EPS, None, ALU.add).then_inc(m_ve, 1)
                dve.wait_ge(m_rs, 2 * b + 2)
                for t in range(NT):
                    last = nc.vector.tensor_scalar(xt[:, t, :], tile(t), bmv[:, t, 0:1], rs12[:, t:t + 1],
                                                   ALU.subtract, ALU.mult)
                last.then_inc(m_xnt, 1)
                dve.wait_ge(m_xh, b + 1)
                nc.vector.tensor_tensor(two(xl[:]), hi_banks, two(xh[:].bitcast(F32)), ALU.subtract).then_inc(m_xl, 1)
                for g in range(3):
                    rows = P if g < 2 else 2 * DS
                    banks = (hi_banks, lo_banks, hi_banks)[g][0:rows].rearrange("p a n -> p (a n)")
                    dve.wait_ge(m_tap, 3 * b + g + 1)
                    for k in range(1, DCONV):
                        ins = nc.vector.scalar_tensor_tensor(cacc[0:rows, g, k:N], banks[:, 0:N - k],
                                                             cw[0:rows, g, DCONV - 1 - k:DCONV - k],
                                                             cacc[0:rows, g, k:N], ALU.mult, ALU.add)
                        if k < DCONV - 1:
                            step(ins)
                    ins.then_inc(m_cv, 1)
                    if g == 0:
                        dve.wait_ge(m_zs, NT * b + NT)
                        x3 = dtr[:]
                        step(nc.vector.tensor_tensor(x3, x3, dtb[:].rearrange("p (o h) -> p o h", o=1).to_broadcast([P, NT, NH]),
                                                     ALU.add))
                        xf = dtr[:].rearrange("p c h -> p (c h)")
                        nc.vector.scalar_tensor_tensor(dta[:], xf, -1.0, xf, ALU.mult, ALU.max).then_inc(m_e1, 1)
                dve.wait_ge(m_a2, 2 * b + 2)
                step(nc.vector.tensor_scalar(dtw[:], dte[:], 1.0, None, ALU.add))
                nc.vector.reciprocal(dti[:], dtw[:])
                step(nc.vector.tensor_scalar(dtc[:], dtw[:], -1.0, None, ALU.add))
                step(nc.vector.tensor_tensor(dtc[:], dte[:], dtc[:], ALU.subtract))
                step(nc.vector.tensor_tensor(dtc[:], dtc[:], dti[:], ALU.mult))
                step(nc.vector.tensor_tensor(dtl[:], dtl[:], dtc[:], ALU.add))
                df = dts[u][:].rearrange("p c h -> p (c h)")
                step(nc.vector.scalar_tensor_tensor(df, xf, 0.0, dtl[:], ALU.max, ALU.add))
                nc.vector.tensor_tensor(dec_a[:].rearrange("p (c h) -> p c h", h=NH), dts[u][:],
                                        a_neg[:].rearrange("p (o h) -> p o h", o=1).to_broadcast([P, NT, NH]),
                                        ALU.mult).then_inc(m_dt, 1)
                dve.wait_ge(m_cum, b + 1)
                nc.vector.tensor_copy(ein[:, 2, :], ps[:, 0, 64:128])
                step(nc.vector.tensor_copy(ein[:, 0, :], ps[:, 0, 0:64]))
                nc.vector.tensor_tensor(ein[:, 1, :], ps[:, 0, 64:128], ein[:, 0, :], ALU.subtract).then_inc(m_e1, 1)
                dve.wait_ge(m_rr, 64 * b)
                step(nc.vector.tensor_copy(cth[:], ps[0:64, 1, 0:P]))
                nc.vector.tensor_tensor(ctl[:], ps[0:64, 1, 0:P], cth[:].bitcast(F32), ALU.subtract).then_inc(m_cte, 1)
                dve.wait_ge(m_eo, b + 1)
                nc.vector.tensor_tensor(wend[u][:].rearrange("p c h -> p (c h)"), eo[u][:, 1, :], df, ALU.mult).then_inc(m_w2, 1)
                dve.wait_ge(m_gp, b + 1)
                nc.vector.tensor_copy(g_sb[u][:].rearrange("p (a t) s -> p a (t s)", a=2), hi_banks).then_inc(m_gs, 1)
                dve.wait_ge(m_gs, b + 1)

                def mixed(c):
                    dve.wait_ge(m_L, NT * b + c + 1)
                    nc.vector.tensor_tensor(mix[c % 2][:], dcy[c % 2][:],
                                            g_sb[u][:, c:c + 1, :].to_broadcast([P, NH, P]), ALU.mult).then_inc(m_M, 1)

                mixed(0)
                for c in range(NT):
                    if c < NT - 1:
                        dve.wait_ge(m_U, (NT - 1) * b + c + 1)
                        if c == 0:
                            dve.wait_ge(m_Y, NT * b)
                            nc.vector.tensor_copy(state[1][:], ps[0:DS, 7, 0:DI]).then_inc(m_S, 1)
                        else:
                            dve.wait_ge(m_sm, (NT - 2) * b + c)
                            dve.wait_ge(m_Y, NT * b + c)
                            nc.vector.tensor_tensor(state[(c + 1) % 2][:], ps[0:DS, 7, 0:DI], sdec[:],
                                                    ALU.add).then_inc(m_S, 1)
                        mixed(c + 1)
                    dve.wait_ge(m_Y, NT * b + c + 1)
                    if c >= 2:
                        dve.wait_ge(m_yz, NT * b + c - 1)
                    if c == 0:
                        nc.vector.tensor_copy(y1[0][:], ps[:, 6, 0:DI]).then_inc(m_y1, 1)
                    else:
                        step(nc.vector.tensor_tensor(heads(yof[:]), heads(ps[:, 6, DI:2 * DI]),
                                                     per_head(eo[u][:, 0, NH * c:NH * c + NH]), ALU.mult))
                        nc.vector.tensor_tensor(y1[c % 2][:], ps[:, 6, 0:DI], yof[:], ALU.add).then_inc(m_y1, 1)
                dve.wait_ge(m_sq, NT * b + NT)
                nc.vector.tensor_scalar(sve[:], ssq[:], 1.0 / DI, GN2_EPS, ALU.mult, ALU.add).then_inc(m_sv, 1)
                dve.wait_ge(m_sr, b + 1)
                dve.wait_ge(m_op, b + 1)
                for c in range(NT):
                    last = nc.vector.scalar_tensor_tensor(X[:, b, c * P:(c + 1) * P],
                                                          ps[:, 4 + c // 4, (c % 4) * P:(c % 4 + 1) * P],
                                                          srs[:, c:c + 1], res[u][:, c, :], ALU.mult, ALU.add)
                last.then_inc(m_t2o, 1)
                assert n[0] == DVE_STEPS, n

            with dve.Fori(0, B // 2) as i:
                for u in range(2):
                    mamba(2 * i + u, u)

            dve.wait_ge(e_w, 16 * len(expert_loads))
            nc.vector.tensor_copy(w1_h[:], w1_f[:])
            nc.vector.tensor_copy(rw_h[:], rw_f[:]).then_inc(e_v, 1)
            dve.wait_ge(e_v, 1)
            nc.vector.tensor_tensor(w1_l[:], w1_f[:], w1_h[:].bitcast(F32), ALU.subtract)
            nc.vector.tensor_tensor(rw_l[:], rw_f[:], rw_h[:].bitcast(F32), ALU.subtract).then_inc(e_wc, 1)

            def by_tile(t, n):
                return t.rearrange("p (t o) -> p t o", o=1).to_broadcast([P, NT, n])

            with dve.Fori(0, B) as b:
                n = [0]

                def step(ins):
                    n[0] += 1
                    ins.then_inc(e_v, 1)
                    dve.wait_ge(e_v, EXPERT_STEPS * b + (1 + n[0]))

                for t in range(NT):
                    last = nc.vector.bn_stats(est[:, t, :], X[:, b, t * P:(t + 1) * P])
                step(last)
                dve.sem_inc(s_turn, 1)
                for t in range(NT):
                    last = nc.vector.bn_aggr(emv[:, t, :], est[:, t, :])
                step(last)
                nc.vector.tensor_scalar(eve[:], emv[:, :, 1], LN_EPS, None, ALU.add).then_inc(e_ve, 1)
                dve.wait_ge(e_rs, b + 1)
                dve.wait_ge(e_acc0, b)
                for t in range(NT):
                    last = nc.vector.tensor_scalar(un[:, t, :], X[:, b, t * P:(t + 1) * P], emv[:, t, 0:1], ers[:, t:t + 1],
                                                   ALU.subtract, ALU.mult)
                last.then_inc(e_un, 1)
                dve.wait_ge(e_uh, b + 1)
                nc.vector.tensor_tensor(two(ul[:]), lo_banks, two(uh[:].bitcast(F32)), ALU.subtract).then_inc(e_ul, 1)
                dve.wait_ge(e_lg, b + 1)
                step(nc.vector.tensor_copy(lg[:].rearrange("p t e -> p (t e)"), ps[:, 2, 0:NT * NE]))
                dve.sem_inc(s_turn, 1)
                for t in range(NT):
                    last = nc.vector.max(top[:, t, :], lg[:, t, :])
                step(last)
                dve.sem_inc(s_turn, 1)
                for t in range(NT):
                    last = nc.vector.max_index(tix[:, t, :], top[:, t, :], lg[:, t, :])
                step(last)
                nc.vector.tensor_tensor(tsh[:], top[:], top[:, :, 0:1].to_broadcast([P, NT, 8]), ALU.subtract).then_inc(e_top, 1)
                step(nc.vector.tensor_copy(tif[:], tix[:, :, 0:2]))
                io = iota[:].rearrange("p (o e) -> p o e", o=1).to_broadcast([P, NT, NE])
                nc.vector.tensor_tensor(oh1[:], io, tif[:, :, 0:1].to_broadcast([P, NT, NE]), ALU.is_equal)
                step(nc.vector.tensor_tensor(oh2[:], io, tif[:, :, 1:2].to_broadcast([P, NT, NE]), ALU.is_equal))
                dve.wait_ge(e_ex, b + 1)
                step(nc.vector.tensor_reduce(tsum[:], tex[:], AX_X, ALU.add))
                step(nc.vector.reciprocal(trc[:], tsum[:]))
                step(nc.vector.tensor_tensor(tp[:], tex[:, :, 0:2], by_tile(trc[:], 2), ALU.mult))
                step(nc.vector.tensor_tensor(tw[:], tp[:, :, 0], tp[:, :, 1], ALU.add))
                step(nc.vector.tensor_scalar(tw[:], tw[:], 1e-12, None, ALU.max))
                step(nc.vector.reciprocal(tw[:], tw[:]))
                step(nc.vector.tensor_tensor(tp[:], tp[:], by_tile(tw[:], 2), ALU.mult))
                nc.vector.tensor_tensor(oh1[:], oh1[:], tp[:, :, 0:1].to_broadcast([P, NT, NE]), ALU.mult)
                step(nc.vector.tensor_tensor(oh2[:], oh2[:], tp[:, :, 1:2].to_broadcast([P, NT, NE]), ALU.mult))
                nc.vector.tensor_tensor(comb[:], oh1[:], oh2[:], ALU.add).then_inc(e_cb, 1)
                dve.wait_ge(e_ct, b + 1)
                nc.vector.tensor_copy(comb_t[:], ps[0:NT * NE, 3, 0:P]).then_inc(e_ctc, 1)
                dve.wait_ge(e_cb, b + 1)
                dve.wait_ge(e_bb, b + 1)
                dve.wait_ge(e_acc0, b + 1)
                nc.vector.tensor_tensor(two(acc[:].rearrange("p t c -> p (t c)")), lo_banks,
                                        two(acc[:].rearrange("p t c -> p (t c)")), ALU.add).then_inc(e_bba, 1)
                dve.wait_ge(e_bba, b + 1)
                for k in range(2 * NE):
                    e, h = k // 2, k % 2
                    dve.wait_ge(e_y, 2 * NE * b + k + 1)
                    if k >= 2:
                        dve.wait_ge(e_a, 2 * NE * b + k - 1)
                    for t in range(4):
                        tt = 4 * h + t
                        last = nc.vector.scalar_tensor_tensor(acc[:, tt, :], ps[:, 6 + k % 2, t * P:(t + 1) * P],
                                                              comb[:, tt, e:e + 1], acc[:, tt, :], ALU.mult, ALU.add)
                    last.then_inc(e_a, 1)
                assert n[0] == EXPERT_STEPS, n


_INS = ['x', 'wqk', 'bqk', 'wv', 'bv_rows', 'wo2', 'bo', 'ident', 'fold', 'group_mean',
        'wz', 'wx', 'norm_w', 'conv_w', 'conv_b', 'dt_bias', 'a_log', 'd_skip', 'wout', 'gnorm_w',
        'tri', 'ones', 'neg_mask', 'sel_rows', 'head_rows',
        'router', 'w1', 'b1', 'w2', 'b2_blocks', 'iota8']


def kernel(**inputs):
    import numpy as np
    import concourse.bacc as bacc
    from concourse.bass_utils import run_bass_kernel_spmd as run

    g = {k: np.asarray(v) for k, v in inputs.items()}
    a = {
        "x": g["x"].reshape(8, 128, 1024),
        "wqk": np.concatenate([g["L0_conv_Wq"].T, g["L0_conv_Wk"].T], 1),
        "bqk": np.concatenate([g["L0_conv_bq"], g["L0_conv_bk"]])[:, None],
        "wv": g["L0_conv_Wv"].T,
        "bv_rows": np.broadcast_to(g["L0_conv_bv"], (128, 64)),
        "wo2": np.concatenate([g["L0_conv_Wo"].T] * 2, 0),
        "bo": g["L0_conv_bo"][:, None],
        "ident": np.eye(128, dtype=np.float32),
        "fold": np.tile(np.eye(64, dtype=np.float32), (2, 1)),
        "group_mean": np.kron(np.eye(32), np.full((4, 4), 0.25)).astype(np.float32),
    }
    w_in, cwt, cbs = g["L1_attn_W_in"], g["L1_attn_conv_w"], g["L1_attn_conv_b"]
    xbc = w_in[256:576]
    order = np.concatenate([np.arange(256), np.tile(np.arange(256, 320), 2)])
    rows = np.arange(32)
    sel = (rows[:, None, None] % 8 == np.arange(8)[None, :, None]) & (rows[:, None, None] < 16)
    head = -1.0 * ((rows[:, None, None] % 8 == np.arange(8)[None, :, None]) & (rows[:, None, None] >= 16))
    full = np.ones((32, 8, 128), np.float32)
    b2_blocks = np.zeros((8, 8, 8, 128), np.float32)
    for t in range(8):
        b2_blocks[t, :, t] = g["L1_ffn_b2"]
    b2_blocks = b2_blocks.reshape(64, 1024)
    a |= {
        "wz": np.concatenate([w_in[:256], w_in[576:]]).T,
        "wx": xbc[order].T.reshape(128, 3, 128),
        "norm_w": g["L1_attn_norm_w"][:, None],
        "conv_w": cwt[order].reshape(3, 128, 4).transpose(1, 0, 2),
        "conv_b": cbs[order].reshape(3, 128).T,
        "dt_bias": np.broadcast_to(g["L1_attn_dt_bias"], (128, 8)),
        "a_log": np.broadcast_to(g["L1_attn_A_log"], (128, 8)),
        "d_skip": np.broadcast_to(g["L1_attn_Dp"], (128, 8)),
        "wout": g["L1_attn_W_out"].T.reshape(2, 128, 128).transpose(1, 0, 2),
        "gnorm_w": g["L1_attn_gnorm_w"].reshape(2, 128).T,
        "tri": np.triu(np.ones((128, 128), np.float32)),
        "ones": np.ones((128, 128), np.float32),
        "neg_mask": np.tile(np.tril(np.full((128, 128), -1e30, np.float32), -1), (1, 4)),
        "sel_rows": (sel * full).astype(np.float32).reshape(32, 1024),
        "head_rows": (head * full).astype(np.float32).reshape(32, 1024),
        "router": g["L1_ffn_router_w"].T,
        "w1": g["L1_ffn_w1"].transpose(1, 0, 2),
        "b1": g["L1_ffn_b1"].T,
        "w2": g["L1_ffn_w2"].transpose(1, 0, 2),
        "b2_blocks": b2_blocks,
        "iota8": np.broadcast_to(np.arange(8, dtype=np.float32), (128, 8)),
    }
    nc = bacc.Bacc("TRN2", target_bir_lowering=False, num_devices=1)
    arrays, args = {}, []
    for name in _INS:
        v = np.ascontiguousarray(a[name])
        arrays[f"in_{name}"] = v
        args.append(nc.dram_tensor(f"in_{name}", v.shape, mybir.dt.from_np(v.dtype), kind="ExternalInput").ap())
    out = nc.dram_tensor("out_0", (8, 128, 1024), F32, kind="ExternalOutput").ap()
    hybrid_kernel(nc, *args, out)
    r = run(nc, [arrays], core_ids=[0])
    return r.results[0]["out_0"].reshape(8, 128, 32, 32)
```

```python
from contextlib import ExitStack

import concourse.bass as bass
from concourse import mybir

ALU = mybir.AluOpType
ACT = mybir.ActivationFunctionType
F32 = mybir.dt.float32
F32R = mybir.dt.float32r
AX_X = mybir.AxisListType.X
AX_XY = mybir.AxisListType.XY

P = 128
BANK = 512


def hybrid_kernel(nc, x, wqk, bqk, wv, bv_rows, wo2, bo, ident, fold, group_mean,
                  wz, wx, norm_w, conv_w, conv_b, dt_bias, a_log, d_skip, wout, gnorm_w,
                  tri, ones, neg_mask, sel_rows, head_rows,
                  router, w1, b1, w2, b2_blocks, iota8, out):
    B, C, N = x.shape
    DK = bqk.shape[0] // 2
    DV = wv.shape[1]
    NT = N // P
    GN_EPS = 1e-5
    R = N // DV
    QSCALE = DK ** -0.5
    DI = wout.shape[1] * P
    NH = dt_bias.shape[1]
    HD = DI // NH
    DS = 32
    DCONV = conv_w.shape[2]
    LN_EPS = 1e-5
    POOL_FRONT_STEPS = 7
    DVE_FRONT_STEPS = 16
    F32_EPS = 2.0 ** -23
    GN2_EPS = 1e-5
    NE = w1.shape[1]
    EXPERT_STEPS = 15

    with ExitStack() as ctx:
        def sb(name, shape, dt=F32):
            return ctx.enter_context(nc.sbuf_tensor(name, shape, dt))

        def sem(name):
            return ctx.enter_context(nc.semaphore(name))

        ps = ctx.enter_context(nc.psum_tensor("ps", [P, 8, BANK], F32))

        w_qk = sb("w_qk", [P, 2 * DK])
        b_qk = sb("b_qk", [P, 1])
        w_v = sb("w_v", [P, DV])
        b_v = sb("b_v", [P, DV])
        w_o = sb("w_o", [P, P])
        b_o = sb("b_o", [P, 1])
        id_f = sb("id_f", [P, P])
        neg_half = sb("neg_half", [P, NT])
        neg_one = sb("neg_one", [P, NT])
        eps_t = sb("eps_t", [P, NT])
        X = sb("X", [P, B, N])
        gst = sb("gst", [P, B, 2, 6])
        gmv = sb("gmv", [P, B, 2])
        gE = sb("gE", [P, B, 2])
        gm = sb("gm", [P, B, 2])
        gvar = sb("gvar", [P, B])
        grs = sb("grs", [P, B])
        w_zh = sb("w_zh", [P, DI + NH], F32R)
        w_zl = sb("w_zl", [P, DI + NH], F32R)
        w_xh = sb("w_xh", [P, 3, P], F32R)
        w_xl = sb("w_xl", [P, 3, P], F32R)
        n_w = sb("n_w", [P, 1])
        cw = sb("cw", [P, 3, DCONV])
        cb = sb("cb", [P, 3])
        dtb = sb("dtb", [P, NH])
        a_neg = sb("a_neg", [P, NH])
        dsk = sb("dsk", [P, NH])
        w_out = sb("w_out", [P, 2, P])
        g_w = sb("g_w", [P, 2])
        tri_f = sb("tri_f", [P, P])
        ones_f = sb("ones_f", [P, P])
        mask_r = sb("mask_r", [P, BANK], F32R)
        id_r = sb("id_r", [P, P], F32R)
        lhs_c = [sb(f"lhs_c{u}", [32, NT, P], F32R) for u in range(2)]
        rhs_c = [sb(f"rhs_c{u}", [32, NH, P], F32R) for u in range(2)]

        A = ExitStack()
        M = ExitStack()

        def asb(name, shape, dt=F32):
            return A.enter_context(nc.sbuf_tensor(name, shape, dt))

        def msb(name, shape, dt=F32):
            return M.enter_context(nc.sbuf_tensor(name, shape, dt))

        xn = asb("xn", [P, N])
        q_a = [asb(f"q_a{u}", [P, N], F32R) for u in range(2)]
        q_b = [asb(f"q_b{u}", [P, N], F32R) for u in range(2)]
        k_a = [asb(f"k_a{u}", [P, N], F32R) for u in range(2)]
        v_f = asb("v_f", [P, NT, DV])
        v_st = [asb(f"v_st{u}", [P, NT, 2 * DV], F32R) for u in range(2)]
        probs = asb("probs", [P, 2, N])
        pt_h = asb("pt_h", [P, NT, N], F32R)
        pt_l = asb("pt_l", [P, NT, N], F32R)
        nmax = asb("nmax", [P, NT])
        rsum = [asb(f"rsum{u}", [P, NT]) for u in range(2)]
        rinv = asb("rinv", [P, NT])
        o_t = asb("o_t", [P, N])
        o_n = asb("o_n", [P, NT, DV])


        w_z = asb("w_z", [P, DI + NH])
        w_x = asb("w_x", [P, 3, P])
        mask_f = asb("mask_f", [P, BANK])
        cst_f = asb("cst_f", [32, 2, N])
        fold_f = asb("fold_f", [P, DV])
        gmean = asb("gmean", [P, P])
        A.close()
        xs = [msb(f"xs{u}", [P, NT, DI]) for u in range(2)]
        zs = [msb(f"zs{u}", [P, NT, DI]) for u in range(2)]
        c_t = [msb(f"c_t{u}", [DS, N]) for u in range(2)]
        b_tok = [msb(f"b_tok{u}", [P, NT, DS]) for u in range(2)]
        g_sb = [msb(f"g_sb{u}", [P, NT, P]) for u in range(2)]
        res = [msb(f"res{u}", [P, NT, P]) for u in range(2)]
        dts = [msb(f"dts{u}", [P, NT, NH]) for u in range(2)]
        wend = [msb(f"wend{u}", [P, NT, NH]) for u in range(2)]
        eo = [msb(f"eo{u}", [P, 3, NT * NH]) for u in range(2)]
        xc = msb("xc", [P, N])
        xt = msb("xt", [P, NT, P])
        xh = msb("xh", [P, N], F32R)
        xl = msb("xl", [P, N], F32R)
        bst = msb("bst", [P, NT, 6])
        bmv = msb("bmv", [P, NT, 2])
        bve = msb("bve", [P, NT])
        bvar = msb("bvar", [P, NT])
        rs1 = msb("rs1", [P, NT])
        rs2 = msb("rs2", [P, NT])
        rs12 = msb("rs12", [P, NT])
        rp1 = msb("rp1", [P, NT])
        rnb = msb("rnb", [P, NT])
        cacc = msb("cacc", [P, 3, N])
        xst = msb("xst", [P, 2, N])
        b_t = msb("b_t", [DS, N])
        dtr = msb("dtr", [P, NT, NH])
        dta = msb("dta", [P, NT * NH])
        dte = msb("dte", [P, NT * NH])
        dtw = msb("dtw", [P, NT * NH])
        dtl = msb("dtl", [P, NT * NH])
        dtc = msb("dtc", [P, NT * NH])
        dti = msb("dti", [P, NT * NH])
        dec_a = msb("dec_a", [P, NT * NH])
        ein = msb("ein", [P, 3, NT * NH])
        cth = msb("cth", [NT * NH, P], F32R)
        ctl = msb("ctl", [NT * NH, P], F32R)
        dcy = [msb(f"dcy{u}", [P, NH, P]) for u in range(2)]
        mix = dcy
        xdt = [msb(f"xdt{u}", [P, DI]) for u in range(2)]
        xw = [msb(f"xw{u}", [P, DI]) for u in range(2)]
        xsk = [msb(f"xsk{u}", [P, DI]) for u in range(2)]
        state = [msb(f"state{u}", [DS, DI]) for u in range(2)]
        sdec = msb("sdec", [DS, DI])
        yof = msb("yof", [P, DI])
        y1 = [msb(f"y1_{u}", [P, DI]) for u in range(2)]
        y2 = [msb(f"y2_{u}", [P, DI]) for u in range(2)]
        yz = [msb(f"yz{u}", [P, DI]) for u in range(2)]
        sq = [msb(f"sq{u}", [P, DI]) for u in range(2)]
        ssq = msb("ssq", [P, NT])
        sve = msb("sve", [P, NT])
        srs = msb("srs", [P, NT])
        y_t = msb("y_t", [P, 2, N])
        M.close()
        E = ExitStack()

        def esb(name, shape, dt=F32):
            return E.enter_context(nc.sbuf_tensor(name, shape, dt))

        w1_f = esb("w1_f", [P, NE, P])
        w1_h = esb("w1_h", [P, NE, P], F32R)
        w1_l = esb("w1_l", [P, NE, P], F32R)
        w2_f = esb("w2_f", [P, NE, P])
        b1_f = esb("b1_f", [P, NE])
        b2_f = esb("b2_f", [NT * NE, N])
        rw_f = esb("rw_f", [P, NE])
        rw_h = esb("rw_h", [P, NE], F32R)
        rw_l = esb("rw_l", [P, NE], F32R)
        iota = esb("iota", [P, NE])
        est = esb("est", [P, NT, 6])
        emv = esb("emv", [P, NT, 2])
        eve = esb("eve", [P, NT])
        ers = esb("ers", [P, NT])
        un = esb("un", [P, NT, P])
        acc = [esb(f"acc{u}", [P, NT, P]) for u in range(2)]
        uh = [esb(f"uh{u}", [P, N], F32R) for u in range(2)]
        ul = [esb(f"ul{u}", [P, N], F32R) for u in range(2)]
        lg = esb("lg", [P, NT, NE])
        top = esb("top", [P, NT, 8])
        tix = esb("tix", [P, NT, 8], mybir.dt.uint32)
        tif = esb("tif", [P, NT, 2])
        tsh = esb("tsh", [P, NT, 8])
        tex = esb("tex", [P, NT, 8])
        tsum = esb("tsum", [P, NT])
        trc = esb("trc", [P, NT])
        tp = esb("tp", [P, NT, 2])
        tw = esb("tw", [P, NT])
        oh1 = esb("oh1", [P, NT, NE])
        oh2 = esb("oh2", [P, NT, NE])
        comb = [esb(f"comb{u}", [P, NT, NE]) for u in range(2)]
        comb_t = esb("comb_t", [NT * NE, P])
        hid = [esb(f"hid{u}", [P, BANK]) for u in range(2)]
        o_ch = [esb(f"o_ch{u}", [P, N]) for u in range(2)]
        E.close()

        s_w = sem("s_w")
        s_w2 = sem("s_w2")
        s_c = sem("s_c")
        s_ld = sem("s_ld")
        moments_ready = sem("moments_ready")
        groups_ready = sem("groups_ready")
        var_ready = sem("var_ready")
        rstd_ready = sem("rstd_ready")
        s_own = sem("s_own")
        s_turn = sem("s_turn")
        s_xn = sem("s_xn")
        s_vf = sem("s_vf")
        s_vh = sem("s_vh")
        s_ri = sem("s_ri")
        s_bn = sem("s_bn")
        s_qk = sem("s_qk")
        s_vp = sem("s_vp")
        s_h = sem("s_h")
        s_l = sem("s_l")
        s_vsb = sem("s_vsb")
        s_sc = sem("s_sc")
        s_mx = sem("s_mx")
        s_ex = sem("s_ex")
        s_tr = sem("s_tr")
        s_ph = sem("s_ph")
        s_pl = sem("s_pl")
        s_pv = sem("s_pv")
        s_ot = sem("s_ot")
        s_on = sem("s_on")
        s_nrm = sem("s_nrm")
        s_wo = sem("s_wo")
        s_res = sem("s_res")
        s_v1 = sem("s_v1")
        s_out = sem("s_out")
        e_w = sem("e_w")
        e_wc = sem("e_wc")
        e_in = sem("e_in")
        e_n = sem("e_n")
        e_ve = sem("e_ve")
        e_rs = sem("e_rs")
        e_un = sem("e_un")
        e_acc0 = sem("e_acc0")
        e_tr = sem("e_tr")
        e_uh = sem("e_uh")
        e_ul = sem("e_ul")
        e_lg = sem("e_lg")
        e_top = sem("e_top")
        e_ex = sem("e_ex")
        e_cb = sem("e_cb")
        e_ct = sem("e_ct")
        e_ctc = sem("e_ctc")
        e_bb = sem("e_bb")
        e_bba = sem("e_bba")
        e_h = sem("e_h")
        e_g = sem("e_g")
        e_y = sem("e_y")
        e_a = sem("e_a")
        e_to = sem("e_to")
        e_oc = sem("e_oc")
        e_fin = sem("e_fin")
        e_v = sem("e_v")
        e_gate2 = sem("e_gate2")
        m_xc = sem("m_xc")
        m_rw = sem("m_rw")
        m_t1 = sem("m_t1")
        m_ve = sem("m_ve")
        m_rs = sem("m_rs")
        m_xnt = sem("m_xnt")
        m_r = sem("m_r")
        m_t2 = sem("m_t2")
        m_xh = sem("m_xh")
        m_xl = sem("m_xl")
        m_z = sem("m_z")
        m_zs = sem("m_zs")
        m_xg = sem("m_xg")
        m_tap = sem("m_tap")
        m_cv = sem("m_cv")
        m_si = sem("m_si")
        m_dt = sem("m_dt")
        m_e1 = sem("m_e1")
        m_cum = sem("m_cum")
        m_cte = sem("m_cte")
        m_tx = sem("m_tx")
        m_txe = sem("m_txe")
        m_gp = sem("m_gp")
        m_gs = sem("m_gs")
        m_rr = sem("m_rr")
        m_pm = sem("m_pm")
        m_df = sem("m_df")
        m_L = sem("m_L")
        m_M = sem("m_M")
        m_xd = sem("m_xd")
        m_xw = sem("m_xw")
        m_sm = sem("m_sm")
        m_U = sem("m_U")
        m_S = sem("m_S")
        m_Y = sem("m_Y")
        m_y1 = sem("m_y1")
        m_y2 = sem("m_y2")
        m_yz = sem("m_yz")
        m_ty = sem("m_ty")
        m_yT = sem("m_yT")
        m_sq = sem("m_sq")
        m_op = sem("m_op")
        m_sv = sem("m_sv")
        m_sr = sem("m_sr")
        m_t2o = sem("m_t2o")
        m_v2 = sem("m_v2")
        m_p2 = sem("m_p2")
        m_p3 = sem("m_p3")
        m_v3 = sem("m_v3")
        m_q2 = sem("m_q2")
        m_a2 = sem("m_a2")
        m_eo = sem("m_eo")
        m_w2 = sem("m_w2")
        m_pe2 = sem("m_pe2")
        m_gate = sem("m_gate")

        stat_groups = [(0, 1), (1, 2), (2, B)]
        S = [ps[:, 0:2, :], ps[:, 2:4, :]]
        T = ps[:, 4:6, :]
        O = ps[:, 6:8, :]

        cum_dram = nc.dram_tensor("cum_dram", (2, 2, NT * NH, P), F32, kind="Internal").ap()
        block = ctx.enter_context(nc.Block())

        loads = [(w_qk, wqk), (b_qk, bqk), (w_v, wv), (b_v, bv_rows), (w_o, wo2), (b_o, bo),
                 (id_f, ident), (fold_f, fold), (gmean, group_mean), (w_z, wz), (w_x, wx), (n_w, norm_w),
                 (cw, conv_w), (cb, conv_b), (dtb, dt_bias), (a_neg, a_log), (dsk, d_skip), (w_out, wout),
                 (g_w, gnorm_w), (tri_f, tri), (ones_f, ones), (mask_f, neg_mask)]

        expert_loads = [(w1_f, w1), (w2_f, w2), (b1_f, b1), (b2_f, b2_blocks), (rw_f, router), (iota, iota8)]

        def scanned(engine, body):
            body(0, 0, True, False)
            with engine.Fori(0, B // 2 - 1) as i:
                for odd in range(2):
                    body(2 * i + (1 + odd), 1 - odd, False, False)
            body(B - 1, 1, False, True)

        def attended(engine, body):
            body(0, 0, True, False)
            with engine.Fori(0, B // 2 - 1) as i:
                for odd in range(2):
                    body(2 * i + (1 + odd), 1 - odd, False, False)
            body(B - 1, 1, False, True)

        def pictures(engine, body):
            with engine.Fori(0, B // 2 - 1) as i:
                for u in range(2):
                    body(2 * i + u, u, True)
            body(B - 2, 0, True)
            body(B - 1, 1, False)

        @block.sync
        def _(sp):
            for b in range(B):
                sp.dma_start(X[:, b, :], x[b]).then_inc(s_ld, 16)
                if b == 0:
                    for dst, src in loads[:9]:
                        sp.dma_start(dst[:], src).then_inc(s_w, 16)
                sp.wait_ge(s_ld, 16 * (b + 1))
            for dst, src in loads[9:]:
                sp.dma_start(dst[:], src).then_inc(s_w2, 16)
            sp.dma_start(cst_f[:, 0, :], sel_rows).then_inc(s_w2, 16)
            sp.dma_start(cst_f[:, 1, :], head_rows).then_inc(s_w2, 16)
            def decay_rows(b, u, first, last):
                sp.wait_ge(m_cte, b + 1)
                sp.sem_inc(s_turn, 1)
                if not first:
                    sp.wait_ge(m_df, NT * (b - 1) + 1)
                    sp.sem_inc(s_turn, 1)
                for part, src in ((0, cth), (1, ctl)):
                    sp.dma_start(cum_dram[u, part], src[:].bitcast(F32)).then_inc(m_rw, 16)
                sp.wait_ge(m_rw, 32 * (b + 1))
                for part in range(2):
                    rows = cum_dram[u, part].rearrange("(c h) t -> c h t", h=NH)
                    sp.dma_start(rhs_c[u][NT * part:NT * part + NT].bitcast(F32), rows).then_inc(m_rr, 16)
                    rows = cum_dram[u, part].rearrange("(c h) t -> h c t", h=NH)
                    r0 = 2 * NT + NH * part
                    sp.dma_start(lhs_c[u][r0:r0 + NH].bitcast(F32), rows).then_inc(m_rr, 16)
                sp.wait_ge(m_rr, 64 * (b + 1))
                sp.sem_inc(s_turn, 1)

            scanned(sp, decay_rows)
            sp.wait_ge(m_t2o, B)
            for dst, src in expert_loads:
                sp.dma_start(dst[:], src).then_inc(e_w, 16)
            with sp.Fori(0, B // 2) as i:
                for u in range(2):
                    b = 2 * i + u
                    sp.wait_ge(e_oc, b + 1)
                    sp.dma_start(out[b], o_ch[u][:]).then_inc(s_out, 16)
                    sp.wait_ge(s_out, 16 * (b + 1))
                    sp.sem_inc(s_turn, 1)

        @block.gpsimd
        def _(pool):
            nc.gpsimd.memset(neg_one[:], -1.0)
            nc.gpsimd.memset(eps_t[:], F32_EPS)
            nc.gpsimd.memset(neg_half[:], -0.5).then_inc(s_c, 1)
            pool.wait_ge(s_c, 1)
            for n, (b0, b1) in enumerate(stat_groups):
                pool.wait_ge(var_ready, n + 1)
                nc.gpsimd.tensor_tensor(grs[:, b0:b1], gvar[:, b0:b1], neg_half[:, b0:b1], ALU.pow).then_inc(rstd_ready, 1)
            pool.wait_ge(s_res, 2 * B)
            def heads(t):
                return t.rearrange("p (h d) -> p h d", h=NH)

            def per_head(t):
                return t.rearrange("p (h o) -> p h o", o=1).to_broadcast([t.shape[0], NH, HD])

            def fetch(b):
                if not isinstance(b, int) or b > 0:
                    pool.wait_ge(m_t1, b)
                nc.gpsimd.tensor_copy(xc[:], X[:, b, :]).then_inc(m_xc, 1)

            def norms(b):
                n = [0]

                def step(ins):
                    n[0] += 1
                    ins.then_inc(m_p2, 1)
                    pool.wait_ge(m_p2, POOL_FRONT_STEPS * b + n[0])

                pool.wait_ge(m_ve, b + 1)
                step(nc.gpsimd.tensor_tensor(rs1[:], bve[:], neg_half[:, 0:NT], ALU.pow))
                step(nc.gpsimd.tensor_tensor(rs2[:], rs1[:], rs1[:], ALU.mult))
                step(nc.gpsimd.tensor_tensor(rs2[:], rs2[:], bmv[:, :, 1], ALU.mult))
                step(nc.gpsimd.tensor_tensor(rs2[:], rs2[:], eps_t[:], ALU.add))
                step(nc.gpsimd.tensor_tensor(rs2[:], rs2[:], neg_half[:, 0:NT], ALU.pow))
                step(nc.gpsimd.tensor_tensor(rnb[:], rs1[:], bmv[:, :, 0], ALU.mult))
                step(nc.gpsimd.tensor_tensor(rnb[:], rnb[:], neg_one[:], ALU.mult))
                nc.gpsimd.tensor_tensor(rp1[:], rs1[:], ones_f[:, 0:NT], ALU.add).then_inc(m_rs, 1)
                nc.gpsimd.tensor_tensor(rs12[:], rs1[:], rs2[:], ALU.mult).then_inc(m_rs, 1)
                assert n[0] == POOL_FRONT_STEPS

            def operands(b, u, c):
                if c >= 2:
                    pool.wait_ge(m_Y, NT * b + c - 1)
                    pool.wait_ge(m_U, (NT - 1) * b + c - 1)
                nc.gpsimd.tensor_tensor(heads(xw[c % 2][:]), heads(xs[u][:, c, :]), per_head(wend[u][:, c, :]),
                                        ALU.mult).then_inc(m_xw, 1)
                nc.gpsimd.tensor_tensor(heads(xdt[c % 2][:]), heads(xs[u][:, c, :]), per_head(dts[u][:, c, :]),
                                        ALU.mult).then_inc(m_xd, 1)
                nc.gpsimd.tensor_tensor(heads(xsk[c % 2][:]), heads(xs[u][:, c, :]), per_head(dsk[:, :]),
                                        ALU.mult).then_inc(m_pm, 1)

            def root(b):
                pool.wait_ge(m_sv, b + 1)
                nc.gpsimd.tensor_tensor(srs[:], sve[:], neg_half[:, 0:NT], ALU.pow).then_inc(m_sr, 1)

            def scan(b, u, first, last):
                pool.wait_ge(m_w2, b + 1)
                pool.wait_ge(m_txe, 3 * b + 2)
                if not first:
                    pool.wait_ge(m_Y, NT * b)
                operands(b, u, 0)
                for c in range(NT):
                    if 1 <= c < NT - 1:
                        pool.wait_ge(m_S, (NT - 1) * b + c)
                        nc.gpsimd.tensor_tensor(heads(sdec[:]), heads(state[c % 2][:]),
                                                per_head(eo[u][0:DS, 2, NH * c:NH * c + NH]),
                                                ALU.mult).then_inc(m_sm, 1)
                    if c + 1 < NT:
                        operands(b, u, c + 1)
                    if c == 1 and not first:
                        root(b - 1)
                    pool.wait_ge(m_pm, NT * b + c + 1)
                    pool.wait_ge(m_y1, NT * b + c + 1)
                    nc.gpsimd.tensor_tensor(y2[c % 2][:], y1[c % 2][:], xsk[c % 2][:], ALU.add).then_inc(m_p3, 1)
                    pool.wait_ge(m_p3, NT * b + c + 1)
                    pool.wait_ge(m_zs, NT * b + NT)
                    if c >= 2 or not first:
                        pool.wait_ge(m_ty, NT * b + c - 1)
                        pool.wait_ge(m_sq, NT * b + c - 1)
                    nc.gpsimd.tensor_tensor(yz[c % 2][:], y2[c % 2][:], zs[u][:, c, :], ALU.mult).then_inc(m_yz, 1)
                    if c == 0 and not last:
                        fetch(b + 1)
                    if c == 1 and not last:
                        norms(b + 1)

            fetch(0)
            norms(0)
            scanned(pool, scan)
            root(B - 1)

            def norm(b, u):
                pool.wait_ge(e_ve, b + 1)
                nc.gpsimd.tensor_tensor(ers[:], eve[:], neg_half[:, 0:NT], ALU.pow).then_inc(e_rs, 1)
                pool.wait_ge(e_un, b + 1)
                pool.wait_ge(e_to, b - 1 if not isinstance(b, int) else max(b - 1, 0))
                nc.gpsimd.tensor_tensor(acc[u][:].rearrange("p t c -> p (t c)"), X[:, b, :],
                                        un[:].rearrange("p t c -> p (t c)"), ALU.add).then_inc(e_acc0, 1)

            def experts(b, u, more):
                if more:
                    norm(b + 1, 1 - u)

            norm(0, 0)
            pictures(pool, experts)

        @block.tensor
        def _(pe):
            def group_means(n):
                b0, b1 = stat_groups[n]
                pe.wait_ge(moments_ready, n + 1)
                nc.tensor.matmul(ps[:, 7, 2 * b0:2 * b1], gmean[:], gE[:, b0:b1, :].rearrange("p b s -> p (b s)"),
                                 start=True, stop=True).then_inc(groups_ready, 1)

            def scores(b, u, j, start=False):
                if not (start and j < 2):
                    pe.wait_ge(s_ex, NT * b + j - 1)
                for h in range(2):
                    o = S[j % 2][:, h, :]
                    kk = k_a[u][:, h * BANK:(h + 1) * BANK]
                    nc.tensor.matmul(o, q_a[u][:, j * P:(j + 1) * P], kk, start=True, stop=False)
                    last = nc.tensor.matmul(o, q_b[u][:, j * P:(j + 1) * P], kk, start=False, stop=True)
                last.then_inc(s_sc, 1)

            def projections(b):
                pe.wait_ge(s_xn, b + 1)
                for h in range(2):
                    last = nc.tensor.matmul(O[:, h, :], w_qk[:], xn[:, h * BANK:(h + 1) * BANK], start=True, stop=True)
                last.then_inc(s_qk, 1)

            def values(b):
                pe.wait_ge(s_l, 3 * b + 3)
                for k in range(NT):
                    last = nc.tensor.matmul(O[:, 0, k * DV:(k + 1) * DV], xn[:, k * P:(k + 1) * P], w_v[:],
                                            start=True, stop=True)
                last.then_inc(s_vp, 1)

            def turn(b, j, start):
                pe.wait_ge(s_ex, NT * b + j + 1)
                for h in range(2):
                    if not (start and j == 0):
                        pe.wait_ge(s_pl, 2 * (NT * b + j - 1) + h + 1)
                    for k in range(4):
                        last = nc.tensor.transpose(T[:, h, k * P:(k + 1) * P],
                                                   probs[:, j % 2, (4 * h + k) * P:(4 * h + k + 1) * P], id_f[:])
                    last.then_inc(s_tr, 1)

            def pv(b, u, h):
                pe.wait_ge(s_pl, 2 * NT * b + NT * (h + 1))
                for k in range(NT):
                    for part in (pt_h, pt_l):
                        last = nc.tensor.matmul(O[:, h, :], v_st[u][:, k, :], part[:, k, h * BANK:(h + 1) * BANK],
                                                start=(k == 0 and part is pt_h), stop=(k == NT - 1 and part is pt_l))
                last.then_inc(s_pv, 1)

            def fold_parts(b):
                pe.wait_ge(s_ot, b + 1)
                for j in range(NT):
                    last = nc.tensor.matmul(O[:, 0, j * DV:(j + 1) * DV], o_t[:, j * P:(j + 1) * P], fold_f[:],
                                            start=True, stop=True)
                last.then_inc(s_on, 1)

            def out_projection(b):
                pe.wait_ge(s_nrm, b + 1)
                for e in range(2):
                    r = slice(64 * e, 64 * e + 64)
                    last = nc.tensor.matmul(O[:, 1 - e, :], w_o[r, :], o_n[r].rearrange("p j v -> p (j v)"),
                                            start=True, stop=True)
                last.then_inc(s_wo, 1)

            def attend(b, u, first, last):
                for j in range(NT):
                    if j + 2 < NT:
                        scores(b, u, j + 2)
                    elif not last:
                        scores(b + 1, 1 - u, j + 2 - NT)
                    if j == 0 and not first:
                        pv(b - 1, 1 - u, 1)
                    turn(b, j, start=first)
                    if j == 1 and not first:
                        fold_parts(b - 1)
                    if j == 2 and not first:
                        out_projection(b - 1)
                    if j == 1 and first:
                        group_means(1)
                    if j == 3 and not last:
                        if not first:
                            pe.wait_ge(s_res, 2 * b)
                        projections(b + 1)
                    if j == 5 and not last:
                        values(b + 1)
                    if j == 6:
                        if last:
                            pe.wait_ge(s_res, 2 * b)
                        else:
                            pe.wait_ge(s_vf, b + 2)
                        pv(b, u, 0)
                    if j == 7 and first:
                        group_means(2)
                        pe.wait_ge(var_ready, 3)

            pe.wait_ge(s_w, 16 * 9)
            group_means(0)
            projections(0)
            values(0)
            pe.wait_ge(s_vf, 1)
            scores(0, 0, 0, start=True)
            scores(0, 0, 1, start=True)
            attended(pe, attend)
            pv(B - 1, 1, 1)
            fold_parts(B - 1)
            out_projection(B - 1)

            pe.wait_ge(m_gate, 1)
            lo_banks = ps[:, 0:2, :]
            hi_banks = ps[:, 2:4, :]

            def cols(banks, t, w):
                q = BANK // w
                return banks[:, t // q, (t % q) * w:(t % q + 1) * w]

            def split(o, lhs, rhs, N0=None):
                nc.tensor.matmul(o, lhs[0], rhs[0], start=True, stop=False)
                nc.tensor.matmul(o, lhs[0], rhs[1], start=False, stop=False)
                return nc.tensor.matmul(o, lhs[1], rhs[0], start=False, stop=True)

            def group(b, g, banks):
                for h in range(2):
                    r = slice(h * BANK, (h + 1) * BANK)
                    last = split(banks[:, h, :], (w_xh[:, g, :], w_xl[:, g, :]), (xh[:, r], xl[:, r]))
                last.then_inc(m_xg, 1)

            def turn_in(b):
                pe.wait_ge(m_xc, b + 1)
                if not isinstance(b, int):
                    pe.wait_ge(m_txe, 3 * b)
                    pe.wait_ge(m_t2o, b - 1)
                elif b > 0:
                    pe.wait_ge(m_txe, 3 * b)
                    if b > 1:
                        pe.wait_ge(m_t2o, b - 1)
                for t in range(NT):
                    last = nc.tensor.transpose(cols(lo_banks, t, P), xc[:, t * P:(t + 1) * P], id_f[:])
                last.then_inc(m_t1, 1)

            def turn_normed(b):
                pe.wait_ge(m_xnt, b + 1)
                if not isinstance(b, int) or b > 0:
                    pe.wait_ge(m_gs, b)
                for t in range(NT):
                    last = nc.tensor.transpose(cols(hi_banks, t, P), xt[:, t, :], id_f[:])
                last.then_inc(m_t2, 1)

            def group_0(b):
                pe.wait_ge(m_xl, b + 1)
                group(b, 0, hi_banks)

            def group_1(b):
                pe.wait_ge(m_r, b + 1)
                group(b, 1, lo_banks)

            def group_2(b):
                pe.wait_ge(m_cv, 3 * b + 1)
                group(b, 2, hi_banks)

            def gates(b):
                pe.wait_ge(m_cv, 3 * b + 2)
                for t in range(NT):
                    if t >= 2:
                        pe.wait_ge(m_zs, NT * b + t - 1)
                    r = slice(t * P, (t + 1) * P)
                    split(lo_banks[:, t % 2, 0:DI + NH], (xh[:, r], xl[:, r]), (w_zh[:], w_zl[:])).then_inc(m_z, 1)

            def turn_x(b):
                pe.wait_ge(m_si, 3 * b + 1)
                pe.wait_ge(m_zs, NT * b + NT)
                for t in range(NT):
                    last = nc.tensor.transpose(cols(lo_banks, t, P), xst[:, 0, t * P:(t + 1) * P], id_f[:])
                last.then_inc(m_tx, 1)
                pe.wait_ge(m_si, 3 * b + 2)
                pe.wait_ge(m_cv, 3 * b + 3)
                for t in range(NT):
                    last = nc.tensor.transpose(cols(hi_banks, t, P), xst[:, 1, t * P:(t + 1) * P], id_f[:])
                last.then_inc(m_tx, 1)

            def cumulate(b):
                pe.wait_ge(m_dt, b + 1)
                pe.wait_ge(m_txe, 3 * b + 1)
                nc.tensor.matmul(lo_banks[:, 0, 0:64], tri_f[:], dec_a[:], start=True, stop=True)
                nc.tensor.matmul(lo_banks[:, 0, 64:128], ones_f[:], dec_a[:], start=True, stop=True)
                nc.tensor.matmul(lo_banks[0:64, 1, 0:P], dec_a[:], tri_f[:], start=True, stop=True).then_inc(m_cum, 1)

            def turn_b(b):
                pe.wait_ge(m_si, 3 * b + 3)
                pe.wait_ge(m_cte, b + 1)
                pe.wait_ge(m_e1, 2 * b + 2)
                pe.sem_inc(s_turn, 1)
                for t in range(NT):
                    last = nc.tensor.transpose(lo_banks[:, 0, t * DS:(t + 1) * DS], b_t[:, t * P:(t + 1) * P],
                                               id_f[0:DS, 0:DS])
                last.then_inc(m_tx, 1)

            def inner_products(b, u):
                pe.wait_ge(m_txe, 3 * b + 2)
                for t in range(NT):
                    r = slice(t * P, (t + 1) * P)
                    last = nc.tensor.matmul(cols(hi_banks, t, P), b_t[:, r], c_t[u][:, r], start=True, stop=True)
                last.then_inc(m_gp, 1)

            def decay(b, u, c, first=False):
                if c == 0:
                    pe.wait_ge(m_rr, 64 * (b + 1))
                if not (first and c == 0):
                    pe.wait_ge(m_L, NT * b + c)
                for h in range(2):
                    o = ps[:, 4 + h, :]
                    nc.tensor.matmul(o, id_r[:], mask_r[:], start=True, stop=False)
                    done = nc.tensor.matmul(o, lhs_c[u][:, c, :],
                                            rhs_c[u][:, 4 * h:4 * h + 4, :].rearrange("p h t -> p (h t)"),
                                            start=False, stop=True)
                done.then_inc(m_df, 1)

            def turn_y(b, c):
                pe.wait_ge(m_yz, NT * b + c + 1)
                pe.wait_ge(m_S, (NT - 1) * b + min(c + 1, NT - 1))
                if c == NT - 1:
                    pe.wait_ge(m_yT, NT * b + c)
                for g in range(2):
                    last = nc.tensor.transpose(ps[:, 7, g * P:(g + 1) * P], yz[c % 2][:, g * P:(g + 1) * P], id_f[:])
                last.then_inc(m_ty, 1)

            def out_product(b):
                pe.wait_ge(m_yT, NT * b + NT)
                if isinstance(b, int) and b == B - 1:
                    pass
                else:
                    pe.wait_ge(m_txe, 3 * b + 6)
                for c in range(NT):
                    for g in range(2):
                        last = nc.tensor.matmul(cols(lo_banks, c, P), y_t[:, g, c * P:(c + 1) * P], w_out[:, g, :],
                                                start=(g == 0), stop=(g == 1))
                last.then_inc(m_op, 1)

            def scan(b, u, first, last):
                for c in range(NT):
                    if c == 0:
                        decay(b, u, 0, first)
                        if not first:
                            turn_y(b - 1, NT - 1)
                            out_product(b - 1)
                    if c + 1 < NT:
                        decay(b, u, c + 1)
                    if c >= 1:
                        turn_y(b, c - 1)
                        pe.wait_ge(m_S, (NT - 1) * b + c)
                    if c >= 1 or not first:
                        pe.wait_ge(m_y1, NT * b + c)
                    if c >= 1:
                        nc.tensor.matmul(ps[:, 6, DI:2 * DI], c_t[u][:, c * P:(c + 1) * P], state[c % 2][:],
                                         start=True, stop=True)
                    pe.wait_ge(m_M, NT * b + c + 1)
                    pe.wait_ge(m_xd, NT * b + c + 1)
                    for h in range(NH):
                        done = nc.tensor.matmul(ps[:, 6, h * HD:(h + 1) * HD], mix[c % 2][:, h, :],
                                                xdt[c % 2][:, h * HD:(h + 1) * HD], start=True, stop=True)
                    done.then_inc(m_Y, 1)
                    if c < NT - 1:
                        pe.wait_ge(m_xw, NT * b + c + 1)
                        if c >= 1 or not first:
                            pe.wait_ge(m_yT, NT * b + c)
                        nc.tensor.matmul(ps[0:DS, 7, 0:DI], b_tok[u][:, c, :], xw[c % 2][:], start=True,
                                         stop=True).then_inc(m_U, 1)
                    if not last:
                        pieces(b + 1, 1 - u, c)

            def pieces(b, u, slot):
                if slot == 1:
                    turn_in(b)
                if slot == 2:
                    turn_normed(b)
                    group_0(b)
                if slot == 3:
                    group_1(b)
                if slot == 4:
                    group_2(b)
                if slot == 5:
                    gates(b)
                if slot == 6:
                    turn_x(b)
                if slot == 7:
                    cumulate(b)
                    turn_b(b)
                    inner_products(b, u)

            for slot in range(NT):
                pieces(0, 0, slot)
            scanned(pe, scan)
            turn_y(B - 1, NT - 1)
            out_product(B - 1)

            pe.wait_ge(e_wc, 1)

            def expert(b, u, n):
                e, h = n // 2, n % 2
                if n >= 2 or not isinstance(b, int) or b > 0:
                    pe.wait_ge(e_g, 2 * NE * b + n - 1)
                pe.wait_ge(e_ul, b + 1)
                r = slice(h * BANK, (h + 1) * BANK)
                split(ps[:, 4 + n % 2, :], (w1_h[:, e, :], w1_l[:, e, :]), (uh[u][:, r], ul[u][:, r])).then_inc(e_h, 1)

            def second(b, n):
                e, h = n // 2, n % 2
                pe.wait_ge(e_g, 2 * NE * b + n + 1)
                if n >= 2:
                    pe.wait_ge(e_a, 2 * NE * b + n - 1)
                for t in range(4):
                    last = nc.tensor.matmul(ps[:, 6 + n % 2, t * P:(t + 1) * P], hid[n % 2][:, t * P:(t + 1) * P],
                                            w2_f[:, e, :], start=True, stop=True)
                last.then_inc(e_y, 1)

            def turn_tokens(b):
                pe.wait_ge(e_un, b + 1)
                pe.wait_ge(e_bba, b)
                for t in range(NT):
                    last = nc.tensor.transpose(cols(lo_banks, t, P), un[:, t, :], id_f[:])
                last.then_inc(e_tr, 1)

            def logits(b, u):
                pe.wait_ge(e_ul, b + 1)
                pe.wait_ge(e_oc, b - 1 if not isinstance(b, int) else max(b - 1, 0))
                for t in range(NT):
                    r = slice(t * P, (t + 1) * P)
                    last = split(ps[:, 2, t * NE:(t + 1) * NE], (uh[u][:, r], ul[u][:, r]), (rw_h[:], rw_l[:]))
                last.then_inc(e_lg, 1)

            def turn_weights(b, u):
                pe.wait_ge(e_cb, b + 1)
                pe.sem_inc(s_turn, 1)
                nc.tensor.transpose(ps[0:NT * NE, 3, 0:P], comb[u][:].rearrange("p t e -> p (t e)"),
                                    id_f[:]).then_inc(e_ct, 1)

            def second_biases(b):
                pe.wait_ge(e_ctc, b + 1)
                for h in range(2):
                    last = nc.tensor.matmul(lo_banks[:, h, :], comb_t[:], b2_f[:, h * BANK:(h + 1) * BANK],
                                            start=True, stop=True)
                last.then_inc(e_bb, 1)

            def experts(b, u, more):
                for n in range(2 * NE):
                    second(b, n)
                    if n + 2 < 2 * NE:
                        expert(b, u, n + 2)
                    elif more:
                        expert(b + 1, 1 - u, n + 2 - 2 * NE)
                    if more and n == 4:
                        turn_tokens(b + 1)
                    if more and n == 7:
                        logits(b + 1, 1 - u)
                    if more and n == 13:
                        turn_weights(b + 1, 1 - u)
                    if more and n == 14:
                        second_biases(b + 1)
                pe.wait_ge(e_a, 2 * NE * b + 2 * NE)
                for t in range(NT):
                    last = nc.tensor.transpose(cols(hi_banks, t, P), acc[u][:, t, :], id_f[:])
                last.then_inc(e_to, 1)

            turn_tokens(0)
            logits(0, 0)
            expert(0, 0, 0)
            expert(0, 0, 1)
            turn_weights(0, 0)
            second_biases(0)
            pictures(pe, experts)

        @block.scalar
        def _(act):
            def q_and_k(b, u):
                act.wait_ge(s_qk, b + 1)
                tq = O[0:DK].rearrange("p a (c r) -> p (a c) r", r=R)
                for dst, r0 in ((q_a[u], 0), (q_b[u], DK)):
                    nc.scalar.activation(dst[r0:r0 + DK].rearrange("p (r c) -> p c r", r=R), tq,
                                         ACT.Identity, bias=b_qk[0:DK, 0:1]).then_inc(s_h, 1)
                nc.scalar.activation(k_a[u][0:DK].rearrange("p (a n) -> p a n", a=2), O[DK:2 * DK],
                                     ACT.Identity, bias=b_qk[DK:2 * DK, 0:1]).then_inc(s_h, 1)

            def exponentials(b, u, j, start=False):
                act.wait_ge(s_mx, NT * b + j + 1)
                if not (start and j < 2):
                    act.wait_ge(s_tr, 2 * (NT * b + j - 1))
                nc.scalar.activation(probs[:, j % 2, :].rearrange("p (a n) -> p a n", a=2), S[j % 2], ACT.Exp,
                                     bias=nmax[:, j:j + 1], accum_out=rsum[u][:, j:j + 1]).then_inc(s_ex, 1)

            def high(b, j, h):
                act.wait_ge(s_tr, 2 * (NT * b + j) + h + 1)
                nc.scalar.activation(pt_h[:, 4 * h:4 * h + 4, j * P:(j + 1) * P],
                                     T[:, h, :].rearrange("p (k n) -> p k n", n=P), ACT.Copy).then_inc(s_ph, 1)

            def attend(b, u, first, last):
                for j in range(NT):
                    if not first and j in (0, 4):
                        act.wait_ge(s_pv, 2 * b - 1 + j // 4)
                    if j + 1 < NT:
                        exponentials(b, u, j + 1, start=first)
                    elif not last:
                        exponentials(b + 1, 1 - u, 0)
                    high(b, j, 0)
                    high(b, j, 1)
                    if j == 0 and not first:
                        act.wait_ge(s_pv, 2 * b)
                        nc.scalar.activation(o_t[:].rearrange("p (a n) -> p a n", a=2), O, ACT.Copy).then_inc(s_ot, 1)
                    if j == 3 and not last:
                        q_and_k(b + 1, 1 - u)

            act.wait_ge(s_w, 16 * 9)
            nc.scalar.preload_act_table_set("exp_and_others")
            act.wait_ge(s_own, 1)
            q_and_k(0, 0)
            exponentials(0, 0, 0, start=True)
            attended(act, attend)
            act.wait_ge(s_pv, 2 * B)
            nc.scalar.activation(o_t[:].rearrange("p (a n) -> p a n", a=2), O, ACT.Copy).then_inc(s_ot, 1)
            act.wait_ge(s_w2, 16 * (len(loads) - 9 + 2))
            nc.scalar.activation(a_neg[:], a_neg[:], ACT.Exp).then_inc(m_q2, 1)

            lo_banks = ps[:, 0:2, :]
            hi_banks = ps[:, 2:4, :]
            act.wait_ge(m_gate, 1)

            def two(t):
                return t.rearrange("p (a n) -> p a n", a=2)

            def shortcut(b, u):
                act.wait_ge(m_xnt, b + 1)
                act.wait_ge(m_rs, 2 * b + 1)
                if not isinstance(b, int) or b > 1:
                    act.wait_ge(m_t2o, b - 1)
                    act.wait_ge(m_yz, NT * (b - 1))
                for t in range(NT):
                    last = nc.scalar.activation(res[u][:, t, :], lo_banks[:, t // 4, (t % 4) * P:(t % 4 + 1) * P],
                                                ACT.Identity, bias=rnb[:, t:t + 1], scale=rp1[:, t:t + 1])
                last.then_inc(m_r, 1)

            def high(b):
                act.wait_ge(m_t2, b + 1)
                nc.scalar.activation(two(xh[:]), hi_banks, ACT.Copy).then_inc(m_xh, 1)

            def tap(b, g):
                banks = (hi_banks, lo_banks, hi_banks)[g]
                act.wait_ge(m_xg, 3 * b + g + 1)
                nc.scalar.activation(two(cacc[:, g, :]), banks, ACT.Identity, bias=cb[:, g:g + 1],
                                     scale=cw[:, g, DCONV - 1:DCONV]).then_inc(m_tap, 1)

            def silus(b, u):
                for t in range(NT):
                    act.wait_ge(m_z, NT * b + t + 1)
                    nc.scalar.activation(dtr[:, t, :], lo_banks[:, t % 2, DI:DI + NH], ACT.Copy)
                    nc.scalar.activation(zs[u][:, t, :], lo_banks[:, t % 2, 0:DI], ACT.Silu).then_inc(m_zs, 1)
                for g in range(2):
                    act.wait_ge(m_cv, 3 * b + g + 1)
                    nc.scalar.activation(xst[:, g, :], cacc[:, g, :], ACT.Silu).then_inc(m_si, 1)
                act.wait_ge(m_cv, 3 * b + 3)
                nc.scalar.activation(b_t[:], cacc[0:DS, 2, :], ACT.Silu)
                nc.scalar.activation(c_t[u][:], cacc[DS:2 * DS, 2, :], ACT.Silu).then_inc(m_si, 1)
                nc.scalar.preload_act_table_set("natural_log_exp_and_others")

            def softplus(b):
                act.wait_ge(m_e1, 2 * b + 1)
                nc.scalar.activation(dte[:], dta[:], ACT.Exp, scale=-1.0).then_inc(m_a2, 1)
                act.wait_ge(m_a2, 2 * b + 1)
                nc.scalar.activation(dtl[:], dte[:], ACT.Ln, bias=1.0).then_inc(m_a2, 1)

            def gather_x(b, u):
                for g in range(2):
                    act.wait_ge(m_tx, 3 * b + g + 1)
                    nc.scalar.activation(xs[u][:, :, g * P:(g + 1) * P].rearrange("p (a t) c -> p a t c", a=2),
                                         (lo_banks, hi_banks)[g].rearrange("p a (t c) -> p a t c", c=P),
                                         ACT.Copy).then_inc(m_txe, 1)

            def factors(b, u):
                act.wait_ge(m_e1, 2 * b + 2)
                nc.scalar.activation(eo[u][:], ein[:], ACT.Exp).then_inc(m_eo, 1)

            def gather_b(b, u):
                act.wait_ge(m_tx, 3 * b + 3)
                nc.scalar.activation(b_tok[u][:].rearrange("p t s -> p (t s)"), lo_banks[:, 0, 0:NT * DS],
                                     ACT.Copy).then_inc(m_txe, 1)

            def turned(b, c):
                act.wait_ge(m_ty, NT * b + c + 1)
                nc.scalar.activation(y_t[:, :, c * P:(c + 1) * P], ps[:, 7, 0:2 * P].rearrange("p (g t) -> p g t", g=2),
                                     ACT.Copy).then_inc(m_yT, 1)

            def square(b, c):
                act.wait_ge(m_yz, NT * b + c + 1)
                nc.scalar.activation(sq[c % 2][:], yz[c % 2][:], ACT.Square, accum_out=ssq[:, c:c + 1]).then_inc(m_sq, 1)

            def decays(b, c, first):
                act.wait_ge(m_df, NT * b + c + 1)
                if c >= 2 or not first:
                    act.wait_ge(m_Y, NT * b + c - 1)
                nc.scalar.activation(dcy[c % 2][:].rearrange("p (a h) t -> p a (h t)", a=2), ps[:, 4:6, :],
                                     ACT.Exp).then_inc(m_L, 1)

            def scan(b, u, first, last):
                for c in range(NT):
                    if c == 0:
                        decays(b, 0, first)
                        if not first:
                            square(b - 1, NT - 1)
                            turned(b - 1, NT - 1)
                    if c + 1 < NT:
                        decays(b, c + 1, first)
                    if c == 1 and not first:
                        act.wait_ge(m_op, b)
                        act.wait_ge(m_sv, b)
                    if c >= 1:
                        square(b, c - 1)
                        turned(b, c - 1)
                    if not last:
                        pieces(b + 1, 1 - u, c)

            def pieces(b, u, slot):
                if slot == 2:
                    shortcut(b, u)
                    high(b)
                if slot == 3:
                    tap(b, 0)
                    tap(b, 1)
                if slot == 4:
                    tap(b, 2)
                if slot == 5:
                    silus(b, u)
                if slot == 6:
                    softplus(b)
                    gather_x(b, u)
                if slot == 7:
                    factors(b, u)
                    gather_b(b, u)

            for slot in range(NT):
                pieces(0, 0, slot)
            scanned(act, scan)
            square(B - 1, NT - 1)
            turned(B - 1, NT - 1)

            def high(b, u):
                act.wait_ge(e_tr, b + 1)
                nc.scalar.activation(two(uh[u][:]), lo_banks, ACT.Copy).then_inc(e_uh, 1)

            def exponentials(b):
                act.wait_ge(e_top, b + 1)
                nc.scalar.activation(tex[:], tsh[:], ACT.Exp).then_inc(e_ex, 1)

            def gelu(b, n):
                act.wait_ge(e_h, 2 * NE * b + n + 1)
                if n >= 2 or not isinstance(b, int) or b > 0:
                    act.wait_ge(e_y, 2 * NE * b + n - 1)
                nc.scalar.activation(hid[n % 2][:], ps[:, 4 + n % 2, :], ACT.Gelu,
                                     bias=b1_f[:, n // 2:n // 2 + 1]).then_inc(e_g, 1)

            def experts(b, u, more):
                for n in range(2, 2 * NE):
                    gelu(b, n)
                    if more and n == 6:
                        high(b + 1, 1 - u)
                    if more and n == 11:
                        exponentials(b + 1)
                if more:
                    gelu(b + 1, 0)
                    gelu(b + 1, 1)
                act.wait_ge(e_to, b + 1)
                act.wait_ge(s_out, 16 * (b - u))
                nc.scalar.activation(two(o_ch[u][:]), hi_banks, ACT.Copy).then_inc(e_oc, 1)

            high(0, 0)
            exponentials(0)
            gelu(0, 0)
            gelu(0, 1)
            pictures(act, experts)

        @block.vector
        def _(dve):
            def statistics(b):
                dve.wait_ge(s_ld, 16 * (b + 1))
                for h in range(2):
                    last = nc.vector.bn_stats(gst[:, b, h, :], X[:, b, h * BANK:(h + 1) * BANK])
                last.then_inc(s_bn, 1)
                dve.wait_ge(s_bn, b + 1)
                return nc.vector.bn_aggr(gmv[:, b, :], gst[:, b, :, :].rearrange("p h s -> p (h s)"))

            own = [0]

            def link(ins):
                own[0] += 1
                ins.then_inc(s_own, 1)
                dve.wait_ge(s_own, own[0])

            def moments(n):
                b = slice(*stat_groups[n])
                nc.vector.tensor_copy(gE[:, b, 0], gmv[:, b, 0])
                link(nc.vector.tensor_tensor(gE[:, b, 1], gmv[:, b, 0], gmv[:, b, 0], ALU.mult))
                nc.vector.tensor_tensor(gE[:, b, 1], gE[:, b, 1], gmv[:, b, 1], ALU.add).then_inc(moments_ready, 1)

            def variances(n):
                b = slice(*stat_groups[n])
                dve.wait_ge(groups_ready, n + 1)
                means = ps[:, 7, 2 * b.start:2 * b.stop].rearrange("p (b s) -> p b s", s=2)
                link(nc.vector.tensor_copy(gm[:, b, :], means))
                link(nc.vector.tensor_tensor(gvar[:, b], gm[:, b, 0], gm[:, b, 0], ALU.mult))
                link(nc.vector.tensor_tensor(gvar[:, b], gm[:, b, 1], gvar[:, b], ALU.subtract))
                nc.vector.tensor_scalar(gvar[:, b], gvar[:, b], 0.0, GN_EPS, ALU.max, ALU.add).then_inc(var_ready, 1)

            def normalize(b, n):
                dve.wait_ge(rstd_ready, n + 1)
                nc.vector.tensor_scalar(xn[:], X[:, b, :], gm[:, b, 0:1], grs[:, bass.ds(b, 1)],
                                        ALU.subtract, ALU.mult).then_inc(s_xn, 1)

            def q_and_k(b, u):
                dve.wait_ge(s_h, 3 * b + 3)
                tq = O[0:DK].rearrange("p a (c r) -> p (a c) r", r=R)
                qh = q_a[u][0:DK].bitcast(F32).rearrange("p (r c) -> p c r", r=R)
                for dst, r0 in ((q_b[u], 0), (q_a[u], DK)):
                    nc.vector.scalar_tensor_tensor(dst[r0:r0 + DK].rearrange("p (r c) -> p c r", r=R), tq,
                                                   b_qk[0:DK, 0:1], qh, ALU.add, ALU.subtract).then_inc(s_l, 1)
                nc.vector.scalar_tensor_tensor(k_a[u][DK:2 * DK].rearrange("p (a n) -> p a n", a=2), O[DK:2 * DK],
                                               b_qk[DK:2 * DK, 0:1],
                                               k_a[u][0:DK].bitcast(F32).rearrange("p (a n) -> p a n", a=2),
                                               ALU.add, ALU.subtract).then_inc(s_l, 1)

            def v_parts(b, u):
                dve.wait_ge(s_vp, b + 1)
                v_bias = b_v[:].rearrange("p (o v) -> p o v", o=1).to_broadcast([P, NT, DV])
                nc.vector.tensor_tensor(v_f[:], O[:, 0, :].rearrange("p (k v) -> p k v", v=DV), v_bias,
                                        ALU.add).then_inc(s_vf, 1)
                dve.wait_ge(s_vf, b + 1)
                nc.vector.tensor_copy(v_st[u][:, :, 0:DV], v_f[:]).then_inc(s_vh, 1)
                dve.wait_ge(s_vh, b + 1)
                nc.vector.tensor_tensor(v_st[u][:, :, DV:2 * DV], v_f[:], v_st[u][:, :, 0:DV].bitcast(F32),
                                        ALU.subtract).then_inc(s_vsb, 1)

            def maximum(b, j):
                dve.wait_ge(s_sc, NT * b + j + 1)
                nc.vector.tensor_reduce(nmax[:, j:j + 1], S[j % 2], AX_XY, ALU.max, negate=True).then_inc(s_mx, 1)

            def low(b, j, h):
                dve.wait_ge(s_ph, 2 * (NT * b + j) + h + 1)
                part = (slice(None), slice(4 * h, 4 * h + 4), slice(j * P, (j + 1) * P))
                nc.vector.tensor_tensor(pt_l[part], T[:, h, :].rearrange("p (k n) -> p k n", n=P),
                                        pt_h[part].bitcast(F32), ALU.subtract).then_inc(s_pl, 1)

            def divide(b, u):
                dve.wait_ge(s_ex, NT * b + NT)
                nc.vector.reciprocal(rinv[:], rsum[u][:]).then_inc(s_ri, 1)
                dve.wait_ge(s_ri, b + 1)
                dve.wait_ge(s_on, b + 1)
                nc.vector.tensor_tensor(o_n[:], O[:, 0, :].rearrange("p (k v) -> p k v", v=DV),
                                        rinv[:].rearrange("p (k o) -> p k o", o=1).to_broadcast([P, NT, DV]),
                                        ALU.mult).then_inc(s_nrm, 1)

            def residual(b):
                dve.wait_ge(s_wo, b + 1)
                for e in range(2):
                    xe = X[:, b, :].rearrange("p (j e v) -> p e j v", e=2, v=DV)[:, e]
                    nc.vector.scalar_tensor_tensor(xe, O[:, 1 - e, :].rearrange("p (j v) -> p j v", v=DV),
                                                   b_o[:, 0:1], xe, ALU.add, ALU.add).then_inc(s_res, 1)

            def attend(b, u, first, last):
                for j in range(NT):
                    if j + 2 < NT:
                        maximum(b, j + 2)
                    elif not last:
                        maximum(b + 1, j + 2 - NT)
                    low(b, j, 0)
                    low(b, j, 1)
                    if j == 0 and first:
                        statistics(1).then_inc(s_own, 1)
                        own[0] += 1
                        dve.wait_ge(s_own, own[0])
                        moments(1)
                    if j == 1 and first:
                        variances(1)
                    if first and 1 <= j < B - 1:
                        aggregated = statistics(j + 1)
                    if first and j == NT - 1:
                        link(aggregated)
                        moments(2)
                        variances(2)
                    if j == 1 and not first:
                        divide(b - 1, 1 - u)
                    if j == 2 and not first:
                        residual(b - 1)
                    if j == 2 and not last:
                        normalize(b + 1, 1 if first else 2)
                    if j == 4 and not last:
                        q_and_k(b + 1, 1 - u)
                    if j == 5 and not last:
                        v_parts(b + 1, 1 - u)

            dve.wait_ge(s_w, 16 * 9)
            nc.vector.tensor_scalar(w_qk[:, 0:DK], w_qk[:, 0:DK], QSCALE, None, ALU.mult)
            link(nc.vector.tensor_scalar(b_qk[0:DK, :], b_qk[0:DK, :], QSCALE, None, ALU.mult))
            link(statistics(0))
            moments(0)
            variances(0)
            normalize(0, 0)
            q_and_k(0, 0)
            v_parts(0, 0)
            maximum(0, 0)
            maximum(0, 1)
            attended(dve, attend)
            divide(B - 1, 1)
            residual(B - 1)

            dve.wait_ge(s_w2, 16 * (len(loads) - 9 + 2))
            link(nc.vector.tensor_scalar(w_z[:], w_z[:], n_w[:, 0:1], None, ALU.mult))
            link(nc.vector.tensor_scalar(w_x[:], w_x[:], n_w[:, 0:1], None, ALU.mult))
            for g in range(2):
                nc.vector.tensor_scalar(w_out[:, g, :], w_out[:, g, :], g_w[:, g:g + 1], None, ALU.mult)
            nc.vector.tensor_copy(w_zh[:], w_z[:])
            nc.vector.tensor_copy(w_xh[:], w_x[:])
            nc.vector.tensor_copy(mask_r[:], mask_f[:])
            nc.vector.tensor_copy(id_r[:], id_f[:])
            for u in range(2):
                nc.vector.tensor_copy(lhs_c[u][:].rearrange("p c t -> p (c t)"), cst_f[:, 0, :])
                done = nc.vector.tensor_copy(rhs_c[u][:].rearrange("p c t -> p (c t)"), cst_f[:, 1, :])
            link(done)
            nc.vector.tensor_tensor(w_zl[:], w_z[:], w_zh[:].bitcast(F32), ALU.subtract)
            link(nc.vector.tensor_tensor(w_xl[:], w_x[:], w_xh[:].bitcast(F32), ALU.subtract))
            dve.wait_ge(m_q2, 1)
            link(nc.vector.tensor_scalar(a_neg[:], a_neg[:], -1.0, None, ALU.mult))

            lo_banks = ps[:, 0:2, :]
            hi_banks = ps[:, 2:4, :]
            dve.wait_ge(s_res, 2 * B)
            dve.sem_inc(m_gate, 1)

            def two(t):
                return t.rearrange("p (a n) -> p a n", a=2)

            def heads(t):
                return t.rearrange("p (h d) -> p h d", h=NH)

            def per_head(t, d=HD):
                return t.rearrange("p (h o) -> p h o", o=1).to_broadcast([t.shape[0], NH, d])

            def tile(t):
                return lo_banks[:, t // 4, (t % 4) * P:(t % 4 + 1) * P]

            def front(b, u):
                n = [0]
                xf = dtr[:].rearrange("p c h -> p (c h)")
                df = dts[u][:].rearrange("p c h -> p (c h)")

                def step(ins):
                    n[0] += 1
                    ins.then_inc(m_v2, 1)
                    dve.wait_ge(m_v2, DVE_FRONT_STEPS * b + n[0])

                def statistics():
                    dve.wait_ge(m_t1, b + 1)
                    for t in range(NT):
                        last = nc.vector.bn_stats(bst[:, t, :], tile(t))
                    step(last)
                    dve.sem_inc(s_turn, 1)
                    for t in range(NT):
                        last = nc.vector.bn_aggr(bmv[:, t, :], bst[:, t, :])
                    step(last)
                    nc.vector.tensor_scalar(bve[:], bmv[:, :, 1], LN_EPS, None, ALU.add).then_inc(m_ve, 1)

                def normed():
                    dve.wait_ge(m_rs, 2 * b + 2)
                    for t in range(NT):
                        last = nc.vector.tensor_scalar(xt[:, t, :], tile(t), bmv[:, t, 0:1], rs12[:, t:t + 1],
                                                       ALU.subtract, ALU.mult)
                    last.then_inc(m_xnt, 1)

                def low():
                    dve.wait_ge(m_xh, b + 1)
                    nc.vector.tensor_tensor(two(xl[:]), hi_banks, two(xh[:].bitcast(F32)),
                                            ALU.subtract).then_inc(m_xl, 1)

                def conv(g):
                    rows = P if g < 2 else 2 * DS
                    banks = (hi_banks, lo_banks, hi_banks)[g][0:rows].rearrange("p a n -> p (a n)")
                    dve.wait_ge(m_tap, 3 * b + g + 1)
                    for k in range(1, DCONV):
                        ins = nc.vector.scalar_tensor_tensor(cacc[0:rows, g, k:N], banks[:, 0:N - k],
                                                             cw[0:rows, g, DCONV - 1 - k:DCONV - k],
                                                             cacc[0:rows, g, k:N], ALU.mult, ALU.add)
                        if k < DCONV - 1:
                            step(ins)
                    ins.then_inc(m_cv, 1)

                def steps():
                    dve.wait_ge(m_zs, NT * b + NT)
                    step(nc.vector.tensor_tensor(dtr[:], dtr[:],
                                                 dtb[:].rearrange("p (o h) -> p o h", o=1).to_broadcast([P, NT, NH]),
                                                 ALU.add))
                    nc.vector.scalar_tensor_tensor(dta[:], xf, -1.0, xf, ALU.mult, ALU.max).then_inc(m_e1, 1)

                def softplus():
                    dve.wait_ge(m_a2, 2 * b + 2)
                    step(nc.vector.tensor_scalar(dtw[:], dte[:], 1.0, None, ALU.add))
                    nc.vector.reciprocal(dti[:], dtw[:])
                    step(nc.vector.tensor_scalar(dtc[:], dtw[:], -1.0, None, ALU.add))
                    step(nc.vector.tensor_tensor(dtc[:], dte[:], dtc[:], ALU.subtract))
                    step(nc.vector.tensor_tensor(dtc[:], dtc[:], dti[:], ALU.mult))
                    step(nc.vector.tensor_tensor(dtl[:], dtl[:], dtc[:], ALU.add))
                    step(nc.vector.scalar_tensor_tensor(df, xf, 0.0, dtl[:], ALU.max, ALU.add))
                    nc.vector.tensor_tensor(dec_a[:].rearrange("p (c h) -> p c h", h=NH), dts[u][:],
                                            a_neg[:].rearrange("p (o h) -> p o h", o=1).to_broadcast([P, NT, NH]),
                                            ALU.mult).then_inc(m_dt, 1)

                def exponents():
                    dve.wait_ge(m_cum, b + 1)
                    nc.vector.tensor_copy(ein[:, 2, :], ps[:, 0, 64:128])
                    if not isinstance(b, int) or b > 0:
                        dve.wait_ge(m_rr, 64 * b)
                    nc.vector.tensor_copy(ein[:, 0, :], ps[:, 0, 0:64])
                    step(nc.vector.tensor_copy(cth[:], ps[0:64, 1, 0:P]))
                    nc.vector.tensor_tensor(ctl[:], ps[0:64, 1, 0:P], cth[:].bitcast(F32),
                                            ALU.subtract).then_inc(m_cte, 1)
                    nc.vector.tensor_tensor(ein[:, 1, :], ps[:, 0, 64:128], ein[:, 0, :], ALU.subtract).then_inc(m_e1, 1)

                def ends():
                    dve.wait_ge(m_eo, b + 1)
                    nc.vector.tensor_tensor(wend[u][:].rearrange("p c h -> p (c h)"), eo[u][:, 1, :], df,
                                            ALU.mult).then_inc(m_w2, 1)

                def inner():
                    assert n[0] == DVE_FRONT_STEPS, n
                    dve.wait_ge(m_gp, b + 1)
                    nc.vector.tensor_copy(g_sb[u][:].rearrange("p (a t) s -> p a (t s)", a=2), hi_banks).then_inc(m_gs, 1)
                    dve.wait_ge(m_gs, b + 1)

                return {1: (statistics,), 2: (normed, low), 3: (lambda: conv(0),), 4: (lambda: conv(1),),
                        5: (lambda: conv(2), steps), 6: (softplus,), 7: (exponents, ends, inner)}

            def mixed(b, u, c):
                dve.wait_ge(m_L, NT * b + c + 1)
                nc.vector.tensor_tensor(mix[c % 2][:], dcy[c % 2][:],
                                        g_sb[u][:, c:c + 1, :].to_broadcast([P, NH, P]), ALU.mult).then_inc(m_M, 1)

            def mean_square(b):
                dve.wait_ge(m_sq, NT * b + NT)
                nc.vector.tensor_scalar(sve[:], ssq[:], 1.0 / DI, GN2_EPS, ALU.mult, ALU.add).then_inc(m_sv, 1)

            def output(b, u):
                dve.wait_ge(m_sr, b + 1)
                dve.wait_ge(m_op, b + 1)
                for c in range(NT):
                    last = nc.vector.scalar_tensor_tensor(X[:, b, c * P:(c + 1) * P], tile(c),
                                                          srs[:, c:c + 1], res[u][:, c, :], ALU.mult, ALU.add)
                last.then_inc(m_t2o, 1)

            def scan(b, u, first, last):
                parts = front(b + 1, 1 - u) if not last else {}
                mixed(b, u, 0)
                for c in range(NT):
                    if c < NT - 1:
                        mixed(b, u, c + 1)
                    if c == 0 and not first:
                        mean_square(b - 1)
                    dve.wait_ge(m_Y, NT * b + c + 1)
                    if c >= 2 or not first:
                        dve.wait_ge(m_yz, NT * b + c - 1)
                    if c == 0:
                        nc.vector.tensor_copy(y1[0][:], ps[:, 6, 0:DI]).then_inc(m_y1, 1)
                    else:
                        nc.vector.tensor_tensor(heads(yof[:]), heads(ps[:, 6, DI:2 * DI]),
                                                per_head(eo[u][:, 0, NH * c:NH * c + NH]), ALU.mult).then_inc(m_v3, 1)
                        dve.wait_ge(m_v3, (NT - 1) * b + c)
                        nc.vector.tensor_tensor(y1[c % 2][:], ps[:, 6, 0:DI], yof[:], ALU.add).then_inc(m_y1, 1)
                    if c < NT - 1:
                        dve.wait_ge(m_U, (NT - 1) * b + c + 1)
                        if c == 0:
                            nc.vector.tensor_copy(state[1][:], ps[0:DS, 7, 0:DI]).then_inc(m_S, 1)
                        else:
                            dve.wait_ge(m_sm, (NT - 2) * b + c)
                            nc.vector.tensor_tensor(state[(c + 1) % 2][:], ps[0:DS, 7, 0:DI], sdec[:],
                                                    ALU.add).then_inc(m_S, 1)
                    if c == 1 and not first:
                        output(b - 1, 1 - u)
                    for part in parts.get(c, ()):
                        part()

            for c, parts in front(0, 0).items():
                for part in parts:
                    part()
            scanned(dve, scan)
            mean_square(B - 1)
            output(B - 1, 1)

            dve.wait_ge(e_w, 16 * len(expert_loads))
            nc.vector.tensor_copy(w1_h[:], w1_f[:])
            nc.vector.tensor_copy(rw_h[:], rw_f[:]).then_inc(e_v, 1)
            dve.wait_ge(e_v, 1)
            nc.vector.tensor_tensor(w1_l[:], w1_f[:], w1_h[:].bitcast(F32), ALU.subtract)
            nc.vector.tensor_tensor(rw_l[:], rw_f[:], rw_h[:].bitcast(F32), ALU.subtract).then_inc(e_wc, 1)

            def by_tile(t, n):
                return t.rearrange("p (t o) -> p t o", o=1).to_broadcast([P, NT, n])

            def scores(b, u):
                n = [0]
                io = iota[:].rearrange("p (o e) -> p o e", o=1).to_broadcast([P, NT, NE])

                def step(ins):
                    n[0] += 1
                    ins.then_inc(e_v, 1)
                    dve.wait_ge(e_v, EXPERT_STEPS * b + (1 + n[0]))

                def statistics():
                    for t in range(NT):
                        last = nc.vector.bn_stats(est[:, t, :], X[:, b, t * P:(t + 1) * P])
                    step(last)
                    dve.sem_inc(s_turn, 1)
                    for t in range(NT):
                        last = nc.vector.bn_aggr(emv[:, t, :], est[:, t, :])
                    step(last)
                    nc.vector.tensor_scalar(eve[:], emv[:, :, 1], LN_EPS, None, ALU.add).then_inc(e_ve, 1)

                def norm():
                    dve.wait_ge(e_rs, b + 1)
                    dve.wait_ge(e_acc0, b)
                    for t in range(NT):
                        last = nc.vector.tensor_scalar(un[:, t, :], X[:, b, t * P:(t + 1) * P], emv[:, t, 0:1],
                                                       ers[:, t:t + 1], ALU.subtract, ALU.mult)
                    last.then_inc(e_un, 1)

                def low():
                    dve.wait_ge(e_uh, b + 1)
                    nc.vector.tensor_tensor(two(ul[u][:]), lo_banks, two(uh[u][:].bitcast(F32)),
                                            ALU.subtract).then_inc(e_ul, 1)

                def largest():
                    dve.wait_ge(e_lg, b + 1)
                    step(nc.vector.tensor_copy(lg[:].rearrange("p t e -> p (t e)"), ps[:, 2, 0:NT * NE]))
                    dve.sem_inc(s_turn, 1)
                    for t in range(NT):
                        last = nc.vector.max(top[:, t, :], lg[:, t, :])
                    step(last)
                    nc.vector.tensor_tensor(tsh[:], top[:], top[:, :, 0:1].to_broadcast([P, NT, 8]),
                                            ALU.subtract).then_inc(e_top, 1)

                def places():
                    for t in range(NT):
                        last = nc.vector.max_index(tix[:, t, :], top[:, t, :], lg[:, t, :])
                    step(last)
                    step(nc.vector.tensor_copy(tif[:], tix[:, :, 0:2]))
                    nc.vector.tensor_tensor(oh1[:], io, tif[:, :, 0:1].to_broadcast([P, NT, NE]), ALU.is_equal)
                    step(nc.vector.tensor_tensor(oh2[:], io, tif[:, :, 1:2].to_broadcast([P, NT, NE]), ALU.is_equal))

                def softmax():
                    dve.wait_ge(e_ex, b + 1)
                    step(nc.vector.tensor_reduce(tsum[:], tex[:], AX_X, ALU.add))
                    step(nc.vector.reciprocal(trc[:], tsum[:]))
                    step(nc.vector.tensor_tensor(tp[:], tex[:, :, 0:2], by_tile(trc[:], 2), ALU.mult))
                    step(nc.vector.tensor_tensor(tw[:], tp[:, :, 0], tp[:, :, 1], ALU.add))
                    step(nc.vector.tensor_scalar(tw[:], tw[:], 1e-12, None, ALU.max))
                    step(nc.vector.reciprocal(tw[:], tw[:]))

                def weights():
                    step(nc.vector.tensor_tensor(tp[:], tp[:], by_tile(tw[:], 2), ALU.mult))
                    nc.vector.tensor_tensor(oh1[:], oh1[:], tp[:, :, 0:1].to_broadcast([P, NT, NE]), ALU.mult)
                    step(nc.vector.tensor_tensor(oh2[:], oh2[:], tp[:, :, 1:2].to_broadcast([P, NT, NE]), ALU.mult))
                    nc.vector.tensor_tensor(comb[u][:], oh1[:], oh2[:], ALU.add).then_inc(e_cb, 1)

                def turned():
                    dve.wait_ge(e_ct, b + 1)
                    nc.vector.tensor_copy(comb_t[:], ps[0:NT * NE, 3, 0:P]).then_inc(e_ctc, 1)

                def biases():
                    assert n[0] == EXPERT_STEPS, n
                    dve.wait_ge(e_cb, b + 1)
                    dve.wait_ge(e_bb, b + 1)
                    dve.wait_ge(e_acc0, b + 1)
                    nc.vector.tensor_tensor(two(acc[u][:].rearrange("p t c -> p (t c)")), lo_banks,
                                            two(acc[u][:].rearrange("p t c -> p (t c)")), ALU.add).then_inc(e_bba, 1)
                    dve.wait_ge(e_bba, b + 1)

                return statistics, norm, low, largest, places, softmax, weights, turned, biases

            def experts(b, u, more):
                parts = dict(zip((0, 2, 5, 8, 9, 11, 12, 13, 15), scores(b + 1, 1 - u))) if more else {}
                for k in range(2 * NE):
                    e, h = k // 2, k % 2
                    dve.wait_ge(e_y, 2 * NE * b + k + 1)
                    if k >= 2:
                        dve.wait_ge(e_a, 2 * NE * b + k - 1)
                    for t in range(4):
                        tt = 4 * h + t
                        last = nc.vector.scalar_tensor_tensor(acc[u][:, tt, :], ps[:, 6 + k % 2, t * P:(t + 1) * P],
                                                              comb[u][:, tt, e:e + 1], acc[u][:, tt, :],
                                                              ALU.mult, ALU.add)
                    last.then_inc(e_a, 1)
                    if k in parts:
                        parts[k]()

            for part in scores(0, 0):
                part()
            pictures(dve, experts)


_INS = ['x', 'wqk', 'bqk', 'wv', 'bv_rows', 'wo2', 'bo', 'ident', 'fold', 'group_mean',
        'wz', 'wx', 'norm_w', 'conv_w', 'conv_b', 'dt_bias', 'a_log', 'd_skip', 'wout', 'gnorm_w',
        'tri', 'ones', 'neg_mask', 'sel_rows', 'head_rows',
        'router', 'w1', 'b1', 'w2', 'b2_blocks', 'iota8']


def kernel(**inputs):
    import numpy as np
    import concourse.bacc as bacc
    from concourse.bass_utils import run_bass_kernel_spmd as run

    g = {k: np.asarray(v) for k, v in inputs.items()}
    a = {
        "x": g["x"].reshape(8, 128, 1024),
        "wqk": np.concatenate([g["L0_conv_Wq"].T, g["L0_conv_Wk"].T], 1),
        "bqk": np.concatenate([g["L0_conv_bq"], g["L0_conv_bk"]])[:, None],
        "wv": g["L0_conv_Wv"].T,
        "bv_rows": np.broadcast_to(g["L0_conv_bv"], (128, 64)),
        "wo2": np.concatenate([g["L0_conv_Wo"].T] * 2, 0),
        "bo": g["L0_conv_bo"][:, None],
        "ident": np.eye(128, dtype=np.float32),
        "fold": np.tile(np.eye(64, dtype=np.float32), (2, 1)),
        "group_mean": np.kron(np.eye(32), np.full((4, 4), 0.25)).astype(np.float32),
    }
    w_in, cwt, cbs = g["L1_attn_W_in"], g["L1_attn_conv_w"], g["L1_attn_conv_b"]
    xbc = w_in[256:576]
    order = np.concatenate([np.arange(256), np.tile(np.arange(256, 320), 2)])
    rows = np.arange(32)
    sel = (rows[:, None, None] % 8 == np.arange(8)[None, :, None]) & (rows[:, None, None] < 16)
    head = -1.0 * ((rows[:, None, None] % 8 == np.arange(8)[None, :, None]) & (rows[:, None, None] >= 16))
    full = np.ones((32, 8, 128), np.float32)
    b2_blocks = np.zeros((8, 8, 8, 128), np.float32)
    for t in range(8):
        b2_blocks[t, :, t] = g["L1_ffn_b2"]
    b2_blocks = b2_blocks.reshape(64, 1024)
    a |= {
        "wz": np.concatenate([w_in[:256], w_in[576:]]).T,
        "wx": xbc[order].T.reshape(128, 3, 128),
        "norm_w": g["L1_attn_norm_w"][:, None],
        "conv_w": cwt[order].reshape(3, 128, 4).transpose(1, 0, 2),
        "conv_b": cbs[order].reshape(3, 128).T,
        "dt_bias": np.broadcast_to(g["L1_attn_dt_bias"], (128, 8)),
        "a_log": np.broadcast_to(g["L1_attn_A_log"], (128, 8)),
        "d_skip": np.broadcast_to(g["L1_attn_Dp"], (128, 8)),
        "wout": g["L1_attn_W_out"].T.reshape(2, 128, 128).transpose(1, 0, 2),
        "gnorm_w": g["L1_attn_gnorm_w"].reshape(2, 128).T,
        "tri": np.triu(np.ones((128, 128), np.float32)),
        "ones": np.ones((128, 128), np.float32),
        "neg_mask": np.tile(np.tril(np.full((128, 128), -1e30, np.float32), -1), (1, 4)),
        "sel_rows": (sel * full).astype(np.float32).reshape(32, 1024),
        "head_rows": (head * full).astype(np.float32).reshape(32, 1024),
        "router": g["L1_ffn_router_w"].T,
        "w1": g["L1_ffn_w1"].transpose(1, 0, 2),
        "b1": g["L1_ffn_b1"].T,
        "w2": g["L1_ffn_w2"].transpose(1, 0, 2),
        "b2_blocks": b2_blocks,
        "iota8": np.broadcast_to(np.arange(8, dtype=np.float32), (128, 8)),
    }
    nc = bacc.Bacc("TRN2", target_bir_lowering=False, num_devices=1)
    arrays, args = {}, []
    for name in _INS:
        v = np.ascontiguousarray(a[name])
        arrays[f"in_{name}"] = v
        args.append(nc.dram_tensor(f"in_{name}", v.shape, mybir.dt.from_np(v.dtype), kind="ExternalInput").ap())
    out = nc.dram_tensor("out_0", (8, 128, 1024), F32, kind="ExternalOutput").ap()
    hybrid_kernel(nc, *args, out)
    r = run(nc, [arrays], core_ids=[0])
    return r.results[0]["out_0"].reshape(8, 128, 32, 32)
```

```python
from contextlib import ExitStack

import concourse.bass as bass
from concourse import mybir

ALU = mybir.AluOpType
ACT = mybir.ActivationFunctionType
F32 = mybir.dt.float32
F32R = mybir.dt.float32r
AX_X = mybir.AxisListType.X
AX_XY = mybir.AxisListType.XY

P = 128
BANK = 512


def hybrid_kernel(nc, x, wqk, bqk, wv, bv_rows, wo2, bo, ident, fold, group_mean,
                  wz, wx, norm_w, conv_w, conv_b, dt_bias, a_log, d_skip, wout, gnorm_w,
                  tri, ones, neg_mask, sel_rows, head_rows,
                  router, w1, b1, w2, b2_blocks, iota8, out):
    B, C, N = x.shape
    DK = bqk.shape[0] // 2
    DV = wv.shape[1]
    NT = N // P
    GN_EPS = 1e-5
    R = N // DV
    QSCALE = DK ** -0.5
    DI = wout.shape[1] * P
    NH = dt_bias.shape[1]
    HD = DI // NH
    DS = 32
    DCONV = conv_w.shape[2]
    LN_EPS = 1e-5
    DVE_FRONT_STEPS = 17
    F32_EPS = 2.0 ** -23
    GN2_EPS = 1e-5
    NE = w1.shape[1]
    EXPERT_STEPS = 15

    with ExitStack() as ctx:
        def sb(name, shape, dt=F32):
            return ctx.enter_context(nc.sbuf_tensor(name, shape, dt))

        def sem(name):
            return ctx.enter_context(nc.semaphore(name))

        ps = ctx.enter_context(nc.psum_tensor("ps", [P, 8, BANK], F32))

        w_qk = sb("w_qk", [P, 2 * DK])
        b_qk = sb("b_qk", [P, 1])
        w_v = sb("w_v", [P, DV])
        b_v = sb("b_v", [P, DV])
        w_o = sb("w_o", [P, P])
        b_o = sb("b_o", [P, 1])
        id_f = sb("id_f", [P, P])
        neg_half = sb("neg_half", [P, 2 * NT])
        neg_one = sb("neg_one", [P, NT])
        X = sb("X", [P, B, N])
        gst = sb("gst", [P, B, 2, 6])
        gmv = sb("gmv", [P, B, 2])
        gE = sb("gE", [P, B, 2])
        gm = sb("gm", [P, B, 2])
        gvar = sb("gvar", [P, B])
        grs = sb("grs", [P, B])
        w_zh = sb("w_zh", [P, DI + NH], F32R)
        w_zl = sb("w_zl", [P, DI + NH], F32R)
        w_xh = sb("w_xh", [P, 3, P], F32R)
        w_xl = sb("w_xl", [P, 3, P], F32R)
        n_w = sb("n_w", [P, 1])
        cw = sb("cw", [P, 3, DCONV])
        cb = sb("cb", [P, 3])
        dtb = sb("dtb", [P, NH])
        a_neg = sb("a_neg", [P, NH])
        dsk = sb("dsk", [P, NH])
        w_out = sb("w_out", [P, 2, P])
        g_w = sb("g_w", [P, 2])
        tri_f = sb("tri_f", [P, P])
        ones_f = sb("ones_f", [P, P])
        mask_r = sb("mask_r", [P, BANK], F32R)
        id_r = sb("id_r", [P, P], F32R)
        lhs_c = [sb(f"lhs_c{u}", [32, NT, P], F32R) for u in range(2)]
        rhs_c = [sb(f"rhs_c{u}", [32, NH, P], F32R) for u in range(2)]

        A = ExitStack()
        M = ExitStack()

        def asb(name, shape, dt=F32):
            return A.enter_context(nc.sbuf_tensor(name, shape, dt))

        def msb(name, shape, dt=F32):
            return M.enter_context(nc.sbuf_tensor(name, shape, dt))

        q_a, q_b, k_a, v_st = [asb("q_a0", [P, N], F32R)], [asb("q_b0", [P, N], F32R)], [asb("k_a0", [P, N], F32R)], \
            [asb("v_st0", [P, NT, 2 * DV], F32R)]
        xn = asb("xn", [P, N])
        v_f = asb("v_f", [P, NT, DV])
        q_a.append(asb("q_a1", [P, N], F32R))
        q_b.append(asb("q_b1", [P, N], F32R))
        k_a.append(asb("k_a1", [P, N], F32R))
        v_st.append(asb("v_st1", [P, NT, 2 * DV], F32R))
        probs = asb("probs", [P, 2, N])
        pt_h = asb("pt_h", [P, NT, N], F32R)
        pt_l = asb("pt_l", [P, NT, N], F32R)
        nmax = asb("nmax", [P, NT])
        rsum = [asb(f"rsum{u}", [P, NT]) for u in range(2)]
        rinv = asb("rinv", [P, NT])
        o_t = asb("o_t", [P, N])
        o_n = asb("o_n", [P, NT, DV])
        w_z = asb("w_z", [P, DI + NH])
        w_x = asb("w_x", [P, 3, P])
        mask_f = asb("mask_f", [P, BANK])
        cst_f = asb("cst_f", [32, 2, N])
        fold_f = asb("fold_f", [P, DV])
        gmean = asb("gmean", [P, P])
        A.close()
        xc = msb("xc", [P, N])
        xt = msb("xt", [P, NT, P])
        xh = msb("xh", [P, N], F32R)
        xl = msb("xl", [P, N], F32R)
        bst = msb("bst", [P, NT, 6])
        bmv = msb("bmv", [P, NT, 2])
        bve = msb("bve", [P, 2, NT])
        nmean = msb("nmean", [P, NT])
        rs = msb("rs", [P, 2, NT])
        rp1 = msb("rp1", [P, NT])
        rnb = msb("rnb", [P, 2, NT])
        res = [msb("res0", [P, NT, P])]
        cacc = msb("cacc", [P, 3, N])
        xst = msb("xst", [P, 2, N])
        b_t = msb("b_t", [DS, N])
        dtr = msb("dtr", [P, NT, NH])
        dta = msb("dta", [P, NT * NH])
        dte = msb("dte", [P, NT * NH])
        dtw = msb("dtw", [P, NT * NH])
        dtl = msb("dtl", [P, NT * NH])
        dtc = msb("dtc", [P, NT * NH])
        dti = msb("dti", [P, NT * NH])
        dec_a = msb("dec_a", [P, NT * NH])
        ein = msb("ein", [P, 3, NT * NH])
        xs = [msb(f"xs{u}", [P, NT, DI]) for u in range(2)]
        zs = [msb(f"zs{u}", [P, 2, N]) for u in range(2)]
        c_t = [msb(f"c_t{u}", [DS, N]) for u in range(2)]
        b_tok = [msb(f"b_tok{u}", [P, NT, DS]) for u in range(2)]
        g_sb = [msb(f"g_sb{u}", [P, NT, P]) for u in range(2)]
        res.append(msb("res1", [P, NT, P]))
        dts = [msb(f"dts{u}", [P, NT, NH]) for u in range(2)]
        wend = [msb(f"wend{u}", [P, NT, NH]) for u in range(2)]
        eo = [msb(f"eo{u}", [P, 3, NT * NH]) for u in range(2)]
        cth = msb("cth", [NT * NH, P], F32R)
        ctl = msb("ctl", [NT * NH, P], F32R)
        dcy = [msb(f"dcy{u}", [P, NH, P]) for u in range(2)]
        mix = dcy
        xdt = [msb(f"xdt{u}", [P, DI]) for u in range(2)]
        xw = [msb(f"xw{u}", [P, DI]) for u in range(2)]
        xsk = [msb(f"xsk{u}", [P, DI]) for u in range(2)]
        state = [msb(f"state{u}", [DS, DI]) for u in range(2)]
        sdec = msb("sdec", [DS, DI])
        yof = [msb(f"yof{u}", [P, DI]) for u in range(2)]
        yo2 = [msb(f"yo2_{u}", [P, DI]) for u in range(2)]
        sqt = msb("sqt", [P, 2, N])
        sve = msb("sve", [P, NT])
        srs = msb("srs", [P, NT])
        y_t = msb("y_t", [P, 2, N])
        M.close()
        E = ExitStack()

        def esb(name, shape, dt=F32):
            return E.enter_context(nc.sbuf_tensor(name, shape, dt))

        w1_f = esb("w1_f", [P, NE, P])
        w1_h = esb("w1_h", [P, NE, P], F32R)
        w1_l = esb("w1_l", [P, NE, P], F32R)
        w2_f = esb("w2_f", [P, NE, P])
        b1_f = esb("b1_f", [P, NE])
        b2_f = esb("b2_f", [NT * NE, N])
        rw_f = esb("rw_f", [P, NE])
        rw_h = esb("rw_h", [P, NE], F32R)
        rw_l = esb("rw_l", [P, NE], F32R)
        iota = esb("iota", [P, NE])
        est = esb("est", [P, NT, 6])
        emv = esb("emv", [P, NT, 2])
        eve = esb("eve", [P, NT])
        ers = esb("ers", [P, NT])
        enb = esb("enb", [P, NT])
        un = esb("un", [P, NT, P])
        acc, uh, ul = [esb("acc0", [P, NT, P])], [esb("uh0", [P, N], F32R)], [esb("ul0", [P, N], F32R)]
        lg = esb("lg", [P, NT, NE])
        top = esb("top", [P, NT, 8])
        tix = esb("tix", [P, NT, 8], mybir.dt.uint32)
        tif = esb("tif", [P, NT, 2])
        tsh = esb("tsh", [P, NT, 8])
        tex = esb("tex", [P, NT, 8])
        tsum = esb("tsum", [P, NT])
        trc = esb("trc", [P, NT])
        tp = esb("tp", [P, NT, 2])
        tw = esb("tw", [P, NT])
        oh1 = esb("oh1", [P, NT, NE])
        oh2 = esb("oh2", [P, NT, NE])
        comb = [esb(f"comb{u}", [P, NT, NE]) for u in range(2)]
        comb_t = esb("comb_t", [NT * NE, P])
        acc.append(esb("acc1", [P, NT, P]))
        uh.append(esb("uh1", [P, N], F32R))
        ul.append(esb("ul1", [P, N], F32R))
        hid = [esb(f"hid{u}", [P, BANK]) for u in range(2)]
        o_ch = [esb(f"o_ch{u}", [P, N]) for u in range(2)]
        E.close()

        attn_weights_loaded = sem("attn_weights_loaded")
        mamba_weights_loaded = sem("mamba_weights_loaded")
        consts_set = sem("consts_set")
        picture_loaded = sem("picture_loaded")
        moments_ready = sem("moments_ready")
        groups_ready = sem("groups_ready")
        var_ready = sem("var_ready")
        rstd_ready = sem("rstd_ready")
        dve_linked = sem("dve_linked")
        wait_carrier = sem("wait_carrier")
        xn_ready = sem("xn_ready")
        v_ready = sem("v_ready")
        v_high_ready = sem("v_high_ready")
        sum_inverse_ready = sem("sum_inverse_ready")
        bn_halves_ready = sem("bn_halves_ready")
        qk_product = sem("qk_product")
        v_product = sem("v_product")
        qk_high_ready = sem("qk_high_ready")
        qk_low_ready = sem("qk_low_ready")
        v_parts_ready = sem("v_parts_ready")
        scores_ready = sem("scores_ready")
        max_ready = sem("max_ready")
        probs_ready = sem("probs_ready")
        probs_turned = sem("probs_turned")
        probs_high_ready = sem("probs_high_ready")
        probs_low_ready = sem("probs_low_ready")
        pv_product = sem("pv_product")
        o_parts_copied = sem("o_parts_copied")
        o_folded = sem("o_folded")
        o_normed = sem("o_normed")
        wo_product = sem("wo_product")
        x_updated = sem("x_updated")
        out_stored = sem("out_stored")
        out_free = sem("out_free")
        e_weights_loaded = sem("e_weights_loaded")
        e_weights_split = sem("e_weights_split")
        e_var_ready = sem("e_var_ready")
        e_rstd_ready = sem("e_rstd_ready")
        e_shift_ready = sem("e_shift_ready")
        e_normed = sem("e_normed")
        e_sum_started = sem("e_sum_started")
        e_turned = sem("e_turned")
        e_high_ready = sem("e_high_ready")
        e_low_ready = sem("e_low_ready")
        e_logits = sem("e_logits")
        e_top_ready = sem("e_top_ready")
        e_top_exp_ready = sem("e_top_exp_ready")
        e_gates_ready = sem("e_gates_ready")
        e_gates_turned = sem("e_gates_turned")
        e_gates_copied = sem("e_gates_copied")
        e_bias_product = sem("e_bias_product")
        e_bias_added = sem("e_bias_added")
        e_hidden_product = sem("e_hidden_product")
        e_hidden_ready = sem("e_hidden_ready")
        e_second_product = sem("e_second_product")
        e_added = sem("e_added")
        e_sum_turned = sem("e_sum_turned")
        e_out_ready = sem("e_out_ready")
        e_dve_step = sem("e_dve_step")
        e_weights_high = sem("e_weights_high")
        m_x_copied = sem("m_x_copied")
        m_rows_written = sem("m_rows_written")
        m_tokens_turned = sem("m_tokens_turned")
        m_var_ready = sem("m_var_ready")
        m_scales_ready = sem("m_scales_ready")
        m_normed = sem("m_normed")
        m_residual_ready = sem("m_residual_ready")
        m_normed_turned = sem("m_normed_turned")
        m_xh_ready = sem("m_xh_ready")
        m_xl_ready = sem("m_xl_ready")
        m_z_product = sem("m_z_product")
        m_z_ready = sem("m_z_ready")
        m_group_product = sem("m_group_product")
        m_tap_ready = sem("m_tap_ready")
        m_conv_ready = sem("m_conv_ready")
        m_silu_ready = sem("m_silu_ready")
        m_dt_ready = sem("m_dt_ready")
        m_exponent_ready = sem("m_exponent_ready")
        m_cumulated = sem("m_cumulated")
        m_rows_ready = sem("m_rows_ready")
        m_x_turned = sem("m_x_turned")
        m_x_gathered = sem("m_x_gathered")
        m_inner_product = sem("m_inner_product")
        m_inner_ready = sem("m_inner_ready")
        m_rows_read = sem("m_rows_read")
        m_skip_ready = sem("m_skip_ready")
        m_decay_product = sem("m_decay_product")
        m_decay_ready = sem("m_decay_ready")
        m_mix_ready = sem("m_mix_ready")
        m_xdt_ready = sem("m_xdt_ready")
        m_xw_ready = sem("m_xw_ready")
        m_state_decayed = sem("m_state_decayed")
        m_state_product = sem("m_state_product")
        m_state_ready = sem("m_state_ready")
        m_y_product = sem("m_y_product")
        m_square_ready = sem("m_square_ready")
        m_out_product = sem("m_out_product")
        m_square_mean_ready = sem("m_square_mean_ready")
        m_rms_ready = sem("m_rms_ready")
        m_x_updated = sem("m_x_updated")
        m_dve_step = sem("m_dve_step")
        m_rstd_ready = sem("m_rstd_ready")
        m_carried_product = sem("m_carried_product")
        m_carried_ready = sem("m_carried_ready")
        m_carried_skip_ready = sem("m_carried_skip_ready")
        m_gated_ready = sem("m_gated_ready")
        m_squares_summed = sem("m_squares_summed")
        m_dt_copied = sem("m_dt_copied")
        a_exp_ready = sem("a_exp_ready")
        m_softplus_step = sem("m_softplus_step")
        m_factors_ready = sem("m_factors_ready")
        m_wend_ready = sem("m_wend_ready")
        attention_done = sem("attention_done")

        stat_groups = [(0, 1), (1, 2), (2, B)]
        S = [ps[:, 0:2, :], ps[:, 2:4, :]]
        T = ps[:, 4:6, :]
        O = ps[:, 6:8, :]
        lo_banks, hi_banks = ps[:, 0:2, :], ps[:, 2:4, :]

        cum_dram = nc.dram_tensor("cum_dram", (2, 2, NT * NH, P), F32, kind="Internal").ap()
        block = ctx.enter_context(nc.Block())

        loads = [(w_qk, wqk), (b_qk, bqk), (w_v, wv), (b_v, bv_rows), (w_o, wo2), (b_o, bo),
                 (id_f, ident), (fold_f, fold), (gmean, group_mean), (w_z, wz), (w_x, wx), (n_w, norm_w),
                 (cw, conv_w), (cb, conv_b), (dtb, dt_bias), (a_neg, a_log), (dsk, d_skip), (w_out, wout),
                 (g_w, gnorm_w), (tri_f, tri), (ones_f, ones), (mask_f, neg_mask)]

        expert_loads = [(w1_f, w1), (w2_f, w2), (b1_f, b1), (b2_f, b2_blocks), (rw_f, router), (iota, iota8)]

        def scanned(engine, body):
            body(0, 0, True, False)
            with engine.Fori(0, B // 2 - 1) as i:
                for odd in range(2):
                    body(2 * i + (1 + odd), 1 - odd, False, False)
            body(B - 1, 1, False, True)

        def by_picture(b, banks):
            return O if isinstance(b, int) and b == 0 else banks

        def attended(engine, body):
            body(0, 0, True, False)
            with engine.Fori(0, B // 2 - 1) as i:
                for odd in range(2):
                    body(2 * i + (1 + odd), 1 - odd, False, False)
            body(B - 1, 1, False, True)

        @block.sync
        def _(sp):
            for b in range(B):
                sp.dma_start(X[:, b, :], x[b]).then_inc(picture_loaded, 16)
                if b == 0:
                    for dst, src in loads[:9]:
                        sp.dma_start(dst[:], src).then_inc(attn_weights_loaded, 16)
                sp.wait_ge(picture_loaded, 16 * (b + 1))
            for dst, src in loads[9:]:
                sp.dma_start(dst[:], src).then_inc(mamba_weights_loaded, 16)
            sp.dma_start(cst_f[:, 0, :], sel_rows).then_inc(mamba_weights_loaded, 16)
            sp.dma_start(cst_f[:, 1, :], head_rows).then_inc(mamba_weights_loaded, 16)
            def decay_rows(b, u, first, last):
                sp.wait_ge(m_rows_ready, b + 1)
                sp.sem_inc(wait_carrier, 1)
                if not first:
                    sp.wait_ge(m_decay_product, NT * (b - 1) + 1)
                    sp.sem_inc(wait_carrier, 1)
                for part, src in ((0, cth), (1, ctl)):
                    sp.dma_start(cum_dram[u, part], src[:].bitcast(F32)).then_inc(m_rows_written, 16)
                sp.wait_ge(m_rows_written, 32 * (b + 1))
                for part in range(2):
                    rows = cum_dram[u, part].rearrange("(c h) t -> c h t", h=NH)
                    sp.dma_start(rhs_c[u][NT * part:NT * part + NT].bitcast(F32), rows).then_inc(m_rows_read, 16)
                    rows = cum_dram[u, part].rearrange("(c h) t -> h c t", h=NH)
                    r0 = 2 * NT + NH * part
                    sp.dma_start(lhs_c[u][r0:r0 + NH].bitcast(F32), rows).then_inc(m_rows_read, 16)
                sp.wait_ge(m_rows_read, 64 * (b + 1))
                sp.sem_inc(wait_carrier, 1)

            scanned(sp, decay_rows)
            sp.wait_ge(m_inner_ready, B)
            sp.wait_ge(m_x_updated, B - 1)
            sp.sem_inc(out_free, 2)
            for dst, src in expert_loads:
                sp.dma_start(dst[:], src).then_inc(e_weights_loaded, 16)
            with sp.Fori(0, B // 2) as i:
                for u in range(2):
                    b = 2 * i + u
                    sp.wait_ge(e_out_ready, b + 1)
                    sp.dma_start(out[b], o_ch[u][:]).then_inc(out_stored, 16)
                    sp.wait_ge(out_stored, 16 * (b + 1))
                    sp.sem_inc(out_free, 1)

        @block.gpsimd
        def _(pool):
            nc.gpsimd.memset(neg_one[:], -1.0)
            nc.gpsimd.memset(neg_half[:], -0.5).then_inc(consts_set, 1)
            pool.wait_ge(consts_set, 1)
            for n, (b0, b1) in enumerate(stat_groups):
                pool.wait_ge(var_ready, n + 1)
                nc.gpsimd.tensor_tensor(grs[:, b0:b1], gvar[:, b0:b1], neg_half[:, b0:b1],
                                        ALU.pow).then_inc(rstd_ready, 1)
            def heads(t):
                return t.rearrange("p (h d) -> p h d", h=NH)

            def per_head(t):
                return t.rearrange("p (h o) -> p h o", o=1).to_broadcast([t.shape[0], NH, HD])

            def norms(b, u):
                pool.wait_ge(m_var_ready, b + 1)
                nc.gpsimd.tensor_tensor(rs[:], bve[:], neg_half[:, 0:2 * NT].rearrange("p (n t) -> p n t", n=2),
                                        ALU.pow).then_inc(m_rstd_ready, 1)
                pool.wait_ge(m_rstd_ready, b + 1)
                nc.gpsimd.tensor_tensor(rp1[:], rs[:, 0, :], ones_f[:, 0:NT], ALU.add)
                nc.gpsimd.tensor_tensor(rnb[:], rs[:], nmean[:].rearrange("p (o t) -> p o t", o=1).to_broadcast([P, 2, NT]),
                                        ALU.mult).then_inc(m_scales_ready, 1)

            def operands(b, u, c, first):
                if c >= 2 or not first:
                    pool.wait_ge(m_y_product, NT * b + c - 1)
                    pool.wait_ge(m_state_product, (NT - 1) * b + max(c - 1, 0))
                nc.gpsimd.tensor_tensor(heads(xw[c % 2][:]), heads(xs[u][:, c, :]), per_head(wend[u][:, c, :]),
                                        ALU.mult).then_inc(m_xw_ready, 1)
                nc.gpsimd.tensor_tensor(heads(xdt[c % 2][:]), heads(xs[u][:, c, :]), per_head(dts[u][:, c, :]),
                                        ALU.mult).then_inc(m_xdt_ready, 1)
                nc.gpsimd.tensor_tensor(heads(xsk[c % 2][:]), heads(xs[u][:, c, :]), per_head(dsk[:, :]),
                                        ALU.mult).then_inc(m_skip_ready, 1)

            def with_skip(b, c):
                pool.wait_ge(m_skip_ready, NT * b + c + 1)
                pool.wait_ge(m_carried_ready, (NT - 1) * b + c)
                nc.gpsimd.tensor_tensor(yo2[c % 2][:], yof[c % 2][:], xsk[c % 2][:],
                                        ALU.add).then_inc(m_carried_skip_ready, 1)

            def root(b):
                pool.wait_ge(m_square_mean_ready, b + 1)
                nc.gpsimd.tensor_tensor(srs[:], sve[:], neg_half[:, 0:NT], ALU.pow).then_inc(m_rms_ready, 1)

            root_at, norms_at = 0, 0.5

            def beside(b, u, first, last, slot):
                if slot == root_at and not first:
                    root(b - 1)
                if slot == norms_at and not last:
                    norms(b + 1, 1 - u)

            def scan(b, u, first, last):
                for c in range(NT):
                    if c == 0:
                        pool.wait_ge(m_wend_ready, b + 1)
                        pool.wait_ge(m_x_gathered, 3 * b + 2)
                        operands(b, u, 0, first)
                    if c < NT - 2:
                        pool.wait_ge(m_state_ready, (NT - 1) * b + c + 1)
                        nc.gpsimd.tensor_tensor(heads(sdec[:]), heads(state[(c + 1) % 2][:]),
                                                per_head(eo[u][0:DS, 2, NH * (c + 1):NH * (c + 2)]),
                                                ALU.mult).then_inc(m_state_decayed, 1)
                    beside(b, u, first, last, c - 0.25)
                    if c >= 1:
                        with_skip(b, c)
                    beside(b, u, first, last, c)
                    if c + 1 < NT:
                        operands(b, u, c + 1, first)
                    beside(b, u, first, last, c + 0.5)
                    if last and c == 1:
                        norm(0, 0)
                    if last and c == 2:
                        start_sum(0, 0)

            def norm(b, u):
                pool.wait_ge(e_var_ready, b + 1)
                nc.gpsimd.tensor_tensor(ers[:], eve[:], neg_half[:, 0:NT], ALU.pow).then_inc(e_rstd_ready, 1)
                pool.wait_ge(e_rstd_ready, b + 1)
                nc.gpsimd.tensor_tensor(enb[:], ers[:], emv[:, :, 0], ALU.mult).then_inc(e_shift_ready, 1)
                pool.wait_ge(e_shift_ready, 2 * b + 1)
                nc.gpsimd.tensor_tensor(enb[:], enb[:], neg_one[:], ALU.mult).then_inc(e_shift_ready, 1)

            def start_sum(b, u):
                pool.wait_ge(e_normed, b + 1)
                if not isinstance(b, int) or b > 1:
                    pool.wait_ge(e_sum_turned, b - 1)
                nc.gpsimd.tensor_tensor(acc[u][:].rearrange("p t c -> p (t c)"), X[:, b, :],
                                        un[:].rearrange("p t c -> p (t c)"), ALU.add).then_inc(e_sum_started, 1)

            def experts(b, u, first, last):
                if not last:
                    norm(b + 1, 1 - u)
                    start_sum(b + 1, 1 - u)

            norms(0, 0)
            pool.wait_ge(x_updated, 2 * B)
            scanned(pool, scan)
            root(B - 1)

            scanned(pool, experts)

        @block.tensor
        def _(pe):
            def group_means(n):
                b0, b1 = stat_groups[n]
                pe.wait_ge(moments_ready, n + 1)
                nc.tensor.matmul(ps[:, 7, 2 * b0:2 * b1], gmean[:], gE[:, b0:b1, :].rearrange("p b s -> p (b s)"),
                                 start=True, stop=True).then_inc(groups_ready, 1)

            def scores(b, u, j, start=False):
                if not (start and j < 2):
                    pe.wait_ge(probs_ready, NT * b + j - 1)
                for h in range(2):
                    o = S[j % 2][:, h, :]
                    kk = k_a[u][:, h * BANK:(h + 1) * BANK]
                    nc.tensor.matmul(o, q_a[u][:, j * P:(j + 1) * P], kk, start=True, stop=False)
                    last = nc.tensor.matmul(o, q_b[u][:, j * P:(j + 1) * P], kk, start=False, stop=True)
                last.then_inc(scores_ready, 1)

            def projections(b):
                pe.wait_ge(xn_ready, b + 1)
                if not isinstance(b, int) or b > 1:
                    pe.wait_ge(x_updated, 2 * (b - 1))
                for h in range(2):
                    last = nc.tensor.matmul(O[:, h, :], w_qk[:], xn[:, h * BANK:(h + 1) * BANK], start=True, stop=True)
                last.then_inc(qk_product, 1)

            def values(b):
                pe.wait_ge(qk_low_ready, 3 * b + 3)
                for k in range(NT):
                    last = nc.tensor.matmul(O[:, 0, k * DV:(k + 1) * DV], xn[:, k * P:(k + 1) * P], w_v[:],
                                            start=True, stop=True)
                last.then_inc(v_product, 1)

            def turn(b, j, start):
                pe.wait_ge(probs_ready, NT * b + j + 1)
                for h in range(2):
                    if not (start and j == 0):
                        pe.wait_ge(probs_low_ready, 2 * (NT * b + j - 1) + h + 1)
                    for k in range(4):
                        last = nc.tensor.transpose(T[:, h, k * P:(k + 1) * P],
                                                   probs[:, j % 2, (4 * h + k) * P:(4 * h + k + 1) * P], id_f[:])
                    last.then_inc(probs_turned, 1)

            def pv(b, u, h, quarter):
                if quarter == 0:
                    pe.wait_ge(probs_low_ready, 2 * NT * b + NT * (h + 1))
                    if h == 0 and not (isinstance(b, int) and b == B - 1):
                        pe.wait_ge(v_ready, b + 2)
                for k in range(2 * quarter, 2 * quarter + 2):
                    for part in (pt_h, pt_l):
                        last = nc.tensor.matmul(O[:, h, :], v_st[u][:, k, :], part[:, k, h * BANK:(h + 1) * BANK],
                                                start=(k == 0 and part is pt_h), stop=(k == NT - 1 and part is pt_l))
                if quarter == 3:
                    last.then_inc(pv_product, 1)

            def fold_parts(b):
                pe.wait_ge(o_parts_copied, b + 1)
                for j in range(NT):
                    last = nc.tensor.matmul(O[:, 0, j * DV:(j + 1) * DV], o_t[:, j * P:(j + 1) * P], fold_f[:],
                                            start=True, stop=True)
                last.then_inc(o_folded, 1)

            def out_projection(b):
                pe.wait_ge(o_normed, b + 1)
                for e in range(2):
                    r = slice(64 * e, 64 * e + 64)
                    last = nc.tensor.matmul(O[:, 1 - e, :], w_o[r, :], o_n[r].rearrange("p j v -> p (j v)"),
                                            start=True, stop=True)
                last.then_inc(wo_product, 1)

            late_pv = [0.5, 0.5, 1, 1]
            fold_at, out_at = 1.5, 2.5
            projections_at, values_at = 3.5, 5.5
            early_pv = [6, 6.5, 7, 7.5]

            def beside(b, u, first, last, slot):
                if not first:
                    for quarter in range(4):
                        if late_pv[quarter] == slot:
                            pv(b - 1, 1 - u, 1, quarter)
                    if slot == fold_at:
                        fold_parts(b - 1)
                    if slot == out_at:
                        out_projection(b - 1)
                if not last:
                    if slot == projections_at:
                        projections(b + 1)
                    if slot == values_at:
                        values(b + 1)
                    for quarter in range(4):
                        if early_pv[quarter] == slot:
                            pv(b, u, 0, quarter)

            def attend(b, u, first, last):
                for j in range(NT):
                    if j + 2 < NT:
                        scores(b, u, j + 2)
                    elif not last:
                        scores(b + 1, 1 - u, j + 2 - NT)
                    beside(b, u, first, last, j)
                    turn(b, j, start=first)
                    beside(b, u, first, last, j + 0.5)
                    if j == 1 and first:
                        group_means(1)
                    if j == 3 and last:
                        pe.wait_ge(x_updated, 2 * b)
                        turn_in(0)
                    if j == 6 and last:
                        turn_normed(0, 0)
                    if j == 7 and first:
                        group_means(2)
                        pe.wait_ge(var_ready, 3)


            def cols(banks, t, w):
                q = BANK // w
                return banks[:, t // q, (t % q) * w:(t % q + 1) * w]

            def split(o, lhs, rhs):
                nc.tensor.matmul(o, lhs[0], rhs[0], start=True, stop=False)
                nc.tensor.matmul(o, lhs[0], rhs[1], start=False, stop=False)
                return nc.tensor.matmul(o, lhs[1], rhs[0], start=False, stop=True)

            def group(b, u, g, h):
                if h == 0:
                    if g == 0:
                        pe.wait_ge(m_xl_ready, b + 1)
                    elif g == 1:
                        pe.wait_ge(m_dt_copied, b + 1)
                    else:
                        pe.wait_ge(m_conv_ready, 3 * b + 1)
                r = slice(h * BANK, (h + 1) * BANK)
                last = split((hi_banks, lo_banks, hi_banks)[g][:, h, :], (w_xh[:, g, :], w_xl[:, g, :]),
                             (xh[:, r], xl[:, r]))
                if h == 1:
                    last.then_inc(m_group_product, 1)

            def turn_in(b):
                pe.wait_ge(m_x_copied, b + 1)
                if not isinstance(b, int) or b > 0:
                    pe.wait_ge(m_x_gathered, 3 * b)
                for t in range(NT):
                    last = nc.tensor.transpose(cols(by_picture(b, lo_banks), t, P), xc[:, t * P:(t + 1) * P], id_f[:])
                last.then_inc(m_tokens_turned, 1)

            def turn_normed(b, u):
                pe.wait_ge(m_normed, b + 1)
                if isinstance(b, int) and b == 0:
                    pe.wait_ge(m_residual_ready, 1)
                else:
                    pe.wait_ge(m_inner_ready, b)
                if not isinstance(b, int) or b > 1:
                    pe.wait_ge(m_x_updated, b - 1)
                for t in range(NT):
                    last = nc.tensor.transpose(cols(by_picture(b, hi_banks), t, P), xt[:, t, :], id_f[:])
                last.then_inc(m_normed_turned, 1)

            def steps(b, u):
                pe.wait_ge(m_residual_ready, b + 1)
                for t in range(NT):
                    r = slice(t * P, (t + 1) * P)
                    last = split(lo_banks[:, 0, t * NH:(t + 1) * NH], (xh[:, r], xl[:, r]),
                                 (w_zh[:, DI:DI + NH], w_zl[:, DI:DI + NH]))
                last.then_inc(m_z_product, 1)

            def gates(b, u, g, h):
                if h == 0:
                    if g == 0:
                        pe.wait_ge(m_rows_ready, b + 1)
                        pe.wait_ge(m_exponent_ready, 2 * b + 2)
                    else:
                        pe.wait_ge(m_conv_ready, 3 * b + 3)
                r = slice(h * BANK, (h + 1) * BANK)
                c = slice(g * P, (g + 1) * P)
                last = split((lo_banks, hi_banks)[g][:, h, :], (w_zh[:, c], w_zl[:, c]), (xh[:, r], xl[:, r]))
                if h == 1:
                    last.then_inc(m_z_product, 1)

            def turn_x(b, u, g):
                pe.wait_ge(m_silu_ready, 3 * b + g + 1)
                pe.wait_ge(m_z_ready, 2 * b + g + 1)
                for t in range(NT):
                    last = nc.tensor.transpose(cols((lo_banks, hi_banks)[g], t, P), xst[:, g, t * P:(t + 1) * P], id_f[:])
                last.then_inc(m_x_turned, 1)

            def cumulate(b, u):
                pe.wait_ge(m_dt_ready, b + 1)
                pe.wait_ge(m_conv_ready, 3 * b + 2)
                nc.tensor.matmul(lo_banks[:, 0, 0:64], tri_f[:], dec_a[:], start=True, stop=True)
                nc.tensor.matmul(lo_banks[:, 0, 64:128], ones_f[:], dec_a[:], start=True, stop=True)
                nc.tensor.matmul(lo_banks[0:64, 1, 0:P], dec_a[:], tri_f[:], start=True,
                                 stop=True).then_inc(m_cumulated, 1)

            def turn_b(b, u):
                pe.wait_ge(m_silu_ready, 3 * b + 3)
                pe.wait_ge(m_x_gathered, 3 * b + 1)
                pe.sem_inc(wait_carrier, 1)
                for t in range(NT):
                    last = nc.tensor.transpose(lo_banks[:, 0, t * DS:(t + 1) * DS], b_t[:, t * P:(t + 1) * P],
                                               id_f[0:DS, 0:DS])
                last.then_inc(m_x_turned, 1)

            def inner_products(b, u):
                pe.wait_ge(m_x_gathered, 3 * b + 2)
                for t in range(NT):
                    r = slice(t * P, (t + 1) * P)
                    last = nc.tensor.matmul(cols(hi_banks, t, P), b_t[:, r], c_t[u][:, r], start=True, stop=True)
                last.then_inc(m_inner_product, 1)

            def decay(b, u, c, first=False):
                if c == 0:
                    pe.wait_ge(m_rows_read, 64 * (b + 1))
                if not (first and c == 0):
                    pe.wait_ge(m_decay_ready, NT * b + c)
                for h in range(2):
                    o = ps[:, 4 + h, :]
                    nc.tensor.matmul(o, id_r[:], mask_r[:], start=True, stop=False)
                    done = nc.tensor.matmul(o, lhs_c[u][:, c, :],
                                            rhs_c[u][:, 4 * h:4 * h + 4, :].rearrange("p h t -> p (h t)"),
                                            start=False, stop=True)
                done.then_inc(m_decay_product, 1)

            def state_product(b, u, c, first):
                pe.wait_ge(m_xw_ready, NT * b + c + 1)
                if c == 0:
                    pe.wait_ge(m_x_gathered, 3 * b + 3)
                    if not first:
                        pe.wait_ge(m_carried_ready, (NT - 1) * b)
                else:
                    pe.wait_ge(m_state_ready, (NT - 1) * b + c)
                    if c >= 2:
                        pe.wait_ge(m_carried_ready, (NT - 1) * b + c - 1)
                nc.tensor.matmul(ps[0:DS, 7, 0:DI], b_tok[u][:, c, :], xw[c % 2][:], start=True,
                                 stop=True).then_inc(m_state_product, 1)

            def sum_of_squares(b, c):
                pe.wait_ge(m_square_ready, NT * b + c + 1)
                for g in range(2):
                    last = nc.tensor.matmul(ps[:, 6, DI + c:DI + c + 1], sqt[:, g, c * P:(c + 1) * P], ones_f[:, 0:1],
                                            start=(g == 0), stop=(g == 1))
                if c == NT - 1:
                    last.then_inc(m_squares_summed, 1)

            def out_product(b):
                pe.wait_ge(m_gated_ready, NT * b + NT)
                if not isinstance(b, int) or b < B - 1:
                    pe.wait_ge(m_inner_ready, b + 2)
                for c in range(NT):
                    for g in range(2):
                        last = nc.tensor.matmul(cols(hi_banks, c, P), y_t[:, g, c * P:(c + 1) * P], w_out[:, g, :],
                                                start=(g == 0), stop=(g == 1))
                last.then_inc(m_out_product, 1)

            def scan(b, u, first, last):
                for c in range(NT):
                    if c == 0:
                        decay(b, u, 0, first)
                        if not first:
                            pe.wait_ge(m_gated_ready, NT * b)
                            sum_of_squares(b - 1, NT - 2)
                            sum_of_squares(b - 1, NT - 1)
                            out_product(b - 1)
                        if not last:
                            turn_in(b + 1)
                    if c < NT - 1:
                        state_product(b, u, c, first)
                    if c >= 1:
                        pe.wait_ge(m_state_ready, (NT - 1) * b + c)
                        if c == NT - 1:
                            pe.wait_ge(m_carried_ready, (NT - 1) * b + c - 1)
                        nc.tensor.matmul(ps[:, 7, DI:2 * DI], c_t[u][:, c * P:(c + 1) * P], state[c % 2][:],
                                         start=True, stop=True).then_inc(m_carried_product, 1)
                    if not last:
                        pieces(b + 1, 1 - u, c - 0.25)
                    if c + 1 < NT:
                        decay(b, u, c + 1)
                    if not last:
                        pieces(b + 1, 1 - u, c)
                    if c >= 1 or not first:
                        pe.wait_ge(m_gated_ready, NT * b + c)
                    if c == 0 and not first:
                        pe.wait_ge(m_square_mean_ready, b)
                    if c >= 2:
                        sum_of_squares(b, c - 2)
                    pe.wait_ge(m_mix_ready, NT * b + c + 1)
                    pe.wait_ge(m_xdt_ready, NT * b + c + 1)
                    for g in range(2):
                        for q in range(4):
                            h = 4 * g + q
                            nc.tensor.matmul(ps[q * HD:(q + 1) * HD, 6, g * P:(g + 1) * P],
                                             xdt[c % 2][:, h * HD:(h + 1) * HD], mix[c % 2][:, h, :],
                                             start=True, stop=False, tile_position=(0, q * HD))
                        if g == 0 and not last:
                            pieces(b + 1, 1 - u, c + 0.25)
                        if c == 0:
                            pe.wait_ge(m_skip_ready, NT * b + 1)
                        else:
                            pe.wait_ge(m_carried_skip_ready, (NT - 1) * b + c)
                        done = nc.tensor.matmul(ps[:, 6, g * P:(g + 1) * P],
                                                (xsk[0] if c == 0 else yo2[c % 2])[:, g * P:(g + 1) * P], id_f[:],
                                                start=False, stop=True)
                    done.then_inc(m_y_product, 1)
                    if not last:
                        pieces(b + 1, 1 - u, c + 0.5)
                    elif c == 3:
                        pe.wait_ge(m_x_gathered, 3 * B)
                        turn_tokens(0)
                    elif c == 4:
                        pe.wait_ge(e_weights_split, 1)
                        pe.wait_ge(m_x_updated, B - 1)
                        logits(0, 0)
                    elif c == 6:
                        turn_weights(0, 0)
                    elif c == 7:
                        second_biases(0)

            pe_parts = [(turn_normed, (), 1.5), (group, (0, 0), 3), (group, (0, 1), 3), (steps, (), 3),
                        (group, (1, 0), 3.5), (group, (1, 1), 3.5), (group, (2, 0), 4.5),
                        (group, (2, 1), 4.5), (cumulate, (), 5), (gates, (0, 0), 6), (gates, (0, 1), 6),
                        (gates, (1, 0), 6), (gates, (1, 1), 6), (turn_x, (0,), 6), (turn_x, (1,), 6),
                        (turn_b, (), 6.75), (inner_products, (), 7.5)]

            def pieces(b, u, slot):
                for part, of, at in pe_parts:
                    if at == slot:
                        part(b, u, *of)


            Y_BANKS = [(3, 6, 7)[n % 3] for n in range(2 * NE - 1)] + [6]

            def expert(b, u, n):
                e, h = n // 2, n % 2
                if n >= 2 or not isinstance(b, int) or b > 0:
                    pe.wait_ge(e_hidden_ready, 2 * NE * b + n - 1)
                pe.wait_ge(e_low_ready, b + 1)
                r = slice(h * BANK, (h + 1) * BANK)
                split(ps[:, 4 + n % 2, :], (w1_h[:, e, :], w1_l[:, e, :]),
                      (uh[u][:, r], ul[u][:, r])).then_inc(e_hidden_product, 1)

            def second(b, n, first):
                e, h = n // 2, n % 2
                pe.wait_ge(e_hidden_ready, 2 * NE * b + n + 1)
                before = 3 if n < 2 * NE - 1 else 2
                if n >= 3:
                    pe.wait_ge(e_added, 2 * NE * b + n - before + 1)
                elif not first:
                    pe.wait_ge(e_added, 2 * NE * b - (3, 0, 1)[n])
                for t in range(4):
                    last = nc.tensor.matmul(ps[:, Y_BANKS[n], t * P:(t + 1) * P], hid[n % 2][:, t * P:(t + 1) * P],
                                            w2_f[:, e, :], start=True, stop=True)
                last.then_inc(e_second_product, 1)

            def turn_tokens(b):
                pe.wait_ge(e_normed, b + 1)
                if not isinstance(b, int) or b > 1:
                    pe.wait_ge(e_out_ready, b - 1)
                elif b == 1:
                    pe.wait_ge(e_bias_added, 1)
                for t in range(NT):
                    last = nc.tensor.transpose(cols(lo_banks, t, P), un[:, t, :], id_f[:])
                last.then_inc(e_turned, 1)

            def logits(b, u):
                pe.wait_ge(e_low_ready, b + 1)
                if not isinstance(b, int) or b > 0:
                    pe.wait_ge(e_gates_copied, b)
                for t in range(NT):
                    r = slice(t * P, (t + 1) * P)
                    last = split(ps[:, 2, t * NE:(t + 1) * NE], (uh[u][:, r], ul[u][:, r]), (rw_h[:], rw_l[:]))
                last.then_inc(e_logits, 1)

            def turn_weights(b, u):
                pe.wait_ge(e_gates_ready, b + 1)
                pe.sem_inc(wait_carrier, 1)
                nc.tensor.transpose(ps[0:NT * NE, 2, P:2 * P], comb[u][:].rearrange("p t e -> p (t e)"),
                                    id_f[:]).then_inc(e_gates_turned, 1)

            def second_biases(b):
                pe.wait_ge(e_gates_copied, b + 1)
                for h in range(2):
                    last = nc.tensor.matmul(lo_banks[:, h, :], comb_t[:], b2_f[:, h * BANK:(h + 1) * BANK],
                                            start=True, stop=True)
                last.then_inc(e_bias_product, 1)

            def turn_out(b, u):
                pe.wait_ge(e_added, 2 * NE * b + 2 * NE)
                if not isinstance(b, int) or b < B - 1:
                    pe.wait_ge(e_bias_added, b + 2)
                for t in range(NT):
                    done = nc.tensor.transpose(cols(lo_banks, t, P), acc[u][:, t, :], id_f[:])
                done.then_inc(e_sum_turned, 1)

            def experts(b, u, first, last):
                for n in range(2 * NE):
                    second(b, n, first)
                    if n + 2 < 2 * NE:
                        expert(b, u, n + 2)
                    elif not last:
                        expert(b + 1, 1 - u, n + 2 - 2 * NE)
                    if n == 1 and not first:
                        turn_out(b - 1, 1 - u)
                    if not last:
                        if n == 5:
                            turn_tokens(b + 1)
                        if n == 7:
                            logits(b + 1, 1 - u)
                        if n == 12:
                            turn_weights(b + 1, 1 - u)
                        if n == 13:
                            second_biases(b + 1)

            pe.wait_ge(attn_weights_loaded, 16 * 9)
            group_means(0)
            projections(0)
            values(0)
            pe.wait_ge(v_ready, 1)
            scores(0, 0, 0, start=True)
            scores(0, 0, 1, start=True)
            attended(pe, attend)
            pe.wait_ge(m_xl_ready, 1)
            for h in range(2):
                for quarter in range(4):
                    pv(B - 1, 1, h, quarter)
            for h in range(2):
                group(0, 0, 0, h)
            fold_parts(B - 1)
            steps(0, 0)
            out_projection(B - 1)
            for part, of, _ in pe_parts[4:]:
                part(0, 0, *of)
            pe.wait_ge(attention_done, 1)
            scanned(pe, scan)
            pe.wait_ge(m_gated_ready, NT * B)
            sum_of_squares(B - 1, NT - 2)
            sum_of_squares(B - 1, NT - 1)
            pe.wait_ge(e_gates_copied, 1)
            out_product(B - 1)
            expert(0, 0, 0)
            expert(0, 0, 1)
            scanned(pe, experts)
            turn_out(B - 1, 1)

        @block.scalar
        def _(act):
            def q_and_k(b, u):
                act.wait_ge(qk_product, b + 1)
                tq = O[0:DK].rearrange("p a (c r) -> p (a c) r", r=R)
                for dst, r0 in ((q_a[u], 0), (q_b[u], DK)):
                    nc.scalar.activation(dst[r0:r0 + DK].rearrange("p (r c) -> p c r", r=R), tq,
                                         ACT.Identity, bias=b_qk[0:DK, 0:1]).then_inc(qk_high_ready, 1)
                nc.scalar.activation(k_a[u][0:DK].rearrange("p (a n) -> p a n", a=2), O[DK:2 * DK],
                                     ACT.Identity, bias=b_qk[DK:2 * DK, 0:1]).then_inc(qk_high_ready, 1)

            def exponentials(b, u, j, start=False):
                act.wait_ge(max_ready, NT * b + j + 1)
                if not (start and j < 2):
                    act.wait_ge(probs_turned, 2 * (NT * b + j - 1))
                nc.scalar.activation(probs[:, j % 2, :].rearrange("p (a n) -> p a n", a=2), S[j % 2], ACT.Exp,
                                     bias=nmax[:, j:j + 1], accum_out=rsum[u][:, j:j + 1]).then_inc(probs_ready, 1)

            def high_parts(b, j, h):
                act.wait_ge(probs_turned, 2 * (NT * b + j) + h + 1)
                nc.scalar.activation(pt_h[:, 4 * h:4 * h + 4, j * P:(j + 1) * P],
                                     T[:, h, :].rearrange("p (k n) -> p k n",
                                                          n=P), ACT.Copy).then_inc(probs_high_ready, 1)

            o_copy_at, q_and_k_at = 1, 4.5

            def copy_o(b):
                act.wait_ge(pv_product, 2 * b + 2)
                nc.scalar.activation(o_t[:].rearrange("p (a n) -> p a n", a=2), O, ACT.Copy).then_inc(o_parts_copied, 1)

            def beside(b, u, first, last, slot):
                if slot == o_copy_at and not first:
                    copy_o(b - 1)
                if slot == q_and_k_at and not last:
                    q_and_k(b + 1, 1 - u)

            def attend(b, u, first, last):
                for j in range(NT):
                    if j + 1 < NT:
                        exponentials(b, u, j + 1, start=first)
                    elif not last:
                        exponentials(b + 1, 1 - u, 0)
                    beside(b, u, first, last, j)
                    if not first and j in (0, 4):
                        act.wait_ge(pv_product, 2 * b - 1 + j // 4)
                    high_parts(b, j, 0)
                    high_parts(b, j, 1)
                    beside(b, u, first, last, j + 0.5)
                    if j == 0 and last:
                        act.wait_ge(mamba_weights_loaded, 16 * (len(loads) - 9 + 2))
                        nc.scalar.activation(a_neg[:], a_neg[:], ACT.Exp).then_inc(a_exp_ready, 1)
                    if j == 2 and last:
                        fetch(0, 0)
                    if j == 5 and last:
                        normed(0, 0)
                        shortcut(0, 0)
                    if j == NT - 1 and last:
                        high(0, 0)


            def two(t):
                return t.rearrange("p (a n) -> p a n", a=2)

            def fetch(b, u):
                if not isinstance(b, int) or b > 0:
                    act.wait_ge(m_tokens_turned, b)
                nc.scalar.activation(xc[:], X[:, b, :], ACT.Copy).then_inc(m_x_copied, 1)

            def normed(b, u):
                act.wait_ge(m_scales_ready, b + 1)
                for t in range(NT):
                    last = nc.scalar.activation(xt[:, t, :], by_picture(b, lo_banks)[:, t // 4, (t % 4) * P:(t % 4 + 1) * P],
                                                ACT.Identity, bias=rnb[:, 1, t:t + 1], scale=rs[:, 1, t:t + 1])
                last.then_inc(m_normed, 1)

            def shortcut(b, u):
                act.wait_ge(m_normed, b + 1)
                if not isinstance(b, int) or b > 1:
                    act.wait_ge(m_x_updated, b - 1)
                    act.wait_ge(m_gated_ready, NT * (b - 1))
                for t in range(NT):
                    last = nc.scalar.activation(res[u][:, t, :], by_picture(b, lo_banks)[:, t // 4, (t % 4) * P:(t % 4 + 1) * P],
                                                ACT.Identity, bias=rnb[:, 0, t:t + 1], scale=rp1[:, t:t + 1])
                last.then_inc(m_residual_ready, 1)

            def high(b, u):
                act.wait_ge(m_normed_turned, b + 1)
                nc.scalar.activation(two(xh[:]), by_picture(b, hi_banks), ACT.Copy).then_inc(m_xh_ready, 1)

            def tap(b, u, g):
                banks = (hi_banks, lo_banks, hi_banks)[g]
                act.wait_ge(m_group_product, 3 * b + g + 1)
                nc.scalar.activation(two(cacc[:, g, :]), banks, ACT.Identity, bias=cb[:, g:g + 1],
                                     scale=cw[:, g, DCONV - 1:DCONV]).then_inc(m_tap_ready, 1)

            def steps(b, u):
                act.wait_ge(m_z_product, 3 * b + 1)
                nc.scalar.activation(dtr[:].rearrange("p t h -> p (t h)"), lo_banks[:, 0, 0:NT * NH],
                                     ACT.Copy).then_inc(m_dt_copied, 1)

            def silus(b, u):
                for g in range(2):
                    act.wait_ge(m_z_product, 3 * b + 2 + g)
                    nc.scalar.activation(two(zs[u][:, g, :]), (lo_banks, hi_banks)[g], ACT.Silu).then_inc(m_z_ready, 1)
                for g in range(2):
                    act.wait_ge(m_conv_ready, 3 * b + g + 1)
                    nc.scalar.activation(xst[:, g, :], cacc[:, g, :], ACT.Silu).then_inc(m_silu_ready, 1)
                act.wait_ge(m_conv_ready, 3 * b + 3)
                nc.scalar.activation(b_t[:], cacc[0:DS, 2, :], ACT.Silu)
                nc.scalar.activation(c_t[u][:], cacc[DS:2 * DS, 2, :], ACT.Silu).then_inc(m_silu_ready, 1)
                nc.scalar.preload_act_table_set("natural_log_exp_and_others")

            def softplus(b, u):
                act.wait_ge(m_exponent_ready, 2 * b + 1)
                nc.scalar.activation(dte[:], dta[:], ACT.Exp, scale=-1.0).then_inc(m_softplus_step, 1)
                act.wait_ge(m_softplus_step, 2 * b + 1)
                nc.scalar.activation(dtl[:], dte[:], ACT.Ln, bias=1.0).then_inc(m_softplus_step, 1)

            def gather_x(b, u):
                for g in range(2):
                    act.wait_ge(m_x_turned, 3 * b + g + 1)
                    nc.scalar.activation(xs[u][:, :, g * P:(g + 1) * P].rearrange("p (a t) c -> p a t c", a=2),
                                         (lo_banks, hi_banks)[g].rearrange("p a (t c) -> p a t c", c=P),
                                         ACT.Copy).then_inc(m_x_gathered, 1)

            def factors(b, u):
                act.wait_ge(m_exponent_ready, 2 * b + 2)
                nc.scalar.activation(eo[u][:], ein[:], ACT.Exp).then_inc(m_factors_ready, 1)

            def gather_b(b, u):
                act.wait_ge(m_x_turned, 3 * b + 3)
                nc.scalar.activation(b_tok[u][:].rearrange("p t s -> p (t s)"), lo_banks[:, 0, 0:NT * DS],
                                     ACT.Copy).then_inc(m_x_gathered, 1)

            def square(b, c):
                act.wait_ge(m_gated_ready, NT * b + c + 1)
                r = slice(c * P, (c + 1) * P)
                nc.scalar.activation(sqt[:, :, r], y_t[:, :, r], ACT.Square).then_inc(m_square_ready, 1)

            def decays(b, c, first):
                act.wait_ge(m_decay_product, NT * b + c + 1)
                if c >= 2 or not first:
                    act.wait_ge(m_y_product, NT * b + c - 1)
                nc.scalar.activation(dcy[c % 2][:].rearrange("p (a h) t -> p a (h t)", a=2), ps[:, 4:6, :],
                                     ACT.Exp).then_inc(m_decay_ready, 1)

            def scan(b, u, first, last):
                for c in range(NT):
                    if c == 0:
                        if not last:
                            pieces(b + 1, 1 - u, c)
                        if not first:
                            square(b - 1, NT - 1)
                        decays(b, 0, first)
                    if not last:
                        pieces(b + 1, 1 - u, c - 0.25)
                    if c + 1 < NT:
                        decays(b, c + 1, first)
                    if c == 1 and not first:
                        act.wait_ge(m_squares_summed, b)
                    if c >= 1 and not last:
                        pieces(b + 1, 1 - u, c)
                    if c >= 1:
                        square(b, c - 1)
                    if not last:
                        pieces(b + 1, 1 - u, c + 0.5)
                    elif c == 2:
                        token_norm(0)
                    elif c == 3:
                        token_high(0, 0)
                    elif c == 5:
                        gate_exponentials(0)

            act_parts = [(fetch, (), 0), (normed, (), 1.5), (high, (), 2), (shortcut, (), 2.5),
                         (steps, (), 3), (tap, (0,), 3), (softplus, (), 4.75), (tap, (1,), 4.75),
                         (factors, (), 5), (tap, (2,), 5), (silus, (), 6), (gather_x, (), 7),
                         (gather_b, (), 7.5)]

            def pieces(b, u, slot):
                for part, of, at in act_parts:
                    if at == slot:
                        part(b, u, *of)

            def token_norm(b):
                act.wait_ge(e_shift_ready, 2 * b + 2)
                if not isinstance(b, int) or b > 0:
                    act.wait_ge(e_sum_started, b)
                    act.wait_ge(e_turned, b)
                for t in range(NT):
                    last = nc.scalar.activation(un[:, t, :], X[:, b, t * P:(t + 1) * P], ACT.Identity,
                                                bias=enb[:, t:t + 1], scale=ers[:, t:t + 1])
                last.then_inc(e_normed, 1)

            def token_high(b, u):
                act.wait_ge(e_turned, b + 1)
                nc.scalar.activation(two(uh[u][:]), lo_banks, ACT.Copy).then_inc(e_high_ready, 1)

            def gate_exponentials(b):
                act.wait_ge(e_top_ready, b + 1)
                nc.scalar.activation(tex[:], tsh[:], ACT.Exp).then_inc(e_top_exp_ready, 1)

            def gelu(b, n):
                act.wait_ge(e_hidden_product, 2 * NE * b + n + 1)
                if n >= 2 or not isinstance(b, int) or b > 0:
                    act.wait_ge(e_second_product, 2 * NE * b + n - 1)
                nc.scalar.activation(hid[n % 2][:], ps[:, 4 + n % 2, :], ACT.Gelu,
                                     bias=b1_f[:, n // 2:n // 2 + 1]).then_inc(e_hidden_ready, 1)

            def store(b, u):
                act.wait_ge(e_sum_turned, b + 1)
                act.wait_ge(out_free, b + 1)
                nc.scalar.activation(two(o_ch[u][:]), lo_banks, ACT.Copy).then_inc(e_out_ready, 1)

            def experts(b, u, first, last):
                for n in range(2, 2 * NE):
                    gelu(b, n)
                    if n == 3 and not first:
                        store(b - 1, 1 - u)
                    if not last:
                        if n == 5:
                            token_norm(b + 1)
                        if n == 7:
                            token_high(b + 1, 1 - u)
                        if n == 9:
                            gate_exponentials(b + 1)
                if not last:
                    gelu(b + 1, 0)
                    gelu(b + 1, 1)

            act.wait_ge(attn_weights_loaded, 16 * 9)
            nc.scalar.preload_act_table_set("exp_and_others")
            act.wait_ge(dve_linked, 1)
            q_and_k(0, 0)
            exponentials(0, 0, 0, start=True)
            attended(act, attend)
            copy_o(B - 1)
            for part, of, _ in act_parts[4:]:
                part(0, 0, *of)
            act.wait_ge(attention_done, 1)
            scanned(act, scan)
            square(B - 1, NT - 1)

            act.wait_ge(m_x_updated, B)
            gelu(0, 0)
            gelu(0, 1)
            scanned(act, experts)
            store(B - 1, 1)

        @block.vector
        def _(dve):
            def statistics(b):
                dve.wait_ge(picture_loaded, 16 * (b + 1))
                for h in range(2):
                    last = nc.vector.bn_stats(gst[:, b, h, :], X[:, b, h * BANK:(h + 1) * BANK])
                last.then_inc(bn_halves_ready, 1)
                dve.wait_ge(bn_halves_ready, b + 1)
                return nc.vector.bn_aggr(gmv[:, b, :], gst[:, b, :, :].rearrange("p h s -> p (h s)"))

            own = [0]

            def link(ins):
                own[0] += 1
                ins.then_inc(dve_linked, 1)
                dve.wait_ge(dve_linked, own[0])

            def moments(n):
                b = slice(*stat_groups[n])
                nc.vector.tensor_copy(gE[:, b, 0], gmv[:, b, 0])
                link(nc.vector.tensor_tensor(gE[:, b, 1], gmv[:, b, 0], gmv[:, b, 0], ALU.mult))
                nc.vector.tensor_tensor(gE[:, b, 1], gE[:, b, 1], gmv[:, b, 1], ALU.add).then_inc(moments_ready, 1)

            def variances(n):
                b = slice(*stat_groups[n])
                dve.wait_ge(groups_ready, n + 1)
                means = ps[:, 7, 2 * b.start:2 * b.stop].rearrange("p (b s) -> p b s", s=2)
                link(nc.vector.tensor_copy(gm[:, b, :], means))
                link(nc.vector.tensor_tensor(gvar[:, b], gm[:, b, 0], gm[:, b, 0], ALU.mult))
                link(nc.vector.tensor_tensor(gvar[:, b], gm[:, b, 1], gvar[:, b], ALU.subtract))
                nc.vector.tensor_scalar(gvar[:, b], gvar[:, b], 0.0, GN_EPS, ALU.max, ALU.add).then_inc(var_ready, 1)

            def prepare_mamba():
                dve.wait_ge(mamba_weights_loaded, 16 * (len(loads) - 9 + 2))
                link(nc.vector.tensor_scalar(w_z[:], w_z[:], n_w[:, 0:1], None, ALU.mult))
                link(nc.vector.tensor_scalar(w_x[:], w_x[:], n_w[:, 0:1], None, ALU.mult))
                for g in range(2):
                    nc.vector.tensor_scalar(w_out[:, g, :], w_out[:, g, :], g_w[:, g:g + 1], None, ALU.mult)
                nc.vector.tensor_copy(w_zh[:], w_z[:])
                nc.vector.tensor_copy(w_xh[:], w_x[:])
                nc.vector.tensor_copy(mask_r[:], mask_f[:])
                nc.vector.tensor_copy(id_r[:], id_f[:])
                for u in range(2):
                    nc.vector.tensor_copy(lhs_c[u][:].rearrange("p c t -> p (c t)"), cst_f[:, 0, :])
                    done = nc.vector.tensor_copy(rhs_c[u][:].rearrange("p c t -> p (c t)"), cst_f[:, 1, :])
                link(done)
                nc.vector.tensor_tensor(w_zl[:], w_z[:], w_zh[:].bitcast(F32), ALU.subtract)
                link(nc.vector.tensor_tensor(w_xl[:], w_x[:], w_xh[:].bitcast(F32), ALU.subtract))
                dve.wait_ge(a_exp_ready, 1)
                link(nc.vector.tensor_scalar(a_neg[:], a_neg[:], -1.0, None, ALU.mult))

            def normalize(b, n):
                dve.wait_ge(rstd_ready, n + 1)
                nc.vector.tensor_scalar(xn[:], X[:, b, :], gm[:, b, 0:1], grs[:, bass.ds(b, 1)],
                                        ALU.subtract, ALU.mult).then_inc(xn_ready, 1)

            def q_and_k(b, u):
                dve.wait_ge(qk_high_ready, 3 * b + 3)
                tq = O[0:DK].rearrange("p a (c r) -> p (a c) r", r=R)
                qh = q_a[u][0:DK].bitcast(F32).rearrange("p (r c) -> p c r", r=R)
                for dst, r0 in ((q_b[u], 0), (q_a[u], DK)):
                    nc.vector.scalar_tensor_tensor(dst[r0:r0 + DK].rearrange("p (r c) -> p c r", r=R), tq,
                                                   b_qk[0:DK, 0:1], qh, ALU.add, ALU.subtract).then_inc(qk_low_ready, 1)
                nc.vector.scalar_tensor_tensor(k_a[u][DK:2 * DK].rearrange("p (a n) -> p a n", a=2), O[DK:2 * DK],
                                               b_qk[DK:2 * DK, 0:1],
                                               k_a[u][0:DK].bitcast(F32).rearrange("p (a n) -> p a n", a=2),
                                               ALU.add, ALU.subtract).then_inc(qk_low_ready, 1)

            def v_parts(b, u):
                dve.wait_ge(v_product, b + 1)
                v_bias = b_v[:].rearrange("p (o v) -> p o v", o=1).to_broadcast([P, NT, DV])
                nc.vector.tensor_tensor(v_f[:], O[:, 0, :].rearrange("p (k v) -> p k v", v=DV), v_bias,
                                        ALU.add).then_inc(v_ready, 1)
                dve.wait_ge(v_ready, b + 1)
                nc.vector.tensor_copy(v_st[u][:, :, 0:DV], v_f[:]).then_inc(v_high_ready, 1)
                dve.wait_ge(v_high_ready, b + 1)
                nc.vector.tensor_tensor(v_st[u][:, :, DV:2 * DV], v_f[:], v_st[u][:, :, 0:DV].bitcast(F32),
                                        ALU.subtract).then_inc(v_parts_ready, 1)

            def maximum(b, j):
                dve.wait_ge(scores_ready, NT * b + j + 1)
                nc.vector.tensor_reduce(nmax[:, j:j + 1], S[j % 2], AX_XY, ALU.max, negate=True).then_inc(max_ready, 1)

            def low(b, j, h):
                dve.wait_ge(probs_high_ready, 2 * (NT * b + j) + h + 1)
                part = (slice(None), slice(4 * h, 4 * h + 4), slice(j * P, (j + 1) * P))
                nc.vector.tensor_tensor(pt_l[part], T[:, h, :].rearrange("p (k n) -> p k n", n=P),
                                        pt_h[part].bitcast(F32), ALU.subtract).then_inc(probs_low_ready, 1)

            def divide(b, u):
                dve.wait_ge(probs_ready, NT * b + NT)
                nc.vector.reciprocal(rinv[:], rsum[u][:]).then_inc(sum_inverse_ready, 1)
                dve.wait_ge(sum_inverse_ready, b + 1)
                dve.wait_ge(o_folded, b + 1)
                nc.vector.tensor_tensor(o_n[:], O[:, 0, :].rearrange("p (k v) -> p k v", v=DV),
                                        rinv[:].rearrange("p (k o) -> p k o", o=1).to_broadcast([P, NT, DV]),
                                        ALU.mult).then_inc(o_normed, 1)

            def residual(b):
                dve.wait_ge(wo_product, b + 1)
                for e in range(2):
                    xe = X[:, b, :].rearrange("p (j e v) -> p e j v", e=2, v=DV)[:, e]
                    nc.vector.scalar_tensor_tensor(xe, O[:, 1 - e, :].rearrange("p (j v) -> p j v", v=DV),
                                                   b_o[:, 0:1], xe, ALU.add, ALU.add).then_inc(x_updated, 1)

            divide_at, residual_at = 1.5, 2.5
            normalize_at, q_and_k_at, v_at = 1.5, 4.5, 5.5

            def beside(b, u, first, last, slot):
                if not first:
                    if slot == divide_at:
                        divide(b - 1, 1 - u)
                    if slot == residual_at:
                        residual(b - 1)
                if not last:
                    if slot == normalize_at:
                        normalize(b + 1, 1 if first else 2)
                    if slot == q_and_k_at:
                        q_and_k(b + 1, 1 - u)
                    if slot == v_at:
                        v_parts(b + 1, 1 - u)

            def attend(b, u, first, last):
                for j in range(NT):
                    if j + 2 < NT:
                        maximum(b, j + 2)
                    elif not last:
                        maximum(b + 1, j + 2 - NT)
                    beside(b, u, first, last, j)
                    low(b, j, 0)
                    low(b, j, 1)
                    if j == 0 and first:
                        statistics(1).then_inc(dve_linked, 1)
                        own[0] += 1
                        dve.wait_ge(dve_linked, own[0])
                        moments(1)
                    if j == 1 and first:
                        variances(1)
                    if first and 1 <= j < B - 1:
                        aggregated = statistics(j + 1)
                    if first and j == NT - 1:
                        link(aggregated)
                        moments(2)
                        variances(2)
                    if j < NT - 1:
                        beside(b, u, first, last, j + 0.5)
                    if j == 3 and last:
                        prepare_mamba()
                    if j == 4 and last:
                        first_parts[0][0]()
                    if j == NT - 1 and last:
                        first_parts[1][0]()

            def two(t):
                return t.rearrange("p (a n) -> p a n", a=2)

            def heads(t):
                return t.rearrange("p (h d) -> p h d", h=NH)

            def per_head(t, d=HD):
                return t.rearrange("p (h o) -> p h o", o=1).to_broadcast([t.shape[0], NH, d])

            def tile(t, banks=lo_banks):
                return banks[:, t // 4, (t % 4) * P:(t % 4 + 1) * P]

            def front(b, u):
                n = [0]
                xf = dtr[:].rearrange("p c h -> p (c h)")
                df = dts[u][:].rearrange("p c h -> p (c h)")

                def step(ins):
                    n[0] += 1
                    ins.then_inc(m_dve_step, 1)
                    dve.wait_ge(m_dve_step, DVE_FRONT_STEPS * b + n[0])

                def statistics():
                    dve.wait_ge(m_tokens_turned, b + 1)
                    for t in range(NT):
                        last = nc.vector.bn_stats(bst[:, t, :], tile(t, by_picture(b, lo_banks)))
                    step(last)
                    dve.sem_inc(wait_carrier, 1)
                    for t in range(NT):
                        last = nc.vector.bn_aggr(bmv[:, t, :], bst[:, t, :])
                    step(last)
                    nc.vector.tensor_scalar(nmean[:], bmv[:, :, 0], -1.0, None, ALU.mult)
                    step(nc.vector.tensor_scalar(bve[:, 0, :], bmv[:, :, 1], LN_EPS, None, ALU.add))
                    nc.vector.scalar_tensor_tensor(bve[:, 1, :], bve[:, 0, :], F32_EPS, bmv[:, :, 1],
                                                   ALU.mult, ALU.add).then_inc(m_var_ready, 1)

                def low():
                    dve.wait_ge(m_xh_ready, b + 1)
                    nc.vector.tensor_tensor(two(xl[:]), by_picture(b, hi_banks), two(xh[:].bitcast(F32)),
                                            ALU.subtract).then_inc(m_xl_ready, 1)

                def conv(g, k):
                    rows = P if g < 2 else 2 * DS
                    banks = (hi_banks, lo_banks, hi_banks)[g][0:rows].rearrange("p a n -> p (a n)")
                    if k == 1:
                        dve.wait_ge(m_tap_ready, 3 * b + g + 1)
                    ins = nc.vector.scalar_tensor_tensor(cacc[0:rows, g, k:N], banks[:, 0:N - k],
                                                         cw[0:rows, g, DCONV - 1 - k:DCONV - k],
                                                         cacc[0:rows, g, k:N], ALU.mult, ALU.add)
                    if k < DCONV - 1:
                        step(ins)
                    else:
                        ins.then_inc(m_conv_ready, 1)

                def steps():
                    dve.wait_ge(m_dt_copied, b + 1)
                    step(nc.vector.tensor_tensor(dtr[:], dtr[:],
                                                 dtb[:].rearrange("p (o h) -> p o h", o=1).to_broadcast([P, NT, NH]),
                                                 ALU.add))
                    nc.vector.scalar_tensor_tensor(dta[:], xf, -1.0, xf, ALU.mult,
                                                   ALU.max).then_inc(m_exponent_ready, 1)

                def softplus(half):
                    if half == 0:
                        dve.wait_ge(m_softplus_step, 2 * b + 2)
                        step(nc.vector.tensor_scalar(dtw[:], dte[:], 1.0, None, ALU.add))
                        nc.vector.reciprocal(dti[:], dtw[:])
                        step(nc.vector.tensor_scalar(dtc[:], dtw[:], -1.0, None, ALU.add))
                        step(nc.vector.tensor_tensor(dtc[:], dte[:], dtc[:], ALU.subtract))
                    else:
                        step(nc.vector.tensor_tensor(dtc[:], dtc[:], dti[:], ALU.mult))
                        step(nc.vector.tensor_tensor(dtl[:], dtl[:], dtc[:], ALU.add))
                        step(nc.vector.scalar_tensor_tensor(df, xf, 0.0, dtl[:], ALU.max, ALU.add))
                        nc.vector.tensor_tensor(dec_a[:].rearrange("p (c h) -> p c h", h=NH), dts[u][:],
                                                a_neg[:].rearrange("p (o h) -> p o h", o=1).to_broadcast([P, NT, NH]),
                                                ALU.mult).then_inc(m_dt_ready, 1)

                def exponents():
                    dve.wait_ge(m_cumulated, b + 1)
                    nc.vector.tensor_copy(ein[:, 2, :], ps[:, 0, 64:128])
                    if not isinstance(b, int) or b > 0:
                        dve.wait_ge(m_rows_read, 64 * b)
                    nc.vector.tensor_copy(ein[:, 0, :], ps[:, 0, 0:64])
                    step(nc.vector.tensor_copy(cth[:], ps[0:64, 1, 0:P]))
                    nc.vector.tensor_tensor(ctl[:], ps[0:64, 1, 0:P], cth[:].bitcast(F32),
                                            ALU.subtract).then_inc(m_rows_ready, 1)
                    nc.vector.tensor_tensor(ein[:, 1, :], ps[:, 0, 64:128], ein[:, 0, :],
                                            ALU.subtract).then_inc(m_exponent_ready, 1)

                def ends():
                    dve.wait_ge(m_factors_ready, b + 1)
                    nc.vector.tensor_tensor(wend[u][:].rearrange("p c h -> p (c h)"), eo[u][:, 1, :], df,
                                            ALU.mult).then_inc(m_wend_ready, 1)

                def inner():
                    assert n[0] == DVE_FRONT_STEPS, n
                    dve.wait_ge(m_inner_product, b + 1)
                    nc.vector.tensor_copy(g_sb[u][:].rearrange("p (a t) s -> p a (t s)", a=2),
                                          hi_banks).then_inc(m_inner_ready, 1)
                    dve.wait_ge(m_inner_ready, b + 1)

                return [(statistics, (), -0.25), (low, (), 2), (conv, (0, 1), 3.5), (conv, (0, 2), 3.5),
                        (conv, (0, 3), 3.5), (steps, (), 3.5), (conv, (1, 1), 4), (conv, (1, 2), 4),
                        (conv, (1, 3), 4), (softplus, (0,), 4.5), (softplus, (1,), 4.5),
                        (exponents, (), 4.5), (conv, (2, 1), 5), (conv, (2, 2), 5), (conv, (2, 3), 5),
                        (ends, (), 7), (inner, (), 7.5)]

            def mixed(b, u, c):
                dve.wait_ge(m_decay_ready, NT * b + c + 1)
                nc.vector.tensor_tensor(mix[c % 2][:], dcy[c % 2][:],
                                        g_sb[u][:, c:c + 1,
                                                :].to_broadcast([P, NH, P]), ALU.mult).then_inc(m_mix_ready, 1)

            def mean_square(b):
                dve.wait_ge(m_squares_summed, b + 1)
                nc.vector.tensor_scalar(sve[:], ps[:, 6, DI:DI + NT], 1.0 / DI, GN2_EPS, ALU.mult,
                                        ALU.add).then_inc(m_square_mean_ready, 1)

            def output(b, u):
                dve.wait_ge(m_rms_ready, b + 1)
                dve.wait_ge(m_out_product, b + 1)
                for c in range(NT):
                    last = nc.vector.scalar_tensor_tensor(X[:, b, c * P:(c + 1) * P], tile(c, hi_banks),
                                                          srs[:, c:c + 1], res[u][:, c, :], ALU.mult, ALU.add)
                last.then_inc(m_x_updated, 1)

            def run_at(parts, slot):
                for part, of, at in parts:
                    if at == slot:
                        part(*of)

            def scan(b, u, first, last):
                if not last:
                    parts = front(b + 1, 1 - u)
                else:
                    statistics, low, largest, places, softmax, weights, turned, biases = scores(0, 0)
                    parts = [(statistics, (), 1.5), (split_weights, (), 3.5), (low, (), 3.5), (largest, (), 4.5),
                             (places, (), 4.5), (softmax, (), 5.5), (weights, (), 5.5), (turned, (), 6.5),
                             (biases, (), 7.5)]
                for c in range(NT):
                    if c == 0:
                        mixed(b, u, 0)
                        if not first:
                            mean_square(b - 1)
                    if c < NT - 1:
                        dve.wait_ge(m_state_product, (NT - 1) * b + c + 1)
                        if c >= 1 or not first:
                            dve.wait_ge(m_carried_product, (NT - 1) * b + c)
                        if c == 0:
                            nc.vector.tensor_copy(state[1][:], ps[0:DS, 7, 0:DI]).then_inc(m_state_ready, 1)
                        else:
                            dve.wait_ge(m_state_decayed, (NT - 2) * b + c)
                            nc.vector.tensor_tensor(state[(c + 1) % 2][:], ps[0:DS, 7, 0:DI], sdec[:],
                                                    ALU.add).then_inc(m_state_ready, 1)
                    if c >= 1:
                        dve.wait_ge(m_carried_product, (NT - 1) * b + c)
                        if c >= 3 or not first:
                            dve.wait_ge(m_carried_skip_ready, (NT - 1) * b + c - 2)
                        nc.vector.tensor_tensor(heads(yof[c % 2][:]), heads(ps[:, 7, DI:2 * DI]),
                                                per_head(eo[u][:, 0, NH * c:NH * c + NH]), ALU.mult).then_inc(m_carried_ready, 1)
                    run_at(parts, c - 0.25)
                    if c < NT - 1:
                        mixed(b, u, c + 1)
                    if c == 1 and not first:
                        output(b - 1, 1 - u)
                    run_at(parts, c)
                    dve.wait_ge(m_y_product, NT * b + c + 1)
                    dve.wait_ge(m_z_ready, 2 * b + 2)
                    if c == 0 and not first:
                        dve.wait_ge(m_out_product, b)
                    r = slice(c * P, (c + 1) * P)
                    nc.vector.tensor_tensor(y_t[:, :, r], ps[:, 6, 0:DI].rearrange("p (g t) -> p g t", g=2),
                                            zs[u][:, :, r], ALU.mult).then_inc(m_gated_ready, 1)
                    if c == 1 and last:
                        dve.wait_ge(m_x_updated, b)
                    run_at(parts, c + 0.5)

            def split_weights():
                dve.wait_ge(e_weights_loaded, 16 * len(expert_loads))
                nc.vector.tensor_copy(w1_h[:], w1_f[:])
                nc.vector.tensor_copy(rw_h[:], rw_f[:]).then_inc(e_weights_high, 1)
                dve.wait_ge(e_weights_high, 1)
                nc.vector.tensor_tensor(w1_l[:], w1_f[:], w1_h[:].bitcast(F32), ALU.subtract)
                nc.vector.tensor_tensor(rw_l[:], rw_f[:], rw_h[:].bitcast(F32),
                                        ALU.subtract).then_inc(e_weights_split, 1)

            def by_tile(t, n):
                return t.rearrange("p (t o) -> p t o", o=1).to_broadcast([P, NT, n])

            def scores(b, u):
                n = [0]
                io = iota[:].rearrange("p (o e) -> p o e", o=1).to_broadcast([P, NT, NE])

                def step(ins):
                    n[0] += 1
                    ins.then_inc(e_dve_step, 1)
                    dve.wait_ge(e_dve_step, EXPERT_STEPS * b + n[0])

                def statistics():
                    for t in range(NT):
                        last = nc.vector.bn_stats(est[:, t, :], X[:, b, t * P:(t + 1) * P])
                    step(last)
                    dve.sem_inc(wait_carrier, 1)
                    for t in range(NT):
                        last = nc.vector.bn_aggr(emv[:, t, :], est[:, t, :])
                    step(last)
                    nc.vector.tensor_scalar(eve[:], emv[:, :, 1], LN_EPS, None, ALU.add).then_inc(e_var_ready, 1)

                def low():
                    dve.wait_ge(e_high_ready, b + 1)
                    nc.vector.tensor_tensor(two(ul[u][:]), lo_banks, two(uh[u][:].bitcast(F32)),
                                            ALU.subtract).then_inc(e_low_ready, 1)

                def largest():
                    dve.wait_ge(e_logits, b + 1)
                    step(nc.vector.tensor_copy(lg[:].rearrange("p t e -> p (t e)"), ps[:, 2, 0:NT * NE]))
                    dve.sem_inc(wait_carrier, 1)
                    for t in range(NT):
                        last = nc.vector.max(top[:, t, :], lg[:, t, :])
                    step(last)
                    nc.vector.tensor_tensor(tsh[:], top[:], top[:, :, 0:1].to_broadcast([P, NT, 8]),
                                            ALU.subtract).then_inc(e_top_ready, 1)

                def places():
                    for t in range(NT):
                        last = nc.vector.max_index(tix[:, t, :], top[:, t, :], lg[:, t, :])
                    step(last)
                    step(nc.vector.tensor_copy(tif[:], tix[:, :, 0:2]))
                    nc.vector.tensor_tensor(oh1[:], io, tif[:, :, 0:1].to_broadcast([P, NT, NE]), ALU.is_equal)
                    step(nc.vector.tensor_tensor(oh2[:], io, tif[:, :, 1:2].to_broadcast([P, NT, NE]), ALU.is_equal))

                def softmax():
                    dve.wait_ge(e_top_exp_ready, b + 1)
                    step(nc.vector.tensor_reduce(tsum[:], tex[:], AX_X, ALU.add))
                    step(nc.vector.reciprocal(trc[:], tsum[:]))
                    step(nc.vector.tensor_tensor(tp[:], tex[:, :, 0:2], by_tile(trc[:], 2), ALU.mult))
                    step(nc.vector.tensor_tensor(tw[:], tp[:, :, 0], tp[:, :, 1], ALU.add))
                    step(nc.vector.tensor_scalar(tw[:], tw[:], 1e-12, None, ALU.max))
                    step(nc.vector.reciprocal(tw[:], tw[:]))

                def weights():
                    step(nc.vector.tensor_tensor(tp[:], tp[:], by_tile(tw[:], 2), ALU.mult))
                    nc.vector.tensor_tensor(oh1[:], oh1[:], tp[:, :, 0:1].to_broadcast([P, NT, NE]), ALU.mult)
                    step(nc.vector.tensor_tensor(oh2[:], oh2[:], tp[:, :, 1:2].to_broadcast([P, NT, NE]), ALU.mult))
                    nc.vector.tensor_tensor(comb[u][:], oh1[:], oh2[:], ALU.add).then_inc(e_gates_ready, 1)

                def turned():
                    dve.wait_ge(e_gates_turned, b + 1)
                    nc.vector.tensor_copy(comb_t[:], ps[0:NT * NE, 2, P:2 * P]).then_inc(e_gates_copied, 1)

                    assert n[0] == EXPERT_STEPS, n

                def biases():
                    dve.wait_ge(e_sum_started, b + 1)
                    dve.wait_ge(e_bias_product, b + 1)
                    sums = two(acc[u][:].rearrange("p t c -> p (t c)"))
                    nc.vector.tensor_tensor(sums, lo_banks, sums, ALU.add).then_inc(e_bias_added, 1)

                return statistics, low, largest, places, softmax, weights, turned, biases

            def experts(b, u, first, last):
                parts = dict(zip((0, 5, 7, 8, 10, 11, 12, 13), scores(b + 1, 1 - u))) if not last else {}
                dve.wait_ge(e_bias_added, b + 1)
                dve.wait_ge(e_gates_ready, b + 1)
                for k in range(2 * NE):
                    e, h = k // 2, k % 2
                    dve.wait_ge(e_second_product, 2 * NE * b + k + 1)
                    if k >= 2:
                        dve.wait_ge(e_added, 2 * NE * b + k - 1)
                    bank = (3, 6, 7)[k % 3] if k < 2 * NE - 1 else 6
                    for t in range(4):
                        tt = 4 * h + t
                        done = nc.vector.scalar_tensor_tensor(acc[u][:, tt, :], ps[:, bank, t * P:(t + 1) * P],
                                                              comb[u][:, tt, e:e + 1], acc[u][:, tt, :],
                                                              ALU.mult, ALU.add)
                    done.then_inc(e_added, 1)
                    if k in parts:
                        parts[k]()

            first_parts = front(0, 0)
            dve.wait_ge(attn_weights_loaded, 16 * 9)
            nc.vector.tensor_scalar(w_qk[:, 0:DK], w_qk[:, 0:DK], QSCALE, None, ALU.mult)
            link(nc.vector.tensor_scalar(b_qk[0:DK, :], b_qk[0:DK, :], QSCALE, None, ALU.mult))
            link(statistics(0))
            moments(0)
            variances(0)
            normalize(0, 0)
            q_and_k(0, 0)
            v_parts(0, 0)
            maximum(0, 0)
            maximum(0, 1)
            attended(dve, attend)
            divide(B - 1, 1)
            residual(B - 1)
            dve.sem_inc(attention_done, 1)
            for part, of, _ in first_parts[2:]:
                part(*of)
            scanned(dve, scan)
            mean_square(B - 1)
            output(B - 1, 1)

            scanned(dve, experts)


_INS = ['x', 'wqk', 'bqk', 'wv', 'bv_rows', 'wo2', 'bo', 'ident', 'fold', 'group_mean',
        'wz', 'wx', 'norm_w', 'conv_w', 'conv_b', 'dt_bias', 'a_log', 'd_skip', 'wout', 'gnorm_w',
        'tri', 'ones', 'neg_mask', 'sel_rows', 'head_rows',
        'router', 'w1', 'b1', 'w2', 'b2_blocks', 'iota8']


def kernel(**inputs):
    import numpy as np
    import concourse.bacc as bacc
    from concourse.bass_utils import run_bass_kernel_spmd as run

    g = {k: np.asarray(v) for k, v in inputs.items()}
    a = {
        "x": g["x"].reshape(8, 128, 1024),
        "wqk": np.concatenate([g["L0_conv_Wq"].T, g["L0_conv_Wk"].T], 1),
        "bqk": np.concatenate([g["L0_conv_bq"], g["L0_conv_bk"]])[:, None],
        "wv": g["L0_conv_Wv"].T,
        "bv_rows": np.broadcast_to(g["L0_conv_bv"], (128, 64)),
        "wo2": np.concatenate([g["L0_conv_Wo"].T] * 2, 0),
        "bo": g["L0_conv_bo"][:, None],
        "ident": np.eye(128, dtype=np.float32),
        "fold": np.tile(np.eye(64, dtype=np.float32), (2, 1)),
        "group_mean": np.kron(np.eye(32), np.full((4, 4), 0.25)).astype(np.float32),
    }
    w_in, cwt, cbs = g["L1_attn_W_in"], g["L1_attn_conv_w"], g["L1_attn_conv_b"]
    xbc = w_in[256:576]
    order = np.concatenate([np.arange(256), np.tile(np.arange(256, 320), 2)])
    rows = np.arange(32)
    sel = (rows[:, None, None] % 8 == np.arange(8)[None, :, None]) & (rows[:, None, None] < 16)
    head = -1.0 * ((rows[:, None, None] % 8 == np.arange(8)[None, :, None]) & (rows[:, None, None] >= 16))
    full = np.ones((32, 8, 128), np.float32)
    b2_blocks = np.zeros((8, 8, 8, 128), np.float32)
    for t in range(8):
        b2_blocks[t, :, t] = g["L1_ffn_b2"]
    b2_blocks = b2_blocks.reshape(64, 1024)
    a |= {
        "wz": np.concatenate([w_in[:256], w_in[576:]]).T,
        "wx": xbc[order].T.reshape(128, 3, 128),
        "norm_w": g["L1_attn_norm_w"][:, None],
        "conv_w": cwt[order].reshape(3, 128, 4).transpose(1, 0, 2),
        "conv_b": cbs[order].reshape(3, 128).T,
        "dt_bias": np.broadcast_to(g["L1_attn_dt_bias"], (128, 8)),
        "a_log": np.broadcast_to(g["L1_attn_A_log"], (128, 8)),
        "d_skip": np.broadcast_to(g["L1_attn_Dp"], (128, 8)),
        "wout": g["L1_attn_W_out"].T.reshape(2, 128, 128).transpose(1, 0, 2),
        "gnorm_w": g["L1_attn_gnorm_w"].reshape(2, 128).T,
        "tri": np.triu(np.ones((128, 128), np.float32)),
        "ones": np.ones((128, 128), np.float32),
        "neg_mask": np.tile(np.tril(np.full((128, 128), -1e30, np.float32), -1), (1, 4)),
        "sel_rows": (sel * full).astype(np.float32).reshape(32, 1024),
        "head_rows": (head * full).astype(np.float32).reshape(32, 1024),
        "router": g["L1_ffn_router_w"].T,
        "w1": g["L1_ffn_w1"].transpose(1, 0, 2),
        "b1": g["L1_ffn_b1"].T,
        "w2": g["L1_ffn_w2"].transpose(1, 0, 2),
        "b2_blocks": b2_blocks,
        "iota8": np.broadcast_to(np.arange(8, dtype=np.float32), (128, 8)),
    }
    nc = bacc.Bacc("TRN2", target_bir_lowering=False, num_devices=1)
    arrays, args = {}, []
    for name in _INS:
        v = np.ascontiguousarray(a[name])
        arrays[f"in_{name}"] = v
        args.append(nc.dram_tensor(f"in_{name}", v.shape, mybir.dt.from_np(v.dtype), kind="ExternalInput").ap())
    out = nc.dram_tensor("out_0", (8, 128, 1024), F32, kind="ExternalOutput").ap()
    hybrid_kernel(nc, *args, out)
    r = run(nc, [arrays], core_ids=[0])
    return r.results[0]["out_0"].reshape(8, 128, 32, 32)
```
